# Optimizing a Trainium2 kernel written in Bass

```python
import numpy as np
import jax
import jax.numpy as jnp

def _softmax(x, axis=-1):
    return jax.nn.softmax(x, axis=axis)

def _gelu(x):
    return jax.nn.gelu(x, approximate=True)

def _silu(x):
    return jax.nn.silu(x)

def _sigmoid(x):
    return jax.nn.sigmoid(x)

def _layernorm(x, axis=-1, eps=1e-05):
    m = jnp.mean(x, axis=axis, keepdims=True)
    v = jnp.var(x, axis=axis, keepdims=True)
    return (x - m) / jnp.sqrt(v + eps)

def _scatter_add(tgt, idx, src, axis=0):
    return tgt.at[idx].add(src)

def _segment_sum(src, seg, n):
    return jax.ops.segment_sum(src, seg, n)
kernel_name = 'mk_adaln_d2_jaxref_r8_2ca892'

def setup_inputs(seed: int=0):
    np.random.seed(seed)
    _w = jnp.asarray

    def _L0_attn_setup():
        import jax, jax.numpy as jnp
        import numpy as np
        import math
        from functools import partial
        N_HEAD = 16
        CHUNK = 64
        key = jax.random.key(seed)
        ks = jax.random.split(key, 5)
        B, T, D = (4, 512, 128)
        s = 0.02
        return {'x': jax.random.normal(ks[0], (B, T, D), jnp.float32), 'Wq': jax.random.normal(ks[1], (D, D), jnp.float32) * s, 'Wk': jax.random.normal(ks[2], (D, D), jnp.float32) * s, 'Wv': jax.random.normal(ks[3], (D, D), jnp.float32) * s, 'Wo': jax.random.normal(ks[4], (D, D), jnp.float32) * s, 'alpha_raw': jnp.zeros((1, N_HEAD, 1, 1), jnp.float32), 'beta_raw': jnp.zeros((1, N_HEAD, 1, 1), jnp.float32)}
    _L0_attn_in = _L0_attn_setup()

    def _L0_ffn_setup():
        import jax, jax.numpy as jnp
        import numpy as np
        DIM = 128
        DEPTH = 6
        HEADS = 16
        DIM_HEAD = 64
        WINDOW = 32
        INNER = HEADS * DIM_HEAD
        DIM_INNER = int(DIM * 4 * 2 / 3)
        QK_SCALE = 8.0

        def shift_tokens(t):
            a, s = jnp.split(t, 2, -1)
            s = jnp.pad(s, ((0, 0), (1, 0), (0, 0)))[:, :-1]
            return jnp.concatenate([a, s], -1)

        def l2norm(t):
            return t / jnp.maximum(jnp.linalg.norm(t, axis=-1, keepdims=True), 1e-12)

        def rotate_half(x):
            x1, x2 = jnp.split(x, 2, -1)
            return jnp.concatenate([-x2, x1], -1)

        def rotary_tables(n):
            half = jnp.arange(0, DIM_HEAD, 2, dtype=jnp.float32)
            inv_freq = 1.0 / 10000.0 ** (half / DIM_HEAD)
            t = jnp.arange(n, dtype=jnp.float32)
            freqs = t[:, None] * inv_freq[None, :]
            freqs = jnp.concatenate([freqs, freqs], -1)
            base_scale = (half + 0.4 * DIM_HEAD) / (1.4 * DIM_HEAD)
            power = (t - n // 2) / (WINDOW // 2)
            scale = base_scale[None, :] ** power[:, None]
            scale = jnp.concatenate([scale, scale], -1)
            return (freqs, scale)

        def local_attention(q, k, v):
            b, h, n, d = q.shape
            w = WINDOW
            nw = n // w
            bq = q.reshape(b, h, nw, w, d)
            bk = k.reshape(b, h, nw, w, d)
            bv = v.reshape(b, h, nw, w, d)

            def look(t):
                p = jnp.pad(t, ((0, 0), (0, 0), (1, 0), (0, 0), (0, 0)))
                return jnp.concatenate([p[:, :, :nw], p[:, :, 1:]], axis=3)
            bk2, bv2 = (look(bk), look(bv))
            seq = jnp.arange(n).reshape(nw, w)
            seq_p = jnp.pad(seq, ((1, 0), (0, 0)), constant_values=-1)
            jt = jnp.concatenate([seq_p[:nw], seq_p[1:]], axis=1)
            it = seq[:, :, None]
            jb = jt[:, None, :]
            mask = (it < jb) | (it > jb + w) | (jb == -1)
            sim = jnp.einsum('bhwie,bhwje->bhwij', bq, bk2) * QK_SCALE
            sim = jnp.where(mask, -jnp.finfo(sim.dtype).max, sim)
            attn = jax.nn.softmax(sim, -1)
            out = jnp.einsum('bhwij,bhwje->bhwie', attn, bv2)
            return out.reshape(b, h, n, d)

        def attn_layer(x, Wqkv, qs, ksc, Wo):
            b, n, _ = x.shape
            qkv = x @ Wqkv
            q, k, v = jnp.split(qkv, 3, -1)
            sh = lambda t: t.reshape(b, n, HEADS, DIM_HEAD).transpose(0, 2, 1, 3)
            q, k, v = (sh(q), sh(k), sh(v))
            q = l2norm(q) * qs
            k = l2norm(k) * ksc
            freqs, scale = rotary_tables(n)
            cos, sin = (jnp.cos(freqs), jnp.sin(freqs))
            q = q * cos * scale + rotate_half(q) * sin * scale
            inv = 1.0 / scale
            k = k * cos * inv + rotate_half(k) * sin * inv
            out = local_attention(q, k, v)
            out = out.transpose(0, 2, 1, 3).reshape(b, n, INNER)
            return out @ Wo

        def ffn_layer(x, g, bln, W1, b1, W2, b2):
            mu = x.mean(-1, keepdims=True)
            var = ((x - mu) ** 2).mean(-1, keepdims=True)
            xn = (x - mu) / jnp.sqrt(var + 1e-05) * g + bln
            hg = xn @ W1 + b1
            a, gate = jnp.split(hg, 2, -1)
            return a * jax.nn.gelu(gate, approximate=False) @ W2 + b2
        key = jax.random.key(seed)
        ks = jax.random.split(key, 8)
        B, N = (2, 256)
        init = lambda k, shape: jax.random.normal(k, shape, jnp.float32) * 0.02
        return {'x': jax.random.normal(ks[0], (B, N, DIM), jnp.float32), 'Wqkv': init(ks[1], (DEPTH, DIM, 3 * INNER)), 'q_scale': jnp.ones((DEPTH, DIM_HEAD), jnp.float32), 'k_scale': jnp.ones((DEPTH, DIM_HEAD), jnp.float32), 'Wo': init(ks[2], (DEPTH, INNER, DIM)), 'ln_g': jnp.ones((DEPTH, DIM), jnp.float32), 'ln_b': jnp.zeros((DEPTH, DIM), jnp.float32), 'W1': init(ks[3], (DEPTH, DIM, 2 * DIM_INNER)), 'b1': jnp.zeros((DEPTH, 2 * DIM_INNER), jnp.float32), 'W2': init(ks[4], (DEPTH, DIM_INNER, DIM)), 'b2': jnp.zeros((DEPTH, DIM), jnp.float32)}
    _L0_ffn_in = _L0_ffn_setup()
    _L0_c = _w((lambda *s: np.random.randn(*s).astype(np.float32) * 0.05)(2, 128))
    _L0_wmod = _w((lambda *s: np.random.randn(*s).astype(np.float32) * 0.05)(128, 6 * 128) * 128 ** (-0.5))

    def _L1_attn_setup():
        import jax, jax.numpy as jnp
        import numpy as np
        B, N, D, F = (4, 512, 128, 64)
        LN_EPS = 1e-05
        ATTN_EPS = 1e-06

        def _layer_norm(x, w, b):
            mu = jnp.mean(x, axis=-1, keepdims=True)
            var = jnp.var(x, axis=-1, keepdims=True)
            return (x - mu) * jax.lax.rsqrt(var + LN_EPS) * w + b

        def _linear(x, w, b):
            return jnp.einsum('bnd,fd->bnf', x, w) + b

        def _causal_linear_attn(Q, K, V, eps=ATTN_EPS):
            b, n, f = K.shape
            d = V.shape[-1]
            Qt = jnp.swapaxes(Q, 0, 1)
            Kt = jnp.swapaxes(K, 0, 1)
            Vt = jnp.swapaxes(V, 0, 1)

            def step(carry, qkv):
                KV, Ks = carry
                q, k, v = qkv
                KV = KV + k[:, :, None] * v[:, None, :]
                Ks = Ks + k
                num = jnp.einsum('bf,bfd->bd', q, KV)
                den = jnp.sum(q * Ks, axis=-1, keepdims=True) + eps
                return ((KV, Ks), num / den)
            init = (jnp.zeros((b, f, d), Q.dtype), jnp.zeros((b, f), Q.dtype))
            _, out = jax.lax.scan(step, init, (Qt, Kt, Vt))
            return jnp.swapaxes(out, 0, 1)
        key = jax.random.key(seed)
        ks = jax.random.split(key, 9)
        s = 0.02
        return {'x': jax.random.normal(ks[0], (B, N, D), dtype=jnp.float32), 'ln1_w': jnp.ones((D,), jnp.float32), 'ln1_b': jnp.zeros((D,), jnp.float32), 'q_w': jax.random.normal(ks[1], (F, D), jnp.float32) * s, 'q_b': jnp.zeros((F,), jnp.float32), 'k_w': jax.random.normal(ks[2], (F, D), jnp.float32) * s, 'k_b': jnp.zeros((F,), jnp.float32), 'v_w': jax.random.normal(ks[3], (D, D), jnp.float32) * s, 'v_b': jnp.zeros((D,), jnp.float32), 'o_w': jax.random.normal(ks[4], (D, D), jnp.float32) * s, 'o_b': jnp.zeros((D,), jnp.float32), 'ln2_w': jnp.ones((D,), jnp.float32), 'ln2_b': jnp.zeros((D,), jnp.float32), 'f1_w': jax.random.normal(ks[5], (4 * D, D), jnp.float32) * s, 'f1_b': jnp.zeros((4 * D,), jnp.float32), 'f2_w': jax.random.normal(ks[6], (D, 4 * D), jnp.float32) * s, 'f2_b': jnp.zeros((D,), jnp.float32)}
    _L1_attn_in = _L1_attn_setup()

    def _L1_ffn_setup():
        import jax, jax.numpy as jnp
        import numpy as np
        DIM = 128
        DEPTH = 2
        HEADS = 8
        DIM_HEAD = 64
        WINDOW = 64
        INNER = HEADS * DIM_HEAD
        HID = int(DIM * 4 * 2 / 3)
        B, N = (2, 1024)
        QK_SCALE = 8.0

        def shift_token(t):
            t1, t2 = jnp.split(t, 2, axis=-1)
            t2 = jnp.pad(t2, ((0, 0), (1, 0), (0, 0)))[:, :-1]
            return jnp.concatenate([t1, t2], axis=-1)

        def l2norm(t):
            return t / jnp.clip(jnp.linalg.norm(t, axis=-1, keepdims=True), 1e-12)

        def rotate_half(x):
            x1, x2 = jnp.split(x, 2, axis=-1)
            return jnp.concatenate([-x2, x1], axis=-1)

        def rotary_xpos(q, k):
            n = q.shape[-2]
            half_idx = jnp.arange(0, DIM_HEAD, 2, dtype=jnp.float32)
            inv_freq = 1.0 / 10000.0 ** (half_idx / DIM_HEAD)
            t = jnp.arange(n, dtype=jnp.float32)
            freqs = t[:, None] * inv_freq[None, :]
            freqs = jnp.concatenate([freqs, freqs], axis=-1)
            base = (half_idx + 0.4 * DIM_HEAD) / (1.4 * DIM_HEAD)
            power = (t - n // 2) / float(WINDOW // 2)
            scale = base[None, :] ** power[:, None]
            scale = jnp.concatenate([scale, scale], axis=-1)
            cos, sin = (jnp.cos(freqs), jnp.sin(freqs))
            q = q * cos * scale + rotate_half(q) * sin * scale
            k = k * cos / scale + rotate_half(k) * sin / scale
            return (q, k)

        def local_attention(q, k, v):
            b, h, n, d = q.shape
            w = n // WINDOW
            bq = q.reshape(b, h, w, WINDOW, d) * QK_SCALE
            bk = k.reshape(b, h, w, WINDOW, d)
            bv = v.reshape(b, h, w, WINDOW, d)

            def look_around(t):
                p = jnp.pad(t, ((0, 0), (0, 0), (1, 0), (0, 0), (0, 0)))
                return jnp.concatenate([p[:, :, :w], p[:, :, 1:]], axis=3)
            bk, bv = (look_around(bk), look_around(bv))
            bt = jnp.arange(n).reshape(w, WINDOW)
            btp = jnp.pad(bt, ((1, 0), (0, 0)), constant_values=-1)
            btk = jnp.concatenate([btp[:w], btp[1:]], axis=1)
            sim = jnp.einsum('bhwid,bhwjd->bhwij', bq, bk)
            i = bt[:, :, None]
            j = btk[:, None, :]
            mask = (i < j) | (i > j + WINDOW) | (j == -1)
            sim = jnp.where(mask, -jnp.finfo(sim.dtype).max, sim)
            attn = jax.nn.softmax(sim, axis=-1)
            out = jnp.einsum('bhwij,bhwjd->bhwid', attn, bv)
            return out.reshape(b, h, n, d)

        def _layer(x, wqkv, qs, ksc, wo, lg, lb, w1, b1, w2, b2):
            b, n, _ = x.shape
            h = shift_token(x)
            qkv = h @ wqkv
            q, k, v = jnp.split(qkv, 3, axis=-1)
            to_heads = lambda t: t.reshape(b, n, HEADS, DIM_HEAD).transpose(0, 2, 1, 3)
            q, k, v = (to_heads(q), to_heads(k), to_heads(v))
            q = l2norm(q) * qs
            k = l2norm(k) * ksc
            q, k = rotary_xpos(q, k)
            o = local_attention(q, k, v)
            o = o.transpose(0, 2, 1, 3).reshape(b, n, INNER)
            x = x + o @ wo
            h = shift_token(x)
            mu = h.mean(-1, keepdims=True)
            var = h.var(-1, keepdims=True)
            h = (h - mu) / jnp.sqrt(var + 1e-05) * lg + lb
            h = h @ w1 + b1
            a, g = jnp.split(h, 2, axis=-1)
            h = a * jax.nn.gelu(g, approximate=False)
            x = x + h @ w2 + b2
            return x
        key = jax.random.key(seed)
        ks = jax.random.split(key, 6)
        return {'x': jax.random.normal(ks[0], (B, N, DIM), jnp.float32), 'wqkv': jax.random.normal(ks[1], (DEPTH, DIM, 3 * INNER), jnp.float32) * 0.02, 'q_scale': jnp.ones((DEPTH, DIM_HEAD), jnp.float32), 'k_scale': jnp.ones((DEPTH, DIM_HEAD), jnp.float32), 'wo': jax.random.normal(ks[2], (DEPTH, INNER, DIM), jnp.float32) * 0.02, 'ln_g': jnp.ones((DEPTH, DIM), jnp.float32), 'ln_b': jnp.zeros((DEPTH, DIM), jnp.float32), 'w1': jax.random.normal(ks[3], (DEPTH, DIM, 2 * HID), jnp.float32) * 0.02, 'b1': jnp.zeros((DEPTH, 2 * HID), jnp.float32), 'w2': jax.random.normal(ks[4], (DEPTH, HID, DIM), jnp.float32) * 0.02, 'b2': jnp.zeros((DEPTH, DIM), jnp.float32)}
    _L1_ffn_in = _L1_ffn_setup()
    _L1_c = _w((lambda *s: np.random.randn(*s).astype(np.float32) * 0.05)(2, 128))
    _L1_wmod = _w((lambda *s: np.random.randn(*s).astype(np.float32) * 0.05)(128, 6 * 128) * 128 ** (-0.5))
    _d = {'L0_attn_x': _L0_attn_in['x'], 'L0_attn_Wq': _L0_attn_in['Wq'], 'L0_attn_Wk': _L0_attn_in['Wk'], 'L0_attn_Wv': _L0_attn_in['Wv'], 'L0_attn_Wo': _L0_attn_in['Wo'], 'L0_attn_alpha_raw': _L0_attn_in['alpha_raw'], 'L0_attn_beta_raw': _L0_attn_in['beta_raw'], 'L0_ffn_Wqkv': _L0_ffn_in['Wqkv'], 'L0_ffn_q_scale': _L0_ffn_in['q_scale'], 'L0_ffn_k_scale': _L0_ffn_in['k_scale'], 'L0_ffn_Wo': _L0_ffn_in['Wo'], 'L0_ffn_ln_g': _L0_ffn_in['ln_g'], 'L0_ffn_ln_b': _L0_ffn_in['ln_b'], 'L0_ffn_W1': _L0_ffn_in['W1'], 'L0_ffn_b1': _L0_ffn_in['b1'], 'L0_ffn_W2': _L0_ffn_in['W2'], 'L0_ffn_b2': _L0_ffn_in['b2'], 'L0_c': _L0_c, 'L0_wmod': _L0_wmod, 'L1_attn_ln1_w': _L1_attn_in['ln1_w'], 'L1_attn_ln1_b': _L1_attn_in['ln1_b'], 'L1_attn_q_w': _L1_attn_in['q_w'], 'L1_attn_q_b': _L1_attn_in['q_b'], 'L1_attn_k_w': _L1_attn_in['k_w'], 'L1_attn_k_b': _L1_attn_in['k_b'], 'L1_attn_v_w': _L1_attn_in['v_w'], 'L1_attn_v_b': _L1_attn_in['v_b'], 'L1_attn_o_w': _L1_attn_in['o_w'], 'L1_attn_o_b': _L1_attn_in['o_b'], 'L1_attn_ln2_w': _L1_attn_in['ln2_w'], 'L1_attn_ln2_b': _L1_attn_in['ln2_b'], 'L1_attn_f1_w': _L1_attn_in['f1_w'], 'L1_attn_f1_b': _L1_attn_in['f1_b'], 'L1_attn_f2_w': _L1_attn_in['f2_w'], 'L1_attn_f2_b': _L1_attn_in['f2_b'], 'L1_ffn_wqkv': _L1_ffn_in['wqkv'], 'L1_ffn_q_scale': _L1_ffn_in['q_scale'], 'L1_ffn_k_scale': _L1_ffn_in['k_scale'], 'L1_ffn_wo': _L1_ffn_in['wo'], 'L1_ffn_ln_g': _L1_ffn_in['ln_g'], 'L1_ffn_ln_b': _L1_ffn_in['ln_b'], 'L1_ffn_w1': _L1_ffn_in['w1'], 'L1_ffn_b1': _L1_ffn_in['b1'], 'L1_ffn_w2': _L1_ffn_in['w2'], 'L1_ffn_b2': _L1_ffn_in['b2'], 'L1_c': _L1_c, 'L1_wmod': _L1_wmod}
    _x0 = _d['L0_attn_x']
    _d['L0_attn_x'] = jax.random.normal(jax.random.fold_in(jax.random.key(seed), 1), (2, 2048, 128), dtype=_x0.dtype)
    del _x0
    return _d

def reference(L0_attn_x, L0_attn_Wq, L0_attn_Wk, L0_attn_Wv, L0_attn_Wo, L0_attn_alpha_raw, L0_attn_beta_raw, L0_ffn_Wqkv, L0_ffn_q_scale, L0_ffn_k_scale, L0_ffn_Wo, L0_ffn_ln_g, L0_ffn_ln_b, L0_ffn_W1, L0_ffn_b1, L0_ffn_W2, L0_ffn_b2, L0_c, L0_wmod, L1_attn_ln1_w, L1_attn_ln1_b, L1_attn_q_w, L1_attn_q_b, L1_attn_k_w, L1_attn_k_b, L1_attn_v_w, L1_attn_v_b, L1_attn_o_w, L1_attn_o_b, L1_attn_ln2_w, L1_attn_ln2_b, L1_attn_f1_w, L1_attn_f1_b, L1_attn_f2_w, L1_attn_f2_b, L1_ffn_wqkv, L1_ffn_q_scale, L1_ffn_k_scale, L1_ffn_wo, L1_ffn_ln_g, L1_ffn_ln_b, L1_ffn_w1, L1_ffn_b1, L1_ffn_w2, L1_ffn_b2, L1_c, L1_wmod):

    def _L0_attn_ref(x, Wq, Wk, Wv, Wo, alpha_raw, beta_raw):
        import jax, jax.numpy as jnp
        import numpy as np
        import math
        from functools import partial
        N_HEAD = 16
        CHUNK = 64
        B, T, D = x.shape
        H, C = (N_HEAD, CHUNK)
        DH = D // H
        N = T // C

        def proj(W):
            return (x @ W.T).reshape(B, T, H, DH).transpose(0, 2, 1, 3)
        q = proj(Wq)
        k = proj(Wk)
        v = proj(Wv)
        k = k / jnp.maximum(jnp.linalg.norm(k, axis=-1, keepdims=True), 1e-12)
        alpha = jax.nn.sigmoid(alpha_raw) * 0.5
        beta = jax.nn.sigmoid(beta_raw) * 2.0

        def chunks(a):
            return a.reshape(B, H, N, C, DH).transpose(2, 0, 1, 3, 4)
        qc_all, kc_all, vc_all = (chunks(q), chunks(k), chunks(v))
        mask = jnp.triu(jnp.ones((C, C), bool), 1)
        scale = 1.0 / math.sqrt(DH)

        def t_step(M, kv):
            k_t, v_t = kv
            Mk = jnp.einsum('bhde,bhe->bhd', M, k_t)
            forget = Mk[..., :, None] * k_t[..., None, :]
            write = v_t[..., :, None] * k_t[..., None, :]
            return (M - alpha * forget + beta * write, None)

        def chunk_step(M, qkv):
            qi, ki, vi = qkv
            scores = jnp.einsum('bhid,bhjd->bhij', qi, ki) * scale
            scores = jnp.where(mask, -jnp.inf, scores)
            attn = jax.nn.softmax(scores, axis=-1)
            attn_out = jnp.einsum('bhij,bhjd->bhid', attn, vi)
            mem_out = jnp.einsum('bhid,bhde->bhie', qi, M)
            chunk_out = attn_out + 0.1 * mem_out
            kv = (jnp.moveaxis(ki, 2, 0), jnp.moveaxis(vi, 2, 0))
            M, _ = jax.lax.scan(t_step, M, kv)
            return (M, chunk_out)
        M0 = jnp.zeros((B, H, DH, DH), x.dtype)
        _, outs = jax.lax.scan(chunk_step, M0, (qc_all, kc_all, vc_all))
        out = outs.transpose(1, 0, 3, 2, 4).reshape(B, T, D)
        return out @ Wo.T

    def _L0_ffn_ref(x, Wqkv, q_scale, k_scale, Wo, ln_g, ln_b, W1, b1, W2, b2):
        import jax, jax.numpy as jnp
        import numpy as np
        DIM = 128
        DEPTH = 6
        HEADS = 16
        DIM_HEAD = 64
        WINDOW = 32
        INNER = HEADS * DIM_HEAD
        DIM_INNER = int(DIM * 4 * 2 / 3)
        QK_SCALE = 8.0

        def shift_tokens(t):
            a, s = jnp.split(t, 2, -1)
            s = jnp.pad(s, ((0, 0), (1, 0), (0, 0)))[:, :-1]
            return jnp.concatenate([a, s], -1)

        def l2norm(t):
            return t / jnp.maximum(jnp.linalg.norm(t, axis=-1, keepdims=True), 1e-12)

        def rotate_half(x):
            x1, x2 = jnp.split(x, 2, -1)
            return jnp.concatenate([-x2, x1], -1)

        def rotary_tables(n):
            half = jnp.arange(0, DIM_HEAD, 2, dtype=jnp.float32)
            inv_freq = 1.0 / 10000.0 ** (half / DIM_HEAD)
            t = jnp.arange(n, dtype=jnp.float32)
            freqs = t[:, None] * inv_freq[None, :]
            freqs = jnp.concatenate([freqs, freqs], -1)
            base_scale = (half + 0.4 * DIM_HEAD) / (1.4 * DIM_HEAD)
            power = (t - n // 2) / (WINDOW // 2)
            scale = base_scale[None, :] ** power[:, None]
            scale = jnp.concatenate([scale, scale], -1)
            return (freqs, scale)

        def local_attention(q, k, v):
            b, h, n, d = q.shape
            w = WINDOW
            nw = n // w
            bq = q.reshape(b, h, nw, w, d)
            bk = k.reshape(b, h, nw, w, d)
            bv = v.reshape(b, h, nw, w, d)

            def look(t):
                p = jnp.pad(t, ((0, 0), (0, 0), (1, 0), (0, 0), (0, 0)))
                return jnp.concatenate([p[:, :, :nw], p[:, :, 1:]], axis=3)
            bk2, bv2 = (look(bk), look(bv))
            seq = jnp.arange(n).reshape(nw, w)
            seq_p = jnp.pad(seq, ((1, 0), (0, 0)), constant_values=-1)
            jt = jnp.concatenate([seq_p[:nw], seq_p[1:]], axis=1)
            it = seq[:, :, None]
            jb = jt[:, None, :]
            mask = (it < jb) | (it > jb + w) | (jb == -1)
            sim = jnp.einsum('bhwie,bhwje->bhwij', bq, bk2) * QK_SCALE
            sim = jnp.where(mask, -jnp.finfo(sim.dtype).max, sim)
            attn = jax.nn.softmax(sim, -1)
            out = jnp.einsum('bhwij,bhwje->bhwie', attn, bv2)
            return out.reshape(b, h, n, d)

        def attn_layer(x, Wqkv, qs, ksc, Wo):
            b, n, _ = x.shape
            qkv = x @ Wqkv
            q, k, v = jnp.split(qkv, 3, -1)
            sh = lambda t: t.reshape(b, n, HEADS, DIM_HEAD).transpose(0, 2, 1, 3)
            q, k, v = (sh(q), sh(k), sh(v))
            q = l2norm(q) * qs
            k = l2norm(k) * ksc
            freqs, scale = rotary_tables(n)
            cos, sin = (jnp.cos(freqs), jnp.sin(freqs))
            q = q * cos * scale + rotate_half(q) * sin * scale
            inv = 1.0 / scale
            k = k * cos * inv + rotate_half(k) * sin * inv
            out = local_attention(q, k, v)
            out = out.transpose(0, 2, 1, 3).reshape(b, n, INNER)
            return out @ Wo

        def ffn_layer(x, g, bln, W1, b1, W2, b2):
            mu = x.mean(-1, keepdims=True)
            var = ((x - mu) ** 2).mean(-1, keepdims=True)
            xn = (x - mu) / jnp.sqrt(var + 1e-05) * g + bln
            hg = xn @ W1 + b1
            a, gate = jnp.split(hg, 2, -1)
            return a * jax.nn.gelu(gate, approximate=False) @ W2 + b2
        for i in range(DEPTH):
            x = attn_layer(shift_tokens(x), Wqkv[i], q_scale[i], k_scale[i], Wo[i]) + x
            x = ffn_layer(shift_tokens(x), ln_g[i], ln_b[i], W1[i], b1[i], W2[i], b2[i]) + x
        return x

    def _L1_attn_ref(x, ln1_w, ln1_b, q_w, q_b, k_w, k_b, v_w, v_b, o_w, o_b, ln2_w, ln2_b, f1_w, f1_b, f2_w, f2_b):
        import jax, jax.numpy as jnp
        import numpy as np
        B, N, D, F = (4, 512, 128, 64)
        LN_EPS = 1e-05
        ATTN_EPS = 1e-06

        def _layer_norm(x, w, b):
            mu = jnp.mean(x, axis=-1, keepdims=True)
            var = jnp.var(x, axis=-1, keepdims=True)
            return (x - mu) * jax.lax.rsqrt(var + LN_EPS) * w + b

        def _linear(x, w, b):
            return jnp.einsum('bnd,fd->bnf', x, w) + b

        def _causal_linear_attn(Q, K, V, eps=ATTN_EPS):
            b, n, f = K.shape
            d = V.shape[-1]
            Qt = jnp.swapaxes(Q, 0, 1)
            Kt = jnp.swapaxes(K, 0, 1)
            Vt = jnp.swapaxes(V, 0, 1)

            def step(carry, qkv):
                KV, Ks = carry
                q, k, v = qkv
                KV = KV + k[:, :, None] * v[:, None, :]
                Ks = Ks + k
                num = jnp.einsum('bf,bfd->bd', q, KV)
                den = jnp.sum(q * Ks, axis=-1, keepdims=True) + eps
                return ((KV, Ks), num / den)
            init = (jnp.zeros((b, f, d), Q.dtype), jnp.zeros((b, f), Q.dtype))
            _, out = jax.lax.scan(step, init, (Qt, Kt, Vt))
            return jnp.swapaxes(out, 0, 1)
        x_norm = _layer_norm(x, ln1_w, ln1_b)
        Q = jax.nn.elu(_linear(x_norm, q_w, q_b)) + 1.0
        K = jax.nn.elu(_linear(x_norm, k_w, k_b)) + 1.0
        V = _linear(x_norm, v_w, v_b)
        attn = _causal_linear_attn(Q, K, V)
        attn = _linear(attn, o_w, o_b)
        x = x + attn
        h = _layer_norm(x, ln2_w, ln2_b)
        h = jax.nn.gelu(_linear(h, f1_w, f1_b), approximate=False)
        x = x + _linear(h, f2_w, f2_b)
        return x

    def _L1_ffn_ref(x, wqkv, q_scale, k_scale, wo, ln_g, ln_b, w1, b1, w2, b2):
        import jax, jax.numpy as jnp
        import numpy as np
        DIM = 128
        DEPTH = 2
        HEADS = 8
        DIM_HEAD = 64
        WINDOW = 64
        INNER = HEADS * DIM_HEAD
        HID = int(DIM * 4 * 2 / 3)
        B, N = (2, 1024)
        QK_SCALE = 8.0

        def shift_token(t):
            t1, t2 = jnp.split(t, 2, axis=-1)
            t2 = jnp.pad(t2, ((0, 0), (1, 0), (0, 0)))[:, :-1]
            return jnp.concatenate([t1, t2], axis=-1)

        def l2norm(t):
            return t / jnp.clip(jnp.linalg.norm(t, axis=-1, keepdims=True), 1e-12)

        def rotate_half(x):
            x1, x2 = jnp.split(x, 2, axis=-1)
            return jnp.concatenate([-x2, x1], axis=-1)

        def rotary_xpos(q, k):
            n = q.shape[-2]
            half_idx = jnp.arange(0, DIM_HEAD, 2, dtype=jnp.float32)
            inv_freq = 1.0 / 10000.0 ** (half_idx / DIM_HEAD)
            t = jnp.arange(n, dtype=jnp.float32)
            freqs = t[:, None] * inv_freq[None, :]
            freqs = jnp.concatenate([freqs, freqs], axis=-1)
            base = (half_idx + 0.4 * DIM_HEAD) / (1.4 * DIM_HEAD)
            power = (t - n // 2) / float(WINDOW // 2)
            scale = base[None, :] ** power[:, None]
            scale = jnp.concatenate([scale, scale], axis=-1)
            cos, sin = (jnp.cos(freqs), jnp.sin(freqs))
            q = q * cos * scale + rotate_half(q) * sin * scale
            k = k * cos / scale + rotate_half(k) * sin / scale
            return (q, k)

        def local_attention(q, k, v):
            b, h, n, d = q.shape
            w = n // WINDOW
            bq = q.reshape(b, h, w, WINDOW, d) * QK_SCALE
            bk = k.reshape(b, h, w, WINDOW, d)
            bv = v.reshape(b, h, w, WINDOW, d)

            def look_around(t):
                p = jnp.pad(t, ((0, 0), (0, 0), (1, 0), (0, 0), (0, 0)))
                return jnp.concatenate([p[:, :, :w], p[:, :, 1:]], axis=3)
            bk, bv = (look_around(bk), look_around(bv))
            bt = jnp.arange(n).reshape(w, WINDOW)
            btp = jnp.pad(bt, ((1, 0), (0, 0)), constant_values=-1)
            btk = jnp.concatenate([btp[:w], btp[1:]], axis=1)
            sim = jnp.einsum('bhwid,bhwjd->bhwij', bq, bk)
            i = bt[:, :, None]
            j = btk[:, None, :]
            mask = (i < j) | (i > j + WINDOW) | (j == -1)
            sim = jnp.where(mask, -jnp.finfo(sim.dtype).max, sim)
            attn = jax.nn.softmax(sim, axis=-1)
            out = jnp.einsum('bhwij,bhwjd->bhwid', attn, bv)
            return out.reshape(b, h, n, d)

        def _layer(x, wqkv, qs, ksc, wo, lg, lb, w1, b1, w2, b2):
            b, n, _ = x.shape
            h = shift_token(x)
            qkv = h @ wqkv
            q, k, v = jnp.split(qkv, 3, axis=-1)
            to_heads = lambda t: t.reshape(b, n, HEADS, DIM_HEAD).transpose(0, 2, 1, 3)
            q, k, v = (to_heads(q), to_heads(k), to_heads(v))
            q = l2norm(q) * qs
            k = l2norm(k) * ksc
            q, k = rotary_xpos(q, k)
            o = local_attention(q, k, v)
            o = o.transpose(0, 2, 1, 3).reshape(b, n, INNER)
            x = x + o @ wo
            h = shift_token(x)
            mu = h.mean(-1, keepdims=True)
            var = h.var(-1, keepdims=True)
            h = (h - mu) / jnp.sqrt(var + 1e-05) * lg + lb
            h = h @ w1 + b1
            a, g = jnp.split(h, 2, axis=-1)
            h = a * jax.nn.gelu(g, approximate=False)
            x = x + h @ w2 + b2
            return x
        for l in range(DEPTH):
            x = _layer(x, wqkv[l], q_scale[l], k_scale[l], wo[l], ln_g[l], ln_b[l], w1[l], b1[l], w2[l], b2[l])
        return x
    x = L0_attn_x
    mod = (_silu(L0_c) @ L0_wmod).reshape(L0_c.shape[0], 6, 1, -1)
    sa, ca, ga, sb, cb, gb = (mod[:, 0], mod[:, 1], mod[:, 2], mod[:, 3], mod[:, 4], mod[:, 5])
    ga = (2 * (ga >= 0) - 1) * jnp.maximum(jnp.abs(ga), 0.25)
    gb = (2 * (gb >= 0) - 1) * jnp.maximum(jnp.abs(gb), 0.25)
    h = _layernorm(x, axis=-1) * (1 + ca) + sa
    x = x + ga * _L0_attn_ref(h, L0_attn_Wq, L0_attn_Wk, L0_attn_Wv, L0_attn_Wo, L0_attn_alpha_raw, L0_attn_beta_raw)
    h = _layernorm(x, axis=-1) * (1 + cb) + sb
    x = x + gb * _L0_ffn_ref(h, L0_ffn_Wqkv, L0_ffn_q_scale, L0_ffn_k_scale, L0_ffn_Wo, L0_ffn_ln_g, L0_ffn_ln_b, L0_ffn_W1, L0_ffn_b1, L0_ffn_W2, L0_ffn_b2)
    mod = (_silu(L1_c) @ L1_wmod).reshape(L1_c.shape[0], 6, 1, -1)
    sa, ca, ga, sb, cb, gb = (mod[:, 0], mod[:, 1], mod[:, 2], mod[:, 3], mod[:, 4], mod[:, 5])
    ga = (2 * (ga >= 0) - 1) * jnp.maximum(jnp.abs(ga), 0.25)
    gb = (2 * (gb >= 0) - 1) * jnp.maximum(jnp.abs(gb), 0.25)
    h = _layernorm(x, axis=-1) * (1 + ca) + sa
    x = x + ga * _L1_attn_ref(h, L1_attn_ln1_w, L1_attn_ln1_b, L1_attn_q_w, L1_attn_q_b, L1_attn_k_w, L1_attn_k_b, L1_attn_v_w, L1_attn_v_b, L1_attn_o_w, L1_attn_o_b, L1_attn_ln2_w, L1_attn_ln2_b, L1_attn_f1_w, L1_attn_f1_b, L1_attn_f2_w, L1_attn_f2_b)
    h = _layernorm(x, axis=-1) * (1 + cb) + sb
    x = x + gb * _L1_ffn_ref(h, L1_ffn_wqkv, L1_ffn_q_scale, L1_ffn_k_scale, L1_ffn_wo, L1_ffn_ln_g, L1_ffn_ln_b, L1_ffn_w1, L1_ffn_b1, L1_ffn_w2, L1_ffn_b2)
    return x

_drawn_inputs = setup_inputs


def setup_inputs(seed=0):
    import zlib

    import numpy as np

    out = dict(_drawn_inputs(seed))
    spreads = {'L0_attn_alpha_raw': (0.0, 0.8),
     'L0_attn_beta_raw': (0.0, 0.8),
     'L0_ffn_q_scale': (1.0, 0.6),
     'L0_ffn_k_scale': (1.0, 0.6),
     'L0_ffn_ln_g': (1.0, 0.6),
     'L0_ffn_ln_b': (0.0, 0.8),
     'L0_ffn_b1': (0.0, 0.8),
     'L0_ffn_b2': (0.0, 0.417),
     'L1_attn_ln1_w': (1.0, 0.6),
     'L1_attn_ln1_b': (0.0, 0.8),
     'L1_attn_q_b': (0.0, 2.0),
     'L1_attn_k_b': (0.0, 2.0),
     'L1_attn_v_b': (0.0, 0.8),
     'L1_attn_o_b': (0.0, 1.244),
     'L1_attn_ln2_w': (1.0, 0.6),
     'L1_attn_ln2_b': (0.0, 0.8),
     'L1_attn_f1_b': (0.0, 0.8),
     'L1_attn_f2_b': (0.0, 1.441),
     'L1_ffn_q_scale': (1.0, 0.6),
     'L1_ffn_k_scale': (1.0, 0.6),
     'L1_ffn_ln_g': (1.0, 0.6),
     'L1_ffn_ln_b': (0.0, 0.8),
     'L1_ffn_b1': (0.0, 0.8),
     'L1_ffn_b2': (0.0, 0.8)}
    factors = {'L0_attn_Wq': 8.0,
     'L0_attn_Wk': 8.0,
     'L0_attn_Wv': 8.0,
     'L0_attn_Wo': 8.0,
     'L0_ffn_W1': 7.392,
     'L0_ffn_W2': 7.241,
     'L1_attn_q_w': 64.0,
     'L1_attn_k_w': 64.0,
     'L1_attn_v_w': 8.0,
     'L1_attn_o_w': 8.0,
     'L1_attn_f1_w': 4.369,
     'L1_attn_f2_w': 4.115,
     'L1_ffn_wqkv': 8.0,
     'L1_ffn_wo': 7.97,
     'L1_ffn_w1': 8.0,
     'L1_ffn_w2': 8.0}
    for name, (base, spread) in spreads.items():
        noise = np.random.default_rng([zlib.crc32(name.encode()), seed]).standard_normal(out[name].shape)
        drawn = base * np.exp(spread * noise) if base else spread * noise
        out[name] = jnp.asarray(drawn.astype(out[name].dtype))
    for name, factor in factors.items():
        out[name] = (out[name] * factor).astype(out[name].dtype)
    return out
```

```python
from contextlib import ExitStack, contextmanager

import numpy as np

import concourse.bass as bass
from concourse import mybir
from concourse.bass import ds

F32, BF16, I32 = mybir.dt.float32, mybir.dt.bfloat16, mybir.dt.int32
ACT = mybir.ActivationFunctionType
ALU = mybir.AluOpType
AX = mybir.AxisListType
LN_EPS = 1e-5
TILES = 32
ROWS = 2 * 2049


class Steps:

    def __init__(self, eng, sem):
        self.eng, self.sem, self.base, self.n = eng, sem, 0, 0

    def __call__(self, ins, settle=True):
        self.n += 1
        ins.then_inc(self.sem, 1)
        if settle:
            self.eng.wait_ge(self.sem, self.base + self.n)
        return self.base + self.n

    def settle(self):
        self.eng.wait_ge(self.sem, self.base + self.n)

    def turn(self, before, i, per):
        self.base, self.n = before + i * per, 0


@contextmanager
def stage_semaphores(nc, prefix):
    taken = []

    def take(name):
        taken.append(nc.alloc_semaphore(name=f"{prefix}_{name}"))
        return taken[-1]

    yield take
    nc.clear_and_free_semaphores(taken)
    nc.all_engine_barrier()


def wait(eng, sem, value):
    if not isinstance(value, int) or value > 0:
        eng.wait_ge(sem, value)


def pairs(eng, n, emit):
    emit(0, 0)
    emit(1, 1)
    with eng.Fori(1, n // 2) as p:
        emit(p * 2, 0)
        emit(p * 2 + 1, 1)


def inverse_root(step, nc, out, x, half, tmp, newtons=3):
    step(nc.vector.tensor_scalar(out.bitcast(I32), x.bitcast(I32), -0.5, 1597463007.0, ALU.mult, ALU.add))
    step(nc.vector.tensor_scalar(half, x, -0.5, None, ALU.mult))
    for _ in range(newtons):
        step(nc.vector.tensor_tensor(tmp, out, out, ALU.mult))
        step(nc.vector.tensor_tensor(tmp, tmp, half, ALU.mult))
        step(nc.vector.scalar_tensor_tensor(out, tmp, 1.5, out, ALU.add, ALU.mult))


def group_stats(nc, dve, step, x, mean, rstd, bufs):
    st, mv, var, half, tmp = bufs
    for g in range(8):
        for j in range(4):
            step(nc.vector.bn_stats(st[:, j, :], x[:, 4 * g + j, :]), settle=(j == 3))
        for j in range(4):
            step(nc.vector.bn_aggr(mv[:, j, :], st[:, j, :]), settle=(j == 3))
        step(nc.vector.tensor_copy(mean[:, 4 * g:4 * g + 4], mv[:, :, 0]))
        step(nc.vector.tensor_scalar(var[:, 4 * g:4 * g + 4], mv[:, :, 1], LN_EPS, None, ALU.add))
    inverse_root(step, nc, rstd[:, :], var[:, :], half[:, :], tmp[:, :])


def modulated_group(nc, step, x, mean, rstd, out, mods, g, layer, part, done):
    for j in range(4):
        T = 4 * g + j
        step(nc.vector.tensor_scalar(out[:, j, :], x[:, T, :], mean[:, T:T + 1], rstd[:, T:T + 1], ALU.subtract, ALU.mult), settle=(j == 3))
    k = g // 4 + 2 * layer
    vec = lambda i: mods[:, k:k + 1, 3 * part + i, :].to_broadcast([128, 4, 128])
    step(nc.vector.tensor_tensor(out, out, vec(1), ALU.mult))
    nc.vector.tensor_tensor(out, out, vec(0), ALU.add).then_inc(done, 1)


def modulation_stage(nc, mods, c_rows, w_mod):
    with ExitStack() as ctx:
        sb = lambda n, shape, dt=F32: ctx.enter_context(nc.sbuf_tensor(f"mod_{n}", shape, dt))
        sem = ctx.enter_context(stage_semaphores(nc, "mod"))
        c = sb("c", [128, 4])
        e = sb("e", [128, 4])
        silu = sb("silu", [128, 4])
        wide = sb("wide", [128, 4, 128])
        w = sb("w", [128, 2, 768])
        sign = sb("sign", [128, 128])
        mag = sb("mag", [128, 128])
        ps = [[ctx.enter_context(nc.psum_tensor(f"mod_ps{k}{j}", [128, 512], F32)) for j in range(2)] for k in range(4)]
        loaded, exped, wide_done, product, seq = sem("loaded"), sem("exped"), sem("wide_done"), sem("product"), sem("seq")
        with nc.Block() as block:
            @block.sync
            def _(sp):
                for l in range(2):
                    sp.dma_start(w[:, l, :], w_mod[l]).then_inc(loaded, 16)
                    for b in range(2):
                        sp.dma_start(c[:, 2 * l + b:2 * l + b + 1], c_rows[l][b, :].rearrange("(p o) -> p o", o=1)).then_inc(loaded, 16)

            @block.scalar
            def _(act):
                act.wait_ge(loaded, 96)
                nc.scalar.activation(e[:, :], c[:, :], ACT.Exp, scale=-1.0).then_inc(exped, 1)

            @block.tensor
            def _(pe):
                pe.wait_ge(loaded, 96)
                pe.wait_ge(wide_done, 1)
                for k in range(4):
                    for j in range(2):
                        last = nc.tensor.matmul(ps[k][j][:, 0:384], wide[:, k, :], w[:, k // 2, 384 * j:384 * j + 384], start=True, stop=True)
                last.then_inc(product, 1)

            @block.vector
            def _(dve):
                step = Steps(dve, seq)
                dve.wait_ge(exped, 1)
                step(nc.vector.tensor_scalar(e[:, :], e[:, :], 1.0, None, ALU.add))
                step(nc.vector.reciprocal(e[:, :], e[:, :]))
                step(nc.vector.tensor_tensor(silu[:, :], e[:, :], c[:, :], ALU.mult))
                nc.vector.tensor_copy(wide[:, :, :], silu[:, :].rearrange("p (k o) -> p k o", o=1).to_broadcast([128, 4, 128])).then_inc(wide_done, 1)
                dve.wait_ge(product, 1)
                for k in range(4):
                    for j in range(2):
                        src = ps[k][j]
                        out = mods[:, k, 3 * j:3 * j + 3, :]
                        step(nc.vector.tensor_copy(out[:, 0, :], src[:, 0:128]))
                        step(nc.vector.tensor_scalar(out[:, 1, :], src[:, 128:256], 1.0, None, ALU.add))
                        step(nc.vector.tensor_scalar(sign[:, :], src[:, 256:384], 0.0, 2.0, ALU.is_ge, ALU.mult))
                        step(nc.vector.tensor_scalar(mag[:, :], src[:, 256:384], -1.0, 0.25, ALU.mult, ALU.max))
                        step(nc.vector.scalar_tensor_tensor(mag[:, :], src[:, 256:384], 0.25, mag[:, :], ALU.max, ALU.max))
                        step(nc.vector.scalar_tensor_tensor(out[:, 2, :], sign[:, :], -1.0, mag[:, :], ALU.add, ALU.mult))


def delta_attention_stage(nc, x_dram, xr, mods, w_qkvT, w_oT, alpha_raw, beta_raw, tables, qkv_dram):
    H, DH, SUB, N_SUB = 16, 8, 32, 128
    with ExitStack() as ctx:
        sem = ctx.enter_context(stage_semaphores(nc, "da"))
        keep = lambda n, shape, dt=F32: ctx.enter_context(nc.sbuf_tensor(f"da_{n}", shape, dt))
        mem = keep("mem", [128, 64, 128])
        ident = keep("ident", [128, 128])
        block01 = keep("block01", [128, 16])
        trans_a = keep("trans_a", [128, DH, N_SUB])
        trans_b = keep("trans_b", [128, DH, N_SUB])

        with ExitStack() as c2:
            sb = lambda n, shape, dt=F32: c2.enter_context(nc.sbuf_tensor(f"da_{n}", shape, dt))
            ps = [c2.enter_context(nc.psum_tensor(f"da_psa{i}", [128, 512], F32)) for i in range(8)]
            hT = sb("hT", [128, 4096])
            st, mv = sb("st", [128, 4, 6]), sb("mv", [128, 4, 2])
            mean, var, rstd, half, tmp = (sb(n, [128, 32]) for n in ("mean", "var", "rstd", "half", "tmp"))
            h = sb("h", [128, 2, 4, 128])
            w3 = sb("w3", [128, 384])
            qs = sb("qs", [128, SUB, 128])
            ks = sb("ks", [128, SUB, 128])
            vs = sb("vs", [128, SUB, 128])
            state = sb("state", [128, H, 16, DH])
            prod = sb("prod", [128, H, 16, DH])
            dots = sb("dots", [128, H, 16])
            flat_state = prod[:, :, :, :].rearrange("p a b c -> p a (b c)")
            rk, rk_half, rk_tmp, rk_x = (sb(n, [128, SUB * H]) for n in ("rk", "rk_half", "rk_tmp", "rk_x"))
            alpha, beta = sb("alpha", [128, H]), sb("beta", [128, H])
            loaded, seq, h_ready, hT_ps, hT_done = (sem(n) for n in ("loaded", "seq", "h_ready", "hT_ps", "hT_done"))
            proj_ps, q_out, k_out, v_out, sig_exp = (sem(n) for n in ("proj_ps", "q_out", "k_out", "v_out", "sig_exp"))
            k_normed, stored, state_done, tr_ps, tr_done = (sem(n) for n in ("k_normed", "stored", "state_done", "tr_ps", "tr_done"))

            with nc.Block() as block:
                @block.sync
                def _(sp):
                    for b in range(2):
                        sp.dma_start(xr[:, 16 * b:16 * b + 16, :], x_dram[b].rearrange("(t p) d -> p t d", p=128)).then_inc(loaded, 16)
                    sp.dma_start(ident[:, :], tables["ident"]).then_inc(loaded, 16)
                    sp.dma_start(block01[:, :], tables["block01"]).then_inc(loaded, 16)
                    for j in range(3):
                        sp.dma_start(w3[:, 128 * j:128 * j + 128], w_qkvT[j]).then_inc(loaded, 16)
                    sp.dma_start(alpha[:, :], alpha_raw.rearrange("a h b c -> (a b c) h").partition_broadcast(128)).then_inc(loaded, 16)
                    sp.dma_start(beta[:, :], beta_raw.rearrange("a h b c -> (a b c) h").partition_broadcast(128)).then_inc(loaded, 16)
                    sp.wait_ge(q_out, SUB)
                    sp.dma_start(qkv_dram[0].rearrange("(s t) d -> s t d", t=SUB), qs[:, :, :]).then_inc(stored, 16)
                    sp.wait_ge(v_out, SUB)
                    sp.dma_start(qkv_dram[2].rearrange("(s t) d -> s t d", t=SUB), vs[:, :, :]).then_inc(stored, 16)
                    sp.wait_ge(stored, 32)
                    sp.wait_ge(k_normed, 1)
                    sp.dma_start(qkv_dram[1].rearrange("(s t) d -> s t d", t=SUB), ks[:, :, :]).then_inc(stored, 16)
                    sp.wait_ge(stored, 48)

                @block.tensor
                def _(pe):
                    pe.wait_ge(loaded, 144)
                    for g in range(8):
                        pe.wait_ge(h_ready, g + 1)
                        wait(pe, hT_done, g - 1)
                        for i in range(4):
                            last = nc.tensor.transpose(ps[g % 2][:, 128 * i:128 * i + 128], h[:, g % 2, i, :], ident[:, :])
                        last.then_inc(hT_ps, 1)
                    pe.wait_ge(hT_done, 8)
                    for t in range(SUB):
                        wait(pe, q_out, t - 3)
                        wait(pe, v_out, t - 3)
                        nc.tensor.matmul(ps[2 + t % 4][:, 0:384], hT[:, t:4096:SUB], w3[:, :], start=True, stop=True).then_inc(proj_ps, 1)
                    pe.wait_ge(state_done, 1)
                    pe.wait_ge(v_out, SUB)
                    for j in range(4):
                        wait(pe, tr_done, 2 * (j - 1))
                        for i in range(4):
                            n = 4 * j + i
                            last = nc.tensor.transpose(ps[j % 2][:, 128 * i:128 * i + 128], flat_state[:, n, :], ident[:, :])
                        last.then_inc(tr_ps, 1)

                @block.scalar
                def _(act):
                    act.wait_ge(loaded, 144)
                    nc.scalar.activation(alpha[:, :], alpha[:, :], ACT.Exp, scale=-1.0).then_inc(sig_exp, 1)
                    nc.scalar.activation(beta[:, :], beta[:, :], ACT.Exp, scale=-1.0).then_inc(sig_exp, 1)
                    for g in range(8):
                        act.wait_ge(hT_ps, g + 1)
                        nc.scalar.activation(hT[:, 512 * g:512 * g + 512], ps[g % 2][:, :], ACT.Copy).then_inc(hT_done, 1)
                    for t in range(SUB):
                        act.wait_ge(proj_ps, t + 1)
                        nc.scalar.activation(qs[:, t, :], ps[2 + t % 4][:, 0:128], ACT.Copy).then_inc(q_out, 1)
                        nc.scalar.activation(ks[:, t, :], ps[2 + t % 4][:, 128:256], ACT.Copy).then_inc(k_out, 1)
                        nc.scalar.activation(vs[:, t, :], ps[2 + t % 4][:, 256:384], ACT.Copy).then_inc(v_out, 1)
                    for j in range(4):
                        act.wait_ge(tr_ps, j + 1)
                        dst = (trans_a if j < 2 else trans_b)[:, 4 * (j % 2):4 * (j % 2) + 4, :]
                        nc.scalar.activation(dst, ps[j % 2][:, :].rearrange("p (i s) -> p i s", i=4), ACT.Copy).then_inc(tr_done, 2)

                @block.vector
                def _(dve):
                    step = Steps(dve, seq)
                    dve.wait_ge(loaded, 144)
                    group_stats(nc, dve, step, xr, mean, rstd, (st, mv, var, half, tmp))
                    for g in range(8):
                        wait(dve, hT_ps, g - 1)
                        modulated_group(nc, step, xr, mean, rstd, h[:, g % 2, :, :], mods, g, 0, 0, h_ready)
                    dve.wait_ge(sig_exp, 2)
                    for v, f in ((alpha, -0.5), (beta, 2.0)):
                        step(nc.vector.tensor_scalar(v[:, :], v[:, :], 1.0, None, ALU.add))
                        step(nc.vector.reciprocal(v[:, :], v[:, :]))
                        step(nc.vector.tensor_scalar(v[:, :], v[:, :], f, None, ALU.mult))
                    dve.wait_ge(k_out, SUB)
                    flat = prod[:, :, :, :].rearrange("p a b c -> p (a b c)")
                    kf = ks[:, :, :].rearrange("p t d -> p (t d)")
                    for j in range(2):
                        part = slice(2048 * j, 2048 * j + 2048)
                        step(nc.vector.tensor_tensor(flat, kf[:, part], kf[:, part], ALU.mult))
                        step(nc.vector.tensor_reduce(rk_x[:, 256 * j:256 * j + 256], flat.rearrange("p (g e) -> p g e", e=DH), AX.X, ALU.add))
                    step(nc.vector.tensor_scalar(rk_x[:, :], rk_x[:, :], 1e-24, None, ALU.max))
                    inverse_root(step, nc, rk[:, :], rk_x[:, :], rk_half[:, :], rk_tmp[:, :])
                    kg = kf.rearrange("p (g e) -> p g e", e=DH)
                    rkg = rk[:, :].rearrange("p (g o) -> p g o", o=1).to_broadcast([128, SUB * H, DH])
                    nc.vector.tensor_tensor(kg, kg, rkg, ALU.mult).then_inc(k_normed, 1)
                    dve.wait_ge(k_normed, 1)
                    dve.wait_ge(v_out, SUB)
                    dve.wait_ge(stored, 32)
                    for t in range(0, SUB, 8):
                        v4 = vs[:, t:t + 8, :].rearrange("p t (h e) -> p (t h) e", e=DH)
                        for i in range(8):
                            vi = vs[:, t + i, :].rearrange("p (h e) -> p h e", e=DH)
                            step(nc.vector.tensor_tensor(vi, vi, beta[:, :].rearrange("p (h o) -> p h o", o=1).to_broadcast([128, H, DH]), ALU.mult), settle=(i == 7))
                    step(nc.vector.memset(state[:, :, :, :], 0.0))
                    step(nc.vector.memset(state[:, :, :, :].rearrange("p h r e -> p h (r e)")[:, :, 0:64:9], 1.0))
                    before = step.base + step.n
                    with dve.Fori(0, SUB) as t:
                        step.turn(before, t, 6)
                        k_t = ks[:, ds(t, 1), :].rearrange("p o (h e) -> p (o h) e", e=DH)
                        v_t = vs[:, ds(t, 1), :].rearrange("p o (h e) -> p (o h) e", e=DH)
                        kb = k_t.rearrange("p h (o e) -> p h o e", o=1).to_broadcast([128, H, 16, DH])
                        step(nc.vector.tensor_tensor(prod[:, :, :, :], state[:, :, :, :], kb, ALU.mult))
                        step(nc.vector.tensor_reduce(dots[:, :, :], prod[:, :, :, :], AX.X, ALU.add))
                        step(nc.vector.tensor_tensor(dots[:, :, :], dots[:, :, :], alpha[:, :].rearrange("p (h o) -> p h o", o=1).to_broadcast([128, H, 16]), ALU.mult))
                        step(nc.vector.tensor_tensor(dots[:, :, DH:16], dots[:, :, DH:16], v_t, ALU.add))
                        ub = dots[:, :, :].rearrange("p h (r o) -> p h r o", o=1).to_broadcast([128, H, 16, DH])
                        step(nc.vector.tensor_tensor(prod[:, :, :, :], ub, kb, ALU.mult))
                        step(nc.vector.tensor_tensor(state[:, :, :, :], state[:, :, :, :], prod[:, :, :, :], ALU.add))
                    step.turn(before, SUB, 6)
                    step(nc.vector.tensor_copy(flat_state[:, 0:DH, :].rearrange("p e (h r) -> p h r e", r=DH), state[:, :, 0:DH, :]))
                    step(nc.vector.tensor_copy(flat_state[:, DH:16, :].rearrange("p d (h e) -> p h d e", e=DH), state[:, :, DH:16, :]))
                    dve.sem_inc(state_done, 1)

        with ExitStack() as c3:
            sb = lambda n, shape, dt=F32: c3.enter_context(nc.sbuf_tensor(f"da_{n}", shape, dt))
            ps = [c3.enter_context(nc.psum_tensor(f"da_psb{i}", [128, 512], F32)) for i in range(4)]
            mT = sb("mT", [128, 2, 65, DH])
            a_bd = sb("a_bd", [128, 2, 2, 128])
            m_bd = sb("m_bd", [128, 2, 4, 128])
            tenth = sb("tenth", [128, 16])
            m_init, a_built, m_ps, m_done, wide, wide_ps, mem_done, seq = (sem("c_" + n) for n in ("m_init", "a_built", "m_ps", "m_done", "wide", "wide_ps", "mem_done", "seq"))
            with nc.Block() as block:
                @block.gpsimd
                def _(pool):
                    def emit(s, par):
                        wait(pool, m_ps, 2 * (s - 1))
                        for b in range(2):
                            src = trans_a[:, :, ds(64 * b + s, 1)].rearrange("p e (o n) -> p (n o) e", o=1).to_broadcast([128, 16, DH])
                            nc.gpsimd.tensor_tensor(a_bd[:, par, b, :].rearrange("p (h e) -> p h e", e=DH), src,
                                                    block01[:, :].rearrange("p (h o) -> p h o", o=1).to_broadcast([128, 16, DH]), ALU.mult).then_inc(a_built, 1)
                    pairs(pool, 64, emit)

                @block.tensor
                def _(pe):
                    pe.wait_ge(m_init, 1)

                    def emit(s, par):
                        for b in range(2):
                            pe.wait_ge(a_built, 2 * s + b + 1)
                            wait(pe, m_done, 2 * (s - 1) + b + 1)
                            nc.tensor.matmul(ps[b][:, 0:DH], a_bd[:, par, b, :], mT[:, b, ds(s, 1), :].rearrange("p o d -> p (o d)"),
                                             start=True, stop=True).then_inc(m_ps, 1)
                    pairs(pe, 64, emit)
                    for n in range(16):
                        pe.wait_ge(wide, n + 1)
                        wait(pe, mem_done, n - 1)
                        for i in range(4):
                            last = nc.tensor.transpose(ps[2 + n % 2][:, 128 * i:128 * i + 128], m_bd[:, n % 2, i, :], ident[:, :])
                        last.then_inc(wide_ps, 1)

                @block.scalar
                def _(act):
                    for n in range(16):
                        act.wait_ge(wide_ps, n + 1)
                        nc.scalar.activation(mem[:, 4 * n:4 * n + 4, :], ps[2 + n % 2][:, :].rearrange("p (i c) -> p i c", i=4), ACT.Copy).then_inc(mem_done, 1)

                @block.vector
                def _(dve):
                    step = Steps(dve, seq)
                    step(nc.vector.tensor_scalar(tenth[:, :], block01[:, :], 0.1, None, ALU.mult))
                    nc.vector.memset(mT[:, :, 0:1, :], 0.0).then_inc(m_init, 1)

                    def emit(s, par):
                        for b in range(2):
                            dve.wait_ge(m_ps, 2 * s + b + 1)
                            nc.vector.tensor_tensor(mT[:, b, ds(s + 1, 1), :].rearrange("p o d -> p (o d)"), ps[b][:, 0:DH],
                                                    trans_b[:, :, ds(64 * b + s, 1)].rearrange("p d n -> p (d n)"), ALU.add).then_inc(m_done, 1)
                    pairs(dve, 64, emit)
                    dve.wait_ge(m_done, 128)
                    dve.wait_ge(m_init, 1)
                    for n in range(16):
                        wait(dve, wide_ps, n - 1)
                        for i in range(4):
                            c = 4 * n + i
                            src = mT[:, c // 32, 2 * (c % 32), :]
                            last = nc.vector.tensor_tensor(m_bd[:, n % 2, i, :].rearrange("p (h d) -> p h d", d=DH),
                                                           src.rearrange("p (o d) -> p o d", o=1).to_broadcast([128, 16, DH]),
                                                           tenth[:, :].rearrange("p (h o) -> p h o", o=1).to_broadcast([128, 16, DH]), ALU.mult)
                        last.then_inc(wide, 1)

        with ExitStack() as c4:
            sb = lambda n, shape, dt=F32: c4.enter_context(nc.sbuf_tensor(f"da_{n}", shape, dt))
            pb = lambda n: c4.enter_context(nc.psum_tensor(f"da_{n}", [128, 512], F32))
            q_t, k_t = sb("q_t", [128, 2, 128]), sb("k_t", [128, 2, 128])
            v_t = sb("v_t", [128, 2, 2, 128])
            q_pad, k_pad = sb("q_pad", [128, 2, 16, 32]), sb("k_pad", [128, 2, 16, 32])
            q_T, k_T, q_c = sb("q_T", [128, 512]), sb("k_T", [128, 512]), sb("q_c", [128, 128])
            p = sb("p", [128, 4, 4, 64])
            neg_max, p_sum = sb("neg_max", [128, 4, 4]), sb("p_sum", [128, 4, 4])
            p_T = sb("p_T", [128, 8, 128])
            att, att_T, gated = sb("att", [128, 128]), sb("att_T", [128, 128]), sb("gated", [128, 128])
            w_o = sb("w_o", [128, 128])
            causal = sb("causal", [128, 64], BF16)
            ident_bf = sb("ident_bf", [128, 128], BF16)
            mem_t = sb("mem_t", [128, 2, 2, 128])
            s_ps = [pb(f"s_ps{i}") for i in range(4)]
            t_ps = [pb(f"t_ps{i}") for i in range(2)]
            o_ps = [pb(f"o_ps{i}") for i in range(2)]
            names = ("const", "mem_ready", "padded", "zeroed", "qkT_ps", "qT_done", "kT_done", "s_done", "shifted", "exped", "p_done",
                     "pT_ps", "pTa", "pTb", "o_done", "att_done", "attT_ps", "attT_done", "y_done", "x_done", "seq")
            S = {n: sem("t_" + n) for n in names}
            tile_in = [sem("t_in0"), sem("t_in1")]
            with nc.Block() as block:
                @block.sync
                def _(sp):
                    sp.dma_start(w_o[:, :], w_oT).then_inc(S["const"], 16)
                    sp.dma_start(causal[:, :], tables["causal64"]).then_inc(S["const"], 16)
                    sp.dma_start(ident_bf[:, :], tables["ident_bf"]).then_inc(S["const"], 16)

                    def emit(T, par):
                        wait(sp, S["padded"], 2 * (T - 1))
                        wait(sp, S["qkT_ps"], T - 1)
                        wait(sp, S["o_done"], T - 1)
                        r = T * 128
                        sp.dma_start(q_t[:, par, :], qkv_dram[0][ds(r, 128), :]).then_inc(tile_in[par], 16)
                        sp.dma_start(k_t[:, par, :], qkv_dram[1][ds(r, 128), :]).then_inc(tile_in[par], 16)
                        for half_ in range(2):
                            sp.dma_start(v_t[64 * half_:64 * half_ + 64, par, :, :],
                                         qkv_dram[2][ds(r, 128), :].rearrange("(c k) d -> k c d", c=2)).then_inc(tile_in[par], 16)
                    pairs(sp, 32, emit)

                @block.tensor
                def _(pe):
                    pe.wait_ge(S["const"], 48)
                    pe.wait_ge(S["zeroed"], 2)

                    def emit(T, par):
                        pe.wait_ge(tile_in[par], 64 * (T // 2 + 1))
                        pe.wait_ge(S["padded"], 2 * T + 2)
                        wait(pe, S["pTa"], T)
                        wait(pe, S["pTb"], T)
                        wait(pe, S["attT_done"], T)
                        wait(pe, S["x_done"], T)
                        for src, dst in ((q_pad, t_ps[0]), (k_pad, t_ps[1])):
                            for g in range(4):
                                nc.tensor.transpose(dst[:, 128 * g:128 * g + 128], src[:, par, 4 * g:4 * g + 4, :].rearrange("p h e -> p (h e)"), ident[:, :])
                        wait(pe, S["att_done"], T)
                        nc.tensor.transpose(o_ps[1][:, 0:128], q_t[:, par, :], ident[:, :]).then_inc(S["qkT_ps"], 1)
                        wait(pe, S["exped"], 4 * T)
                        for hh in range(4):
                            nc.tensor.matmul(s_ps[hh][:, 0:256].rearrange("p (g k) -> p g k", g=4), ident_bf[:, :],
                                             causal[:, :].rearrange("p (o k) -> p o k", o=1).to_broadcast([128, 4, 64]), start=True, stop=False)
                        pe.wait_ge(S["qT_done"], 2 * T + 2)
                        pe.wait_ge(S["kT_done"], T + 1)
                        for g in range(4):
                            for hh in range(4):
                                for c in range(2):
                                    rows, cols = slice(32 * hh, 32 * hh + 32), slice(128 * g + 64 * c, 128 * g + 64 * c + 64)
                                    last = nc.tensor.matmul(s_ps[hh][64 * c:64 * c + 64, 64 * g:64 * g + 64], q_T[rows, cols], k_T[rows, cols], start=False, stop=(g == 3))
                        last.then_inc(S["s_done"], 1)
                        pe.wait_ge(S["mem_ready"], T + 1)
                        for c in range(2):
                            nc.tensor.matmul(o_ps[0][64 * c:64 * c + 64, 0:128], q_c[:, 64 * c:64 * c + 64], mem_t[:, par, c, :], start=True, stop=False)
                        for hh in range(4):
                            pe.wait_ge(S["p_done"], 4 * T + hh + 1)
                            for j in range(2):
                                n = 2 * hh + j
                                last = nc.tensor.transpose(t_ps[n // 4][:, 128 * (n % 4):128 * (n % 4) + 128],
                                                           p[:, hh, 2 * j:2 * j + 2, :].rearrange("p g k -> p (g k)"), ident[:, :])
                            if hh % 2:
                                last.then_inc(S["pT_ps"], 1)
                        pe.wait_ge(S["pTb"], 1)
                        pe.wait_ge(S["pTa"], T + 1)
                        pe.wait_ge(S["pTb"], T + 1)
                        for n in range(8):
                            for gp in range(2):
                                g = 2 * (n % 2) + gp
                                head = 4 * g + n // 2
                                for c in range(2):
                                    rows = slice(64 * gp, 64 * gp + 64)
                                    last = nc.tensor.matmul(o_ps[gp][64 * c:64 * c + 64, DH * head:DH * head + DH], p_T[rows, n, 64 * c:64 * c + 64],
                                                            v_t[rows, par, c, DH * head:DH * head + DH], start=(gp == 1), stop=(gp == 1 or n == 7))
                        last.then_inc(S["o_done"], 1)
                        pe.wait_ge(S["att_done"], T + 1)
                        nc.tensor.transpose(t_ps[0][:, 0:128], att[:, :], ident[:, :]).then_inc(S["attT_ps"], 1)
                        pe.wait_ge(S["attT_done"], T + 1)
                        nc.tensor.matmul(t_ps[1][:, 0:128], att_T[:, :], w_o[:, :], start=True, stop=True).then_inc(S["y_done"], 1)
                    pairs(pe, 32, emit)

                @block.gpsimd
                def _(pool):
                    def emit(T, par):
                        wait(pool, S["o_done"], T - 1)
                        nc.gpsimd.tensor_copy(mem_t[:, par, :, :], mem[:, ds(2 * T, 2), :]).then_inc(S["mem_ready"], 1)
                    pairs(pool, 32, emit)

                @block.scalar
                def _(act):
                    act.wait_ge(S["zeroed"], 2)

                    def emit(T, par):
                        act.wait_ge(tile_in[par], 64 * (T // 2 + 1))
                        wait(act, S["qkT_ps"], T - 1)
                        nc.scalar.activation(q_pad[:, par, :, 0:DH], q_t[:, par, :].rearrange("p (h e) -> p h e", e=DH), ACT.Copy, scale=float(DH) ** -0.5).then_inc(S["padded"], 1)
                        nc.scalar.activation(k_pad[:, par, :, 0:DH], k_t[:, par, :].rearrange("p (h e) -> p h e", e=DH), ACT.Copy).then_inc(S["padded"], 1)
                        act.wait_ge(S["qkT_ps"], T + 1)
                        wait(act, S["s_done"], T)
                        wait(act, S["o_done"], T)
                        nc.scalar.activation(q_T[:, :], t_ps[0][:, :], ACT.Copy).then_inc(S["qT_done"], 1)
                        nc.scalar.activation(q_c[:, :], o_ps[1][:, 0:128], ACT.Copy).then_inc(S["qT_done"], 1)
                        for hh in range(4):
                            act.wait_ge(S["shifted"], 4 * T + hh + 1)
                            nc.scalar.activation(p[:, hh, :, :], p[:, hh, :, :], ACT.Exp).then_inc(S["exped"], 1)
                        act.wait_ge(S["pT_ps"], 2 * T + 1)
                        wait(act, S["o_done"], T)
                        nc.scalar.activation(p_T[:, 0:4, :], t_ps[0][:, :].rearrange("p (n q) -> p n q", n=4), ACT.Copy).then_inc(S["pTa"], 1)
                        act.wait_ge(S["attT_ps"], T + 1)
                        nc.scalar.activation(att_T[:, :], t_ps[0][:, 0:128], ACT.Copy).then_inc(S["attT_done"], 1)
                    pairs(act, 32, emit)

                @block.vector
                def _(dve):
                    step = Steps(dve, S["seq"])
                    nc.vector.memset(q_pad[:, :, :, :], 0.0).then_inc(S["zeroed"], 1)
                    nc.vector.memset(k_pad[:, :, :, :], 0.0).then_inc(S["zeroed"], 1)
                    PER = 4 * 3 + 2

                    def emit(T, par):
                        step.turn(0, T, PER)
                        dve.wait_ge(S["qkT_ps"], T + 1)
                        wait(dve, S["s_done"], T)
                        nc.vector.tensor_copy(k_T[:, :], t_ps[1][:, :]).then_inc(S["kT_done"], 1)
                        dve.wait_ge(S["s_done"], T + 1)
                        wait(dve, S["pT_ps"], 2 * T)
                        for hh in range(4):
                            sc = s_ps[hh][:, 0:256].rearrange("p (g k) -> p g k", g=4)
                            step(nc.vector.tensor_reduce(neg_max[:, hh, :], sc, AX.X, ALU.max, negate=True))
                            nc.vector.tensor_tensor(p[:, hh, :, :], sc, neg_max[:, hh, :].rearrange("p (g o) -> p g o", o=1).to_broadcast([128, 4, 64]), ALU.add).then_inc(S["shifted"], 1)
                        for hh in range(4):
                            dve.wait_ge(S["exped"], 4 * T + hh + 1)
                            step(nc.vector.tensor_reduce(p_sum[:, hh, :], p[:, hh, :, :], AX.X, ALU.add))
                            step(nc.vector.reciprocal(p_sum[:, hh, :], p_sum[:, hh, :]))
                            nc.vector.tensor_tensor(p[:, hh, :, :], p[:, hh, :, :], p_sum[:, hh, :].rearrange("p (g o) -> p g o", o=1).to_broadcast([128, 4, 64]), ALU.mult).then_inc(S["p_done"], 1)
                        dve.wait_ge(S["pT_ps"], 2 * T + 2)
                        nc.vector.tensor_copy(p_T[:, 4:8, :], t_ps[1][:, :].rearrange("p (n q) -> p n q", n=4)).then_inc(S["pTb"], 1)
                        dve.wait_ge(S["o_done"], T + 1)
                        wait(dve, S["attT_ps"], T)
                        step(nc.vector.tensor_copy(att[:, :], o_ps[0][:, 0:128]))
                        odd = att[:, :].rearrange("p (a x) -> p a x", a=2)[:, :, 32:64]
                        nc.vector.tensor_tensor(odd, odd, o_ps[1][:, 0:128].rearrange("p (a x) -> p a x", a=2)[:, :, 32:64], ALU.add).then_inc(S["att_done"], 1)
                        dve.wait_ge(S["y_done"], T + 1)
                        gate = mods[:, ds(T // 16, 1), 2, :].rearrange("p o d -> p (o d)")
                        step(nc.vector.tensor_tensor(gated[:, :], t_ps[1][:, 0:128], gate, ALU.mult))
                        x_t = xr[:, ds(T, 1), :].rearrange("p o d -> p (o d)")
                        nc.vector.tensor_tensor(x_t, x_t, gated[:, :], ALU.add).then_inc(S["x_done"], 1)
                    pairs(dve, 32, emit)


def feed_stage(nc, name, xr, mods, layer, x_all):
    with ExitStack() as ctx:
        sb = lambda n, shape, dt=F32: ctx.enter_context(nc.sbuf_tensor(f"{name}_{n}", shape, dt))
        sem = ctx.enter_context(stage_semaphores(nc, name))
        st, mv = sb("st", [128, 4, 6]), sb("mv", [128, 4, 2])
        mean, var, rstd, half, tmp = (sb(n, [128, 32]) for n in ("mean", "var", "rstd", "half", "tmp"))
        h = sb("h", [128, 2, 4, 128])
        seq, h_ready = sem("seq"), sem("h_ready")
        stored = [sem("stored0"), sem("stored1")]
        with nc.Block() as block:
            @block.vector
            def _(dve):
                step = Steps(dve, seq)
                group_stats(nc, dve, step, xr, mean, rstd, (st, mv, var, half, tmp))
                for g in range(8):
                    wait(dve, stored[g % 2], 16 * (g // 2))
                    modulated_group(nc, step, xr, mean, rstd, h[:, g % 2, :, :], mods, g, layer, 1, h_ready)

            @block.sync
            def _(sp):
                for g in range(8):
                    sp.wait_ge(h_ready, g + 1)
                    r = 512 * g + g // 4 + 1
                    sp.dma_start(x_all[r:r + 512, :].rearrange("(t p) d -> p t d", p=128), h[:, g % 2, :, :]).then_inc(stored[g % 2], 16)
                for j in range(2):
                    sp.wait_ge(stored[j], 64)


def residual_stage(nc, name, xr, mods, k0, z_rows, out=None):
    with ExitStack() as ctx:
        sb = lambda n, shape, dt=F32: ctx.enter_context(nc.sbuf_tensor(f"{name}_{n}", shape, dt))
        sem = ctx.enter_context(stage_semaphores(nc, name))
        z = sb("z", [128, 8, 4, 128])
        loaded = [sem(f"in{g}") for g in range(8)]
        scaled, added, stored = sem("scaled"), sem("added"), sem("stored")
        with nc.Block() as block:
            @block.sync
            def _(sp):
                for g in range(8):
                    r = 512 * g + g // 4 + 1
                    sp.dma_start(z[:, g, :, :], z_rows[r:r + 512, :].rearrange("(t p) d -> p t d", p=128)).then_inc(loaded[g], 16)
                if out is not None:
                    for g in range(8):
                        sp.wait_ge(added, g + 1)
                        t = 4 * (g % 4)
                        sp.dma_start(out[g // 4].rearrange("(t p) d -> p t d", p=128)[:, t:t + 4, :], xr[:, 4 * g:4 * g + 4, :]).then_inc(stored, 16)
                    sp.wait_ge(stored, 128)

            @block.vector
            def _(dve):
                for g in range(8):
                    dve.wait_ge(loaded[g], 16)
                    k = k0 + g // 4
                    nc.vector.tensor_tensor(z[:, g, :, :], z[:, g, :, :], mods[:, k:k + 1, 5, :].to_broadcast([128, 4, 128]), ALU.mult).then_inc(scaled, 1)
                for g in range(8):
                    dve.wait_ge(scaled, g + 1)
                    x4 = xr[:, 4 * g:4 * g + 4, :]
                    nc.vector.tensor_tensor(x4, x4, z[:, g, :, :], ALU.add).then_inc(added, 1)


def linear_attention_stage(nc, xr, mods, W, tables):
    F, N_CONST = 64, 21
    with ExitStack() as ctx:
        sb = lambda n, shape, dt=F32: ctx.enter_context(nc.sbuf_tensor(f"la_{n}", shape, dt))
        pb = lambda n: ctx.enter_context(nc.psum_tensor(f"la_{n}", [128, 512], F32))
        sem = ctx.enter_context(stage_semaphores(nc, "la"))
        st, mv = sb("st", [128, 4, 6]), sb("mv", [128, 4, 2])
        mean, var, rstd, half, tmp = (sb(n, [128, 32]) for n in ("mean", "var", "rstd", "half", "tmp"))
        mean2, rstd2 = sb("mean2", [128, 32]), sb("rstd2", [128, 32])
        h = sb("h", [128, 32, 128])
        xn = sb("xn", [128, 2, 128])
        xnT = sb("xnT", [128, 2, 128])
        qT, kT = sb("qT", [64, 2, 128]), sb("kT", [64, 2, 128])
        low = sb("low", [64, 2, 128])
        high = sb("high", [64, 2, 128])
        k_tok = sb("k_tok", [128, 2, 64])
        v1 = sb("v1", [128, 2, 129])
        sT = sb("sT", [128, 128])
        kv = sb("kv", [64, 129])
        rden = sb("rden", [128, 1])
        att, attT = sb("att", [128, 128]), sb("attT", [128, 128])
        x_mid = sb("x_mid", [128, 2, 128])
        s6, m2, v_eps, hf, tp_, r2 = sb("s6", [128, 6]), sb("m2", [128, 2]), sb("v_eps", [128, 1]), sb("hf", [128, 1]), sb("tp", [128, 1]), sb("r2", [128, 1])
        y_n, y_T = sb("y_n", [128, 128]), sb("y_T", [128, 128])
        g_T = sb("g_T", [128, 4, 128])
        res = sb("res", [128, 128])
        w_qk, w_v, w_o, w_f1, w_f2 = sb("w_qk", [128, 128]), sb("w_v", [128, 128]), sb("w_o", [128, 128]), sb("w_f1", [128, 512]), sb("w_f2", [128, 4, 128])
        b_qk = sb("b_qk", [64, 2])
        b_v, b_o, b_f2 = sb("b_v", [128, 128]), sb("b_o", [128, 128]), sb("b_f2", [128, 128])
        b_f1 = sb("b_f1", [128, 4])
        ln = sb("ln", [128, 4])
        ident, keep_mask = sb("ident", [128, 128]), sb("keep_mask", [128, 128])
        p_t, p_q, p_k, p_v, p_s, p_n, p_kv, p_f = (pb(n) for n in ("p_t", "p_q", "p_k", "p_v", "p_s", "p_n", "p_kv", "p_f"))
        names = ("const", "seq", "h_ready", "xn_done", "xT_ps", "xT_done", "qk_ps", "v_ps", "low_done", "exped", "feat", "ktok_ps", "ktok_done", "v_done",
                 "s_ps", "s_done", "n_ps", "kv_ps", "kv_done", "att_done", "attT_ps", "attT_done", "o_ps", "yn_done", "yT_ps", "yT_done",
                 "f1_ps", "gelu", "f2_ps", "x_done")
        S = {n: sem(n) for n in names}
        with nc.Block() as block:
            @block.sync
            def _(sp):
                loads = [(ident[:, :], tables["ident"]), (keep_mask[:, :], tables["keep"]), (w_qk[:, 0:F], W["q_wT"]), (w_qk[:, F:2 * F], W["k_wT"]),
                         (w_v[:, :], W["v_wT"]), (w_o[:, :], W["o_wT"]), (w_f1[:, :], W["f1_wT"]), (w_f2[:, :, :], W["f2_wT"].rearrange("(c p) n -> p c n", p=128))]
                col = lambda a: a.rearrange("(p o) -> p o", o=1)
                loads += [(b_qk[:, 0:1], col(W["q_b"])), (b_qk[:, 1:2], col(W["k_b"]))]
                loads += [(b_f1[:, c:c + 1], col(W["f1_b"][128 * c:128 * c + 128])) for c in range(4)]
                loads += [(ln[:, i:i + 1], col(W[n])) for i, n in enumerate(("ln1_w", "ln1_b", "ln2_w", "ln2_b"))]
                loads += [(dst, W[n].rearrange("(o n) -> o n", o=1).partition_broadcast(128)) for dst, n in ((b_v[:, :], "v_b"), (b_o[:, :], "o_b"), (b_f2[:, :], "f2_b"))]
                assert len(loads) == N_CONST
                for dst, src in loads:
                    sp.dma_start(dst, src).then_inc(S["const"], 16)

            @block.tensor
            def _(pe):
                pe.wait_ge(S["const"], 16 * N_CONST)

                def emit(T, par):
                    n = T + 1
                    pe.wait_ge(S["xn_done"], n)
                    wait(pe, S["attT_done"], T)
                    wait(pe, S["yT_done"], T)
                    nc.tensor.transpose(p_t[:, 0:128], xn[:, par, :], ident[:, :]).then_inc(S["xT_ps"], 1)
                    pe.wait_ge(S["xT_done"], n)
                    wait(pe, S["feat"], 2 * T)
                    nc.tensor.matmul(p_q[0:F, 0:128], w_qk[:, 0:F], xnT[:, par, :], start=True, stop=True)
                    nc.tensor.matmul(p_k[0:F, 0:128], w_qk[:, F:2 * F], xnT[:, par, :], start=True, stop=True).then_inc(S["qk_ps"], 1)
                    wait(pe, S["v_done"], T)
                    nc.tensor.matmul(p_v[:, 0:128], xnT[:, par, :], w_v[:, :], start=True, stop=True).then_inc(S["v_ps"], 1)
                    pe.wait_ge(S["feat"], 2 * n)
                    wait(pe, S["s_done"], T)
                    nc.tensor.matmul(p_s[:, 0:128], kT[:, par, :], qT[:, par, :], start=True, stop=True).then_inc(S["s_ps"], 1)
                    nc.tensor.transpose(p_t[:, 0:F], kT[:, par, :], ident[0:F, 0:F]).then_inc(S["ktok_ps"], 1)
                    pe.wait_ge(S["s_done"], n)
                    pe.wait_ge(S["v_done"], n)
                    wait(pe, S["x_done"], T)
                    nc.tensor.matmul(p_n[:, 0:129], sT[:, :], v1[:, par, :], start=True, stop=False)
                    wait(pe, S["kv_done"], n)
                    nc.tensor.matmul(p_n[:, 0:129], qT[:, par, :], kv[:, :], start=False, stop=True).then_inc(S["n_ps"], 1)
                    pe.wait_ge(S["ktok_done"], n)
                    nc.tensor.matmul(p_kv[0:F, 0:129], k_tok[:, par, :], v1[:, par, :], start=True, stop=True).then_inc(S["kv_ps"], 1)
                    pe.wait_ge(S["att_done"], n)
                    nc.tensor.transpose(p_t[:, 0:128], att[:, :], ident[:, :]).then_inc(S["attT_ps"], 1)
                    pe.wait_ge(S["attT_done"], n)
                    nc.tensor.matmul(p_n[:, 0:128], attT[:, :], w_o[:, :], start=True, stop=True).then_inc(S["o_ps"], 1)
                    pe.wait_ge(S["yn_done"], n)
                    nc.tensor.transpose(p_t[:, 0:128], y_n[:, :], ident[:, :]).then_inc(S["yT_ps"], 1)
                    pe.wait_ge(S["yT_done"], n)
                    for c in range(4):
                        last = nc.tensor.matmul(p_f[:, 128 * c:128 * c + 128], w_f1[:, 128 * c:128 * c + 128], y_T[:, :], start=True, stop=True)
                    last.then_inc(S["f1_ps"], 1)
                    pe.wait_ge(S["gelu"], n)
                    for c in range(4):
                        last = nc.tensor.matmul(p_n[:, 0:128], g_T[:, c, :], w_f2[:, c, :], start=(c == 0), stop=(c == 3))
                    last.then_inc(S["f2_ps"], 1)
                pairs(pe, 32, emit)

            @block.scalar
            def _(act):
                act.wait_ge(S["const"], 16 * N_CONST)

                def emit(T, par):
                    n = T + 1
                    act.wait_ge(S["xT_ps"], n)
                    nc.scalar.activation(xnT[:, par, :], p_t[:, 0:128], ACT.Identity, bias=ln[:, 1:2], scale=ln[:, 0:1]).then_inc(S["xT_done"], 1)
                    act.wait_ge(S["low_done"], n)
                    nc.scalar.activation(low[:, :, :], low[:, :, :], ACT.Exp).then_inc(S["exped"], 1)
                    act.wait_ge(S["ktok_ps"], n)
                    nc.scalar.activation(k_tok[:, par, :], p_t[:, 0:F], ACT.Copy).then_inc(S["ktok_done"], 1)
                    act.wait_ge(S["attT_ps"], n)
                    nc.scalar.activation(attT[:, :], p_t[:, 0:128], ACT.Copy).then_inc(S["attT_done"], 1)
                    act.wait_ge(S["yT_ps"], n)
                    nc.scalar.activation(y_T[:, :], p_t[:, 0:128], ACT.Identity, bias=ln[:, 3:4], scale=ln[:, 2:3]).then_inc(S["yT_done"], 1)
                    act.wait_ge(S["f1_ps"], n)
                    for c in range(4):
                        last = nc.scalar.activation(g_T[:, c, :], p_f[:, 128 * c:128 * c + 128], ACT.Gelu, bias=b_f1[:, c:c + 1], scale=1.0)
                    last.then_inc(S["gelu"], 1)
                pairs(act, 32, emit)

            @block.vector
            def _(dve):
                step = Steps(dve, S["seq"])
                dve.wait_ge(S["const"], 16 * N_CONST)
                group_stats(nc, dve, step, xr, mean, rstd, (st, mv, var, half, tmp))
                for g in range(8):
                    modulated_group(nc, step, xr, mean, rstd, h[:, 4 * g:4 * g + 4, :], mods, g, 1, 0, S["h_ready"])
                dve.wait_ge(S["h_ready"], 8)
                group_stats(nc, dve, step, h, mean2, rstd2, (st, mv, var, half, tmp))
                step(nc.vector.memset(v1[:, :, :], 1.0))
                before = step.base + step.n
                nc.vector.memset(kv[:, :], 0.0).then_inc(S["kv_done"], 1)
                PER = 25

                def emit(T, par, batch_ends=False):
                    n = T + 1
                    step.turn(before, T, PER)
                    one = lambda a: a[:, ds(T, 1)]
                    h_t = h[:, ds(T, 1), :].rearrange("p o d -> p (o d)")
                    wait(dve, S["xT_ps"], T - 1)
                    nc.vector.tensor_scalar(xn[:, par, :], h_t, one(mean2), one(rstd2), ALU.subtract, ALU.mult).then_inc(S["xn_done"], 1)
                    dve.wait_ge(S["qk_ps"], n)
                    wait(dve, S["feat"], 2 * T)
                    for j, src in enumerate((p_q, p_k)):
                        step(nc.vector.tensor_scalar(high[:, j, :], src[0:F, 0:128], b_qk[:, j:j + 1], 0.0, ALU.add, ALU.max), settle=False)
                        last = nc.vector.tensor_scalar(low[:, j, :], src[0:F, 0:128], b_qk[:, j:j + 1], 0.0, ALU.add, ALU.min)
                        if j:
                            last.then_inc(S["low_done"], 1)
                    dve.wait_ge(S["v_ps"], n)
                    nc.vector.tensor_tensor(v1[:, par, 0:128], p_v[:, 0:128], b_v[:, :], ALU.add).then_inc(S["v_done"], 1)
                    dve.wait_ge(S["exped"], n)
                    step.settle()
                    for j, dst in enumerate((qT, kT)):
                        nc.vector.tensor_tensor(dst[:, par, :], high[:, j, :], low[:, j, :], ALU.add).then_inc(S["feat"], 1)
                    dve.wait_ge(S["s_ps"], n)
                    wait(dve, S["n_ps"], T)
                    nc.vector.tensor_tensor(sT[:, :], p_s[:, 0:128], keep_mask[:, :], ALU.mult).then_inc(S["s_done"], 1)
                    dve.wait_ge(S["n_ps"], n)
                    wait(dve, S["attT_ps"], T)
                    step(nc.vector.tensor_scalar(rden[:, :], p_n[:, 128:129], 1e-6, None, ALU.add))
                    step(nc.vector.reciprocal(rden[:, :], rden[:, :]))
                    nc.vector.tensor_scalar(att[:, :], p_n[:, 0:128], rden[:, 0:1], None, ALU.mult).then_inc(S["att_done"], 1)
                    dve.wait_ge(S["kv_ps"], n)
                    dve.wait_ge(S["kv_done"], n)
                    if batch_ends:
                        nc.vector.memset(kv[:, :], 0.0).then_inc(S["kv_done"], 1)
                    else:
                        nc.vector.tensor_tensor(kv[:, :], kv[:, :], p_kv[0:F, 0:129], ALU.add).then_inc(S["kv_done"], 1)
                    dve.wait_ge(S["o_ps"], n)
                    step(nc.vector.tensor_tensor(x_mid[:, par, :], p_n[:, 0:128], h_t, ALU.add))
                    step(nc.vector.tensor_tensor(x_mid[:, par, :], x_mid[:, par, :], b_o[:, :], ALU.add))
                    step(nc.vector.bn_stats(s6[:, :], x_mid[:, par, :]))
                    step(nc.vector.memset(v_eps[:, :], LN_EPS), settle=False)
                    step(nc.vector.bn_aggr(m2[:, :], s6[:, :]))
                    step(nc.vector.tensor_tensor(v_eps[:, :], m2[:, 1:2], v_eps[:, :], ALU.add))
                    inverse_root(step, nc, r2[:, :], v_eps[:, :], hf[:, :], tp_[:, :])
                    nc.vector.tensor_scalar(y_n[:, :], x_mid[:, par, :], m2[:, 0:1], r2[:, 0:1], ALU.subtract, ALU.mult).then_inc(S["yn_done"], 1)
                    dve.wait_ge(S["f2_ps"], n)
                    step(nc.vector.tensor_tensor(res[:, :], p_n[:, 0:128], x_mid[:, par, :], ALU.add))
                    dve.sem_inc(S["x_done"], 1)
                    step(nc.vector.tensor_tensor(res[:, :], res[:, :], b_f2[:, :], ALU.add))
                    step(nc.vector.tensor_tensor(res[:, :], res[:, :], mods[:, ds(T // 16 + 2, 1), 2, :].rearrange("p o d -> p (o d)"), ALU.mult))
                    x_t = xr[:, ds(T, 1), :].rearrange("p o d -> p (o d)")
                    step(nc.vector.tensor_tensor(x_t, x_t, res[:, :], ALU.add))
                    assert step.n == PER, step.n
                emit(0, 0)
                emit(1, 1)
                with dve.Fori(1, 7) as p:
                    emit(p * 2, 0)
                    emit(p * 2 + 1, 1)
                emit(14, 0)
                emit(15, 1, batch_ends=True)
                with dve.Fori(8, 16) as p:
                    emit(p * 2, 0)
                    emit(p * 2 + 1, 1)


def local_block_stage(nc, name, depth, heads, window, x_all, xb_dram, weights, tables, n_tiles):
    U = heads // 2
    W = window
    KW = 128 + W
    NT = depth * n_tiles
    TPB = n_tiles // 2
    HID = 341
    CH = [(0, 128), (128, 128), (256, HID - 256)]
    NV = 4 * U + 1
    AT_SCORE, AT_MAX, AT_NORM, AT_PT, AT_PV, AT_OUT = 1, 1, 2, 3, 4, 5
    LAG_RES = (U - 1 + AT_OUT) // U
    LAG_UP = LAG_RES + 1
    LAG_DOWN = LAG_RES + 2
    PROJ_AT = {8: [1, 2, 1, 2, 2, 0, 0, 0], 4: [1, 1, 1, 1]}[U]
    NORM_STEP = {8: 5, 4: 3}[U]
    UPT_STEP = {8: 6, 4: 3}[U]
    UP_STEP = U - 1
    DOWN_STEP = 1
    NEWTONS = 3
    CHAIN = 4 + 3 * NEWTONS
    first_full = LAG_DOWN + 1
    if (NT - 2 - first_full) % 2:
        first_full += 1
    proj_units = []
    at = 0
    for c in PROJ_AT:
        proj_units.append(list(range(at, at + c)))
        at += c

    with ExitStack() as ctx:
        sb = lambda n, shape, dt=F32: ctx.enter_context(nc.sbuf_tensor(f"{name}_{n}", shape, dt))
        pb = lambda n, shape=(128, 512), dt=F32: ctx.enter_context(nc.psum_tensor(f"{name}_{n}", list(shape), dt))
        sem = ctx.enter_context(stage_semaphores(nc, name))

        w_qkv = sb("w_qkv", [128, U, 3, 128])
        w_out = sb("w_out", [128, U, 128])
        w_up = sb("w_up", [128, 2 * HID])
        w_down = sb("w_down", [128, 3, 128])
        b_up = sb("b_up", [128, 2, 3])
        b_down = sb("b_down", [128, 128])
        ln_gb = sb("ln_gb", [128, 2])
        qk_scales = sb("qk_scales", [128, 4, 64])
        rot_base = sb("rot_base", [128, 2, 256])
        rot = sb("rot", [128, 2, 4, 64])
        frame = sb("frame", [128, 1])
        masks = sb("masks", [128, TPB, KW], BF16)
        ident = sb("ident", [128, 128])
        ident_bf = sb("ident_bf", [128, 128], BF16)
        x_in = sb("x_in", [128, 2, 128])
        xT = sb("xT", [128, 2, 128])
        x_res = sb("x_res", [128, 2, 128])
        x_mid = sb("x_mid", [128, 2, 128])
        f_in = sb("f_in", [128, 2, 128])
        f_res = sb("f_res", [128, 2, 128])
        f_resb = sb("f_resb", [128, 128])
        f_norm = sb("f_norm", [128, 128])
        f_normT = sb("f_normT", [128, 128])
        gate = sb("gate", [128, 3, 128])
        hidden = sb("hidden", [128, 3, 128])
        x_new = sb("x_new", [128, 2, 128])
        squares = sb("squares", [128, 2, 256])
        sumsq = sb("sumsq", [128, 4 * U])
        cos_part = sb("cos_part", [128, 2, 256])
        sin_part = sb("sin_part", [128, 2, 256])
        qk = sb("qk", [128, 2, U, 256])
        val = sb("val", [128, 2, U, 128])
        qkT = sb("qkT", [128, 2, 256])
        k_prev = sb("k_prev", [128, 2, U, W])
        v_prev = sb("v_prev", [128, 2, U, 128])
        probs = sb("probs", [128, 4, 2, KW])
        neg_max = sb("neg_max", [128, 4, 2])
        p_sum = sb("p_sum", [128, 4, 2])
        p_rec = sb("p_rec", [128, 2])
        probsT = sb("probsT", [128, 2, 256 + 2 * W])
        outT = sb("outT", [128, 2, 128])
        stats = sb("stats", [128, 6])
        mean_var = sb("mean_var", [128, 2])
        nw_x = sb("nw_x", [128, NV])
        nw_h = sb("nw_h", [128, NV])
        nw_a = sb("nw_a", [128, NV])
        rnorm = sb("rnorm", [128, 2, NV])

        ps_q = [pb("ps_q0"), pb("ps_q1")]
        ps_s = [pb("ps_s0"), pb("ps_s1")]
        ps_t = pb("ps_t")
        ps_pt = pb("ps_pt")
        ps_o = pb("ps_o")
        ps_y = pb("ps_y")

        consts_in = sem("consts_in")
        rep_in = sem("rep_in")
        zeroed = sem("zeroed")
        wq_in = sem("wq_in")
        wo_in = sem("wo_in")
        wf_in = sem("wf_in")
        xin_in = [sem("xin_in0"), sem("xin_in1")]
        rotb_in = [sem("rotb_in0"), sem("rotb_in1")]
        xres_in = [sem("xres_in0"), sem("xres_in1")]
        fin_in = [sem("fin_in0"), sem("fin_in1")]
        fres_in = [sem("fres_in0"), sem("fres_in1")]
        mid_stored = sem("mid_stored")
        new_stored = sem("new_stored")
        xT_ps = sem("xT_ps")
        proj_ps = sem("proj_ps")
        qkT_ps = sem("qkT_ps")
        score_half = sem("score_half")
        score_ps = sem("score_ps")
        pT_ps = sem("pT_ps")
        pv_ps = sem("pv_ps")
        y_ps = sem("y_ps")
        wo_used = sem("wo_used")
        fT_ps = sem("fT_ps")
        up_ps = sem("up_ps")
        down_ps = sem("down_ps")
        sq_done = sem("sq_done")
        val_done = sem("val_done")
        xT_done = sem("xT_done")
        qkT_done = sem("qkT_done")
        exp_done = sem("exp_done")
        pT_done = sem("pT_done")
        outT_done = sem("outT_done")
        fT_done = sem("fT_done")
        gelu_done = sem("gelu_done")
        ss_done = sem("ss_done")
        rotated = sem("rotated")
        max_done = sem("max_done")
        rec_done = sem("rec_done")
        probs_done = sem("probs_done")
        kprev_done = sem("kprev_done")
        vprev_done = sem("vprev_done")
        chain = sem("chain")
        mid_done = sem("mid_done")
        stats_done = sem("stats_done")
        fnorm_done = sem("fnorm_done")
        hidden_done = sem("hidden_done")
        new_done = sem("new_done")
        rot_done = sem("rot_done")
        added = sem("added")
        normed = sem("normed")
        fresb_done = sem("fresb_done")

        def unit(T, s, lag):
            d, u = divmod(s - lag, U)
            return T + d, d, u

        def nth(T, u, per=U):
            return T * per + (u + 1)

        def loads(T):
            return T // 2 + 1

        def live(T):
            return not isinstance(T, int) or 0 <= T < NT

        def bodies(eng, emit):
            for T in range(-2, first_full):
                emit(T, T % 2)
            with eng.Fori(0, (NT - 2 - first_full) // 2) as p:
                T = p * 2 + first_full
                emit(T, first_full % 2)
                emit(T + 1, (first_full + 1) % 2)
            for T in range(NT - 2, NT + LAG_DOWN):
                emit(T, T % 2)

        with nc.Block() as block:

            @block.sync
            def _(sp):
                W_ = weights

                def load_qkv(l, u):
                    for j in range(3):
                        sp.dma_start(w_qkv[:, u, j, :], W_["qkv"][l, :, (j * U + u) * 128:(j * U + u + 1) * 128]).then_inc(wq_in, 16)

                def load_out(l, u):
                    sp.dma_start(w_out[:, u, :], W_["out"][l, u * 128:(u + 1) * 128, :]).then_inc(wo_in, 16)

                def load_scales(l):
                    for j, nm in enumerate(("q_scale", "k_scale")):
                        src = W_[nm]
                        sp.dma_start(qk_scales[:, 2 * j, :], src[ds(l, 1), :].partition_broadcast(128)).then_inc(rep_in, 16)
                        sp.dma_start(qk_scales[:, 2 * j + 1, 0:32], src[ds(l, 1), 32:64].partition_broadcast(128)).then_inc(rep_in, 16)
                        sp.dma_start(qk_scales[:, 2 * j + 1, 32:64], src[ds(l, 1), 0:32].partition_broadcast(128)).then_inc(rep_in, 16)

                def load_ffn(l):
                    sp.dma_start(w_up[:, :], W_["w1"][l, :, :]).then_inc(wf_in, 16)
                    for c, (c0, cn) in enumerate(CH):
                        sp.dma_start(w_down[0:cn, c, :], W_["w2"][l, c0:c0 + cn, :]).then_inc(wf_in, 16)
                        for j in range(2):
                            sp.dma_start(b_up[0:cn, j, c:c + 1], W_["b1"][l, j * HID + c0:j * HID + c0 + cn].rearrange("(p o) -> p o", o=1)).then_inc(wf_in, 16)
                    sp.dma_start(b_down[:, :], W_["b2"][ds(l, 1), :].partition_broadcast(128)).then_inc(wf_in, 16)
                    sp.dma_start(ln_gb[:, 0:1], W_["ln_g"][l, :].rearrange("(p o) -> p o", o=1)).then_inc(wf_in, 16)
                    sp.dma_start(ln_gb[:, 1:2], W_["ln_b"][l, :].rearrange("(p o) -> p o", o=1)).then_inc(wf_in, 16)

                sp.dma_start(ident[:, :], tables["ident"]).then_inc(consts_in, 16)
                sp.dma_start(ident_bf[:, :], tables["ident_bf"]).then_inc(consts_in, 16)
                sp.dma_start(masks[:, :, :], tables[f"masks{W}"].rearrange("t p k -> p t k")).then_inc(consts_in, 16)
                sp.dma_start(frame[:, :], tables[f"frame{W}"]).then_inc(consts_in, 16)
                load_scales(0)

                def emit(T, par, next_weights=None, next_out=None):
                    pos = lambda t: t * 128 + t // TPB
                    if live(T + 2):
                        wait(sp, xT_ps, nth(T, 0, 1))
                        r = pos(T + 2)
                        sp.dma_start(x_in[:, par, 0:64], x_all[ds(r + 1, 128), 0:64]).then_inc(xin_in[par], 16)
                        sp.dma_start(x_in[:, par, 64:128], x_all[ds(r, 128), 64:128]).then_inc(xin_in[par], 16)
                        wait(sp, rot_done, nth(T, 0, 1))
                        sp.dma_start(rot_base[:, par, :], tables[f"rot{W}"][ds((T + 2) % TPB * 128, 128), :]).then_inc(rotb_in[par], 16)
                    if isinstance(T, int) and T == -2:
                        for u in range(U):
                            load_qkv(0, u)
                        for u in range(U):
                            load_out(0, u)
                        load_ffn(0)
                    if live(T):
                        wait(sp, mid_done, nth(T - 2, 0, 1))
                        sp.dma_start(x_res[:, par, :], x_all[ds(pos(T) + 1, 128), :]).then_inc(xres_in[par], 16)
                    if next_weights is not None:
                        l = next_weights
                        wait(sp, rot_done, nth(T + 1, 0, 1))
                        load_scales(l)
                        for u in range(U):
                            wait(sp, proj_ps, nth(T + 1, u))
                            load_qkv(l, u)
                    if next_out is not None:
                        for u in range(U):
                            wait(sp, wo_used, nth(T - LAG_RES, u))
                            load_out(next_out, u)
                    if live(T - LAG_DOWN):
                        wait(sp, new_done, nth(T - LAG_DOWN, 0, 1))
                        wait(sp, new_stored, T * 16 - 16 * LAG_DOWN)
                        sp.dma_start(x_all[ds(pos(T - LAG_DOWN + n_tiles) + 1, 128), :],
                                     x_new[:, (par + LAG_DOWN) % 2, :]).then_inc(new_stored, 16)
                    if live(T - LAG_RES):
                        t = T - LAG_RES
                        rp = (par + LAG_RES) % 2
                        wait(sp, mid_done, nth(t, 0, 1))
                        sp.dma_start(xb_dram[ds(pos(t) + 1, 128), :], x_mid[:, rp, :]).then_inc(mid_stored, 16)
                        sp.wait_ge(mid_stored, 16 * (t + 1))
                        wait(sp, fnorm_done, nth(t - 2, 0, 1))
                        sp.dma_start(f_in[:, rp, 0:64], xb_dram[ds(pos(t) + 1, 128), 0:64]).then_inc(fin_in[rp], 16)
                        sp.dma_start(f_in[:, rp, 64:128], xb_dram[ds(pos(t), 128), 64:128]).then_inc(fin_in[rp], 16)
                        wait(sp, fresb_done, nth(t - 2, 0, 1))
                        sp.dma_start(f_res[:, rp, :], xb_dram[ds(pos(t) + 1, 128), :]).then_inc(fres_in[rp], 16)

                def ffn_weights(T, l):
                    wait(sp, down_ps, nth(T, 0, 1))
                    wait(sp, fresb_done, nth(T, 0, 1))
                    load_ffn(l)

                lead = LAG_DOWN
                for T in range(-2, lead):
                    emit(T, T % 2)
                inner = n_tiles - 2 - lead
                with_layers = depth - 1

                def steady(first, count):
                    half = count // 2
                    if half:
                        with sp.Fori(0, half) as p:
                            emit(first + p * 2, lead % 2)
                            emit(first + p * 2 + 1, (lead + 1) % 2)
                    if count % 2:
                        emit(first + (count - 1), (lead + count - 1) % 2)

                with sp.Fori(0, with_layers) as l:
                    base = l * n_tiles
                    steady(base + lead, inner)
                    T = base + (n_tiles - 2)
                    emit(T, 0, next_weights=l + 1)
                    for j in range(-1, lead):
                        emit(base + n_tiles + j, j % 2, next_out=l + 1 if j == LAG_RES - 1 else None)
                    ffn_weights(base + n_tiles - 1, l + 1)
                steady((depth - 1) * n_tiles + lead, inner)
                for T in range(NT - 2, NT + LAG_DOWN):
                    emit(T, T % 2)
                sp.wait_ge(new_stored, 16 * NT)
                sp.wait_ge(mid_stored, 16 * NT)

            @block.tensor
            def _(pe):
                pe.wait_ge(consts_in, 64)
                pe.wait_ge(zeroed, 5)

                def score_head(t, tp, u, h):
                    rows = slice(64 * h, 64 * h + 64)
                    c0 = h * KW
                    nc.tensor.matmul(ps_s[u % 2][0:W, c0 + 128:c0 + KW], qkT[rows, u % 2, 0:W], k_prev[rows, (tp + 1) % 2, u, :],
                                     start=False, stop=False)
                    nc.tensor.matmul(ps_s[u % 2][:, c0:c0 + 128], qkT[rows, u % 2, 0:128], qkT[rows, u % 2, 128:256],
                                     start=False, stop=(h == 1)).then_inc(score_ps if h else score_half, 1)

                def emit(T, par):
                    for s in range(U):
                        t, d, u = unit(T, s, AT_SCORE)
                        if live(t):
                            tp = (par + d) % 2
                            b = ps_s[u % 2]
                            sc = b[:, 0:2 * KW].rearrange("p (h k) -> p h k", h=2)
                            wait(pe, exp_done, nth(t, u - 2))
                            pe.wait_ge(qkT_done, nth(t, u))
                            wait(pe, kprev_done, nth(t - 1, u))
                            nc.tensor.matmul(sc, ident_bf[:, :], masks[:, ds(t % TPB, 1), :].to_broadcast([128, 2, KW]), start=True, stop=False)
                            score_head(t, tp, u, 0)
                        if live(T + 1):
                            for u in proj_units[s]:
                                pe.wait_ge(xT_done, nth(T + 1, 0, 1))
                                pe.wait_ge(wq_in, 16 * 3 * U * ((T + 1) // n_tiles + 1))
                                n = nth(T + 1, u - 2)
                                wait(pe, sq_done, n)
                                wait(pe, val_done, n)
                                wait(pe, rotated, n)
                                if u < 2:
                                    wait(pe, hidden_done, nth(T - LAG_UP - 1, 0, 1))
                                nc.tensor.matmul(ps_q[u % 2][:, 0:384], xT[:, (par + 1) % 2, :], w_qkv[:, u, :, :].rearrange("p j n -> p (j n)"),
                                                 start=True, stop=True).then_inc(proj_ps, 1)
                        t, d, u = unit(T, s, AT_PT)
                        if live(t):
                            wait(pe, pT_done, nth(t, u - 1))
                            pe.wait_ge(probs_done, nth(t, u))
                            pr = probs[:, u % 4, :, :]
                            for h in range(2):
                                nc.tensor.transpose(ps_pt[:, 128 * h:128 * h + 128], pr[:, h, 0:128], ident[:, :])
                            for h in range(2):
                                last = nc.tensor.transpose(ps_pt[:, 256 + W * h:256 + W * h + W], pr[0:W, h, W:KW], ident[0:W, 0:W])
                            last.then_inc(pT_ps, 1)
                        t, d, u = unit(T, s, AT_SCORE)
                        if live(t):
                            pe.wait_ge(consts_in, 64)
                            pe.wait_ge(score_half, nth(t, u))
                            score_head(t, (par + d) % 2, u, 1)
                        if live(T):
                            pe.wait_ge(normed, nth(T, s))
                            wait(pe, qkT_done, nth(T, s - 1))
                            if s == 0:
                                wait(pe, xT_done, nth(T + 1, 0, 1) if live(T + 1) else NT)
                                wait(pe, fT_done, nth(T - 1 - LAG_UP, 0, 1))
                            if s == UPT_STEP + 1:
                                wait(pe, fT_done, nth(T - LAG_UP, 0, 1))
                            nc.tensor.transpose(ps_t[:, 0:128], qk[:, par, s, 0:128], ident[:, :])
                            nc.tensor.transpose(ps_t[:, 128:256], qk[:, par, s, 128:256], ident[:, :]).then_inc(qkT_ps, 1)
                        t, d, u = unit(T, s, AT_PV)
                        if live(t):
                            tp = (par + d) % 2
                            wait(pe, outT_done, nth(t, u - 1))
                            if s == (DOWN_STEP + 1) % U:
                                wait(pe, new_done, nth(T - LAG_DOWN, 0, 1))
                            pe.wait_ge(pT_done, nth(t, u))
                            pe.wait_ge(val_done, nth(t, u))
                            wait(pe, vprev_done, nth(t - 1, u))
                            for h in range(2):
                                nc.tensor.matmul(ps_o[64 * h:64 * h + 64, 0:128], val[:, tp, u, 64 * h:64 * h + 64],
                                                 probsT[:, u % 2, 128 * h:128 * h + 128], start=True, stop=False)
                                last = nc.tensor.matmul(ps_o[64 * h:64 * h + 64, 0:W], v_prev[128 - W:128, (tp + 1) % 2, u, 64 * h:64 * h + 64],
                                                        probsT[128 - W:128, u % 2, 256 + W * h:256 + W * h + W], start=False, stop=True)
                            last.then_inc(pv_ps, 1)
                        t, d, u = unit(T, s, AT_OUT)
                        if live(t):
                            pe.wait_ge(outT_done, nth(t, u))
                            pe.wait_ge(wo_in, 16 * U * (t // n_tiles + 1))
                            if u == 0:
                                wait(pe, mid_done, nth(t - 1, 0, 1))
                            last = nc.tensor.matmul(ps_y[:, 0:128], outT[:, u % 2, :], w_out[:, u, :], start=(u == 0), stop=(u == U - 1))
                            last.then_inc(wo_used, 1)
                        if s == DOWN_STEP and live(T - LAG_DOWN):
                            t = T - LAG_DOWN
                            pe.wait_ge(hidden_done, nth(t, 0, 1))
                            wait(pe, new_done, nth(t - 1, 0, 1))
                            tt, d, u = unit(T, s, AT_PV)
                            wait(pe, outT_done, nth(tt, u) if live(tt) else NT * U)
                            for c, (c0, cn) in enumerate(CH):
                                last = nc.tensor.matmul(ps_o[:, 0:128], hidden[0:cn, c, :], w_down[0:cn, c, :], start=(c == 0), stop=(c == 2))
                            last.then_inc(down_ps, 1)
                        if s == UPT_STEP and live(T - LAG_UP):
                            pe.wait_ge(fnorm_done, nth(T - LAG_UP, 0, 1))
                            wait(pe, qkT_done, nth(T, s) if live(T) else NT * U)
                            wait(pe, fT_done, nth(T - LAG_UP - 1, 0, 1))
                            nc.tensor.transpose(ps_t[:, 0:128], f_norm[:, :], ident[:, :]).then_inc(fT_ps, 1)
                        if s == U - 1 and live(T + 2):
                            pe.wait_ge(xin_in[par], 32 * loads(T + 2))
                            wait(pe, qkT_done, nth(T, s))
                            wait(pe, xT_done, nth(T + 1, 0, 1))
                            if live(T - LAG_UP):
                                wait(pe, fT_done, nth(T - LAG_UP, 0, 1))
                            nc.tensor.transpose(ps_t[:, 0:128], x_in[:, par, :], ident[:, :]).then_inc(xT_ps, 1)
                        if s == UP_STEP and live(T - LAG_UP):
                            t = T - LAG_UP
                            pe.wait_ge(fT_done, nth(t, 0, 1))
                            pe.wait_ge(wf_in, 16 * 13 * (t // n_tiles + 1))
                            n = nth(T + 1, U - 1) if live(T + 1) else NT * U
                            wait(pe, sq_done, n)
                            wait(pe, val_done, n)
                            wait(pe, rotated, n)
                            wait(pe, hidden_done, nth(t - 1, 0, 1))
                            for j in range(2):
                                for c, (c0, cn) in enumerate(CH):
                                    last = nc.tensor.matmul(ps_q[j][0:cn, 128 * c:128 * c + 128], w_up[:, j * HID + c0:j * HID + c0 + cn],
                                                            f_normT[:, :], start=True, stop=True)
                            last.then_inc(up_ps, 1)

                bodies(pe, emit)

            @block.scalar
            def _(act):
                act.wait_ge(consts_in, 64)

                def emit(T, par):
                    for s in range(U):
                        if live(T + 1):
                            for u in proj_units[s]:
                                act.wait_ge(proj_ps, nth(T + 1, u))
                                wait(act, ss_done, nth(T + 1, u - 2))
                                nc.scalar.activation(squares[:, u % 2, :], ps_q[u % 2][:, 0:256], ACT.Square).then_inc(sq_done, 1)
                                wait(act, pv_ps, nth(T - 1, u))
                                wait(act, vprev_done, nth(T - 1, u))
                                nc.scalar.activation(val[:, (par + 1) % 2, u, :], ps_q[u % 2][:, 256:384], ACT.Copy).then_inc(val_done, 1)
                        if live(T):
                            act.wait_ge(qkT_ps, nth(T, s))
                            wait(act, score_ps, nth(T, s - 2))
                            wait(act, kprev_done, nth(T, s - 2))
                            nc.scalar.activation(qkT[:, s % 2, :], ps_t[:, 0:256], ACT.Copy).then_inc(qkT_done, 1)
                        t, d, u = unit(T, s, AT_MAX)
                        if live(t):
                            act.wait_ge(max_done, nth(t, u))
                            wait(act, pT_ps, nth(t, u - 4))
                            sc = ps_s[u % 2][:, 0:2 * KW].rearrange("p (h k) -> p h k", h=2)
                            for h in range(2):
                                last = nc.scalar.activation(probs[:, u % 4, h, :], sc[:, h, :], ACT.Exp, bias=neg_max[:, u % 4, h:h + 1], scale=1.0,
                                                            accum_out=p_sum[:, u % 4, h:h + 1])
                            last.then_inc(exp_done, 1)
                        t, d, u = unit(T, s, AT_PT)
                        if live(t):
                            act.wait_ge(pT_ps, nth(t, u))
                            wait(act, pv_ps, nth(t, u - 2))
                            nc.scalar.activation(probsT[:, u % 2, :], ps_pt[:, 0:256 + 2 * W], ACT.Copy).then_inc(pT_done, 1)
                        t, d, u = unit(T, s, AT_PV)
                        if live(t):
                            act.wait_ge(pv_ps, nth(t, u))
                            wait(act, wo_used, nth(t, u - 2))
                            nc.scalar.activation(outT[:, u % 2, :], ps_o[:, 0:128], ACT.Copy).then_inc(outT_done, 1)
                        if s == UPT_STEP and live(T - LAG_UP):
                            act.wait_ge(fT_ps, nth(T - LAG_UP, 0, 1))
                            act.wait_ge(wf_in, 16 * 13 * ((T - LAG_UP) // n_tiles + 1))
                            wait(act, up_ps, nth(T - LAG_UP - 1, 0, 1))
                            nc.scalar.activation(f_normT[:, :], ps_t[:, 0:128], ACT.Identity, bias=ln_gb[:, 1:2], scale=ln_gb[:, 0:1]).then_inc(fT_done, 1)
                        if s == U - 1 and live(T + 2):
                            act.wait_ge(xT_ps, nth(T + 2, 0, 1))
                            wait(act, proj_ps, nth(T, U - 1))
                            nc.scalar.activation(xT[:, par, :], ps_t[:, 0:128], ACT.Copy).then_inc(xT_done, 1)
                        if s == UP_STEP and live(T - LAG_UP):
                            act.wait_ge(up_ps, nth(T - LAG_UP, 0, 1))
                            wait(act, hidden_done, nth(T - LAG_UP - 1, 0, 1))
                            for c, (c0, cn) in enumerate(CH):
                                last = nc.scalar.activation(gate[0:cn, c, :], ps_q[1][0:cn, 128 * c:128 * c + 128], ACT.Gelu, bias=b_up[0:cn, 1, c:c + 1], scale=1.0)
                            last.then_inc(gelu_done, 1)

                bodies(act, emit)

            @block.vector
            def _(dve):
                nc.vector.memset(hidden[:, :, :], 0.0).then_inc(zeroed, 1)
                nc.vector.memset(k_prev[:, 1, :, :], 0.0).then_inc(zeroed, 1)
                nc.vector.memset(v_prev[:, 1, :, :], 0.0).then_inc(zeroed, 1)
                nc.vector.memset(mean_var[:, :], 1.0).then_inc(zeroed, 1)
                nc.vector.memset(sumsq[:, :], 1.0).then_inc(zeroed, 1)
                dve.wait_ge(zeroed, 5)
                dve.wait_ge(consts_in, 64)
                R4 = lambda ap: ap.rearrange("p (a h t x) -> p a h t x", a=2, h=2, t=2)

                def emit(T, par):
                    np_ = (par + 1) % 2
                    for s in range(U):
                        if live(T + 1):
                            for u in proj_units[s]:
                                dve.wait_ge(val_done, nth(T + 1, u))
                                if u == 0:
                                    dve.wait_ge(rot_done, nth(T + 1, 0, 1))
                                wait(dve, added, nth(T + 1, u - 2))
                                qkp = R4(ps_q[u % 2][:, 0:256])
                                cs = rot[:, np_, :, :].rearrange("p (a c) (o t x) -> p a c o t x", a=2, c=2, o=1, t=2)
                                nc.vector.tensor_tensor(R4(cos_part[:, u % 2, :]), qkp, cs[:, :, 0, :, :, :].to_broadcast([128, 2, 2, 2, 32]), ALU.mult)
                                nc.vector.tensor_tensor(R4(sin_part[:, u % 2, :]), qkp[:, :, :, ::-1, :], cs[:, :, 1, :, :, :].to_broadcast([128, 2, 2, 2, 32]), ALU.mult).then_inc(rotated, 1)
                                nc.vector.tensor_reduce(sumsq[:, 4 * u:4 * u + 4], squares[:, u % 2, :].rearrange("p (g d) -> p g d", g=4), AX.X, ALU.add).then_inc(ss_done, 1)
                        t, d, u = unit(T, s, AT_MAX)
                        if live(t):
                            dve.wait_ge(score_ps, nth(t, u))
                            wait(dve, exp_done, nth(t, u - 4))
                            sc = ps_s[u % 2][:, 0:2 * KW].rearrange("p (h k) -> p h k", h=2)
                            nc.vector.tensor_reduce(neg_max[:, u % 4, :], sc, AX.X, ALU.max, negate=True).then_inc(max_done, 1)
                        t, d, u = unit(T, s, AT_NORM)
                        if live(t):
                            dve.wait_ge(exp_done, nth(t, u))
                            wait(dve, probs_done, nth(t, u - 1))
                            nc.vector.reciprocal(p_rec[:, :], p_sum[:, u % 4, :]).then_inc(rec_done, 1)
                            dve.wait_ge(rec_done, nth(t, u))
                            pr = probs[:, u % 4, :, :]
                            nc.vector.tensor_tensor(pr, pr, p_rec[:, :].rearrange("p (h o) -> p h o", o=1).to_broadcast([128, 2, KW]), ALU.mult).then_inc(probs_done, 1)
                        if live(T):
                            dve.wait_ge(qkT_done, nth(T, s))
                            wait(dve, score_ps, nth(T - 1, s))
                            nc.vector.tensor_scalar(k_prev[:, par, s, :], qkT[:, s % 2, 256 - W:256], frame[:, 0:1], None, ALU.mult).then_inc(kprev_done, 1)
                            dve.wait_ge(val_done, nth(T, s))
                            wait(dve, pv_ps, nth(T - 1, s))
                            nc.vector.tensor_copy(v_prev[128 - W:128, par, s, :], val[128 - W:128, par, s, :]).then_inc(vprev_done, 1)
                        t, d, u = unit(T, s, AT_OUT)
                        if live(t) and u == U - 1:
                            tp = (par + d) % 2
                            dve.wait_ge(wo_used, nth(t, u))
                            dve.wait_ge(xres_in[tp], 16 * loads(t))
                            wait(dve, mid_stored, 16 * (t - 1))
                            nc.vector.tensor_tensor(x_mid[:, tp, :], ps_y[:, 0:128], x_res[:, tp, :], ALU.add).then_inc(mid_done, 1)
                        if s == DOWN_STEP and live(T - LAG_DOWN):
                            t = T - LAG_DOWN
                            tp = (par + LAG_DOWN) % 2
                            dve.wait_ge(down_ps, nth(t, 0, 1))
                            dve.wait_ge(fresb_done, nth(t, 0, 1))
                            wait(dve, new_stored, 16 * (t - 1))
                            nc.vector.tensor_tensor(x_new[:, tp, :], ps_o[:, 0:128], f_resb[:, :], ALU.add).then_inc(new_done, 1)
                        if s == NORM_STEP and (live(T + 1) or live(T - LAG_UP)):
                            Tc = T + 1
                            if live(T - LAG_UP):
                                t = T - LAG_UP
                                fp = (par + LAG_UP) % 2
                                dve.wait_ge(fin_in[fp], 32 * loads(t))
                                wait(dve, fnorm_done, nth(t - 1, 0, 1))
                                nc.vector.bn_stats(stats[:, :], f_in[:, fp, :]).then_inc(stats_done, 1)
                                dve.wait_ge(stats_done, nth(t, 0, 2))
                            r = rnorm[:, np_, :]
                            ri = r.bitcast(I32)
                            k = [0]

                            def link(ins, settle=True):
                                k[0] += 1
                                ins.then_inc(chain, 1)
                                if settle:
                                    dve.wait_ge(chain, Tc * CHAIN + k[0])

                            if live(T + 1):
                                dve.wait_ge(ss_done, nth(T + 1, U - 1))
                            wait(dve, normed, nth(T - 1, U - 1) if live(T - 1) else NT * U if not isinstance(T, int) or T > 0 else 0)
                            link(nc.vector.tensor_scalar(nw_x[:, 0:NV - 1], sumsq[:, :], 1e-24, None, ALU.max), settle=False)
                            if live(T - LAG_UP):
                                t = T - LAG_UP
                                nc.vector.bn_aggr(mean_var[:, :], stats[:, :]).then_inc(stats_done, 1)
                                dve.wait_ge(stats_done, nth(t, 1, 2))
                            link(nc.vector.tensor_scalar(nw_x[:, NV - 1:NV], mean_var[:, 1:2], 1e-5, None, ALU.add))
                            link(nc.vector.tensor_scalar(ri, nw_x[:, :].bitcast(I32), -0.5, 1597463007.0, ALU.mult, ALU.add))
                            link(nc.vector.tensor_scalar(nw_h[:, :], nw_x[:, :], -0.5, None, ALU.mult))
                            for _ in range(NEWTONS):
                                link(nc.vector.tensor_tensor(nw_a[:, :], r, r, ALU.mult))
                                link(nc.vector.tensor_tensor(nw_a[:, :], nw_a[:, :], nw_h[:, :], ALU.mult))
                                link(nc.vector.scalar_tensor_tensor(r, nw_a[:, :], 1.5, r, ALU.add, ALU.mult))
                            if live(T - LAG_UP):
                                t = T - LAG_UP
                                wait(dve, fT_ps, nth(t - 1, 0, 1))
                                nc.vector.tensor_scalar(f_norm[:, :], f_in[:, fp, :], mean_var[:, 0:1], rnorm[:, np_, NV - 1:NV], ALU.subtract, ALU.mult).then_inc(fnorm_done, 1)
                        if s == UP_STEP and live(T - LAG_UP):
                            t = T - LAG_UP
                            dve.wait_ge(gelu_done, nth(t, 0, 1))
                            wait(dve, down_ps, nth(t - 1, 0, 1))
                            for c, (c0, cn) in enumerate(CH):
                                last = nc.vector.scalar_tensor_tensor(hidden[0:cn, c, :], ps_q[0][0:cn, 128 * c:128 * c + 128], b_up[0:cn, 0, c:c + 1],
                                                                      gate[0:cn, c, :], ALU.add, ALU.mult)
                            last.then_inc(hidden_done, 1)

                bodies(dve, emit)

            @block.gpsimd
            def _(pool):
                def emit(T, par):
                    np_ = (par + 1) % 2
                    for s in range(U):
                        if live(T + 1):
                            for u in proj_units[s]:
                                pool.wait_ge(rotated, nth(T + 1, u))
                                wait(pool, qkT_ps, nth(T - 1, u))
                                nc.gpsimd.tensor_tensor(qk[:, np_, u, :], cos_part[:, u % 2, :], sin_part[:, u % 2, :], ALU.add).then_inc(added, 1)
                        if s == NORM_STEP:
                            if live(T + 1):
                                pool.wait_ge(chain, (T + 2) * CHAIN)
                                pool.wait_ge(added, nth(T + 1, U - 1))
                                for u in range(U):
                                    v = qk[:, np_, u, :].rearrange("p (g d) -> p g d", g=4)
                                    rr = rnorm[:, np_, 4 * u:4 * u + 4].rearrange("p (g o) -> p g o", o=1).to_broadcast([128, 4, 64])
                                    nc.gpsimd.tensor_tensor(v, v, rr, ALU.mult).then_inc(normed, 1)
                            if live(T + 2):
                                pool.wait_ge(rotb_in[par], 16 * loads(T + 2))
                                pool.wait_ge(rep_in, 16 * 6 * ((T + 2) // n_tiles + 1))
                                wait(pool, rotated, nth(T, U - 1))
                                nc.gpsimd.tensor_tensor(rot[:, par, :, :].rearrange("p a d -> p (a d)"), rot_base[:, par, :], qk_scales[:, :, :].rearrange("p a d -> p (a d)"), ALU.mult).then_inc(rot_done, 1)
                            if live(T - LAG_UP):
                                t = T - LAG_UP
                                pool.wait_ge(fres_in[(par + LAG_UP) % 2], 16 * loads(t))
                                pool.wait_ge(wf_in, 16 * 13 * (t // n_tiles + 1))
                                wait(pool, new_done, nth(t - 1, 0, 1))
                                nc.gpsimd.tensor_tensor(f_resb[:, :], f_res[:, (par + LAG_UP) % 2, :], b_down[:, :], ALU.add).then_inc(fresb_done, 1)

                bodies(pool, emit)


def two_layer_kernel(nc, t, out):
    dram = lambda n, shape: nc.dram_tensor(n, shape, F32, kind="Internal").ap()
    qkv = [dram(f"l0_{n}", [4096, 128]) for n in "qkv"]
    x_all0 = dram("x_all0", [7 * ROWS, 128])
    x_mid0 = dram("x_mid0", [6 * ROWS, 128])
    x_all1 = dram("x_all1", [3 * ROWS, 128])
    x_mid1 = dram("x_mid1", [2 * ROWS, 128])
    with ExitStack() as ctx:
        mods = ctx.enter_context(nc.sbuf_tensor("mods", [128, 4, 6, 128], F32))
        xr = ctx.enter_context(nc.sbuf_tensor("xr", [128, TILES, 128], F32))
        zero_rows(nc, (x_all0, x_mid0, x_all1, x_mid1), t["zeros"])
        modulation_stage(nc, mods, [t["L0_c"], t["L1_c"]], [t["L0_wmod"], t["L1_wmod"]])
        delta_attention_stage(nc, t["L0_attn_x"], xr, mods, [t["L0_attn_WqT"], t["L0_attn_WkT"], t["L0_attn_WvT"]], t["L0_attn_WoT"],
                              t["L0_attn_alpha_raw"], t["L0_attn_beta_raw"], t, qkv)
        feed_stage(nc, "feed0", xr, mods, 0, x_all0)
        names = dict(qkv="Wqkv", out="Wo", w1="W1", w2="W2", b1="b1", b2="b2", ln_g="ln_g", ln_b="ln_b", q_scale="q_scale", k_scale="k_scale")
        local_block_stage(nc, "L0", 6, 16, 32, x_all0, x_mid0, {k: t["L0_ffn_" + v] for k, v in names.items()}, t, TILES)
        residual_stage(nc, "res0", xr, mods, 0, x_all0[6 * ROWS:7 * ROWS, :])
        linear_attention_stage(nc, xr, mods, {k[8:]: v for k, v in t.items() if k.startswith("L1_attn_")}, t)
        feed_stage(nc, "feed1", xr, mods, 1, x_all1)
        local_block_stage(nc, "L1", 2, 8, 64, x_all1, x_mid1, {k: t["L1_ffn_" + v.lower()] for k, v in names.items()}, t, TILES)
        residual_stage(nc, "res1", xr, mods, 2, x_all1[2 * ROWS:3 * ROWS, :], out)


def zero_rows(nc, arrays, zeros):
    with stage_semaphores(nc, "zr") as sem, nc.Block() as block:
        stored = sem("stored")

        @block.sync
        def _(sp):
            total = 0
            for a in arrays:
                n = a.shape[0] // 2049
                sp.dma_start(a.rearrange("(n r) d -> n r d", r=2049)[:, 0, :], zeros[0:n, :]).then_inc(stored, 16)
                total += 16
            sp.wait_ge(stored, total)


def rotary_table(window, n=2048, dim=64):
    half = np.arange(0, dim, 2, dtype=np.float32)
    inv = (np.float32(1.0) / np.float32(10000.0) ** (half / np.float32(dim))).astype(np.float32)
    angle = (np.arange(n, dtype=np.float32)[:, None] * inv[None, :]).astype(np.float32).astype(np.float64)
    base = (half.astype(np.float64) + 0.4 * dim) / (1.4 * dim)
    scale = base[None, :] ** ((np.arange(n) % 128 - 64) / (window // 2))[:, None]
    out = np.zeros((n, 2, 2, dim))
    for a, f in ((0, 8.0 * scale), (1, 1.0 / scale)):
        out[:, a, 0, :] = np.tile(np.cos(angle) * f, 2)
        out[:, a, 1, :] = np.concatenate([-np.sin(angle) * f, np.sin(angle) * f], 1)
    frame = np.tile(base, 4) ** (128 / (window // 2))
    return out.reshape(n, 256).astype(np.float32), frame.reshape(128, 1).astype(np.float32)


def window_masks(window, tiles):
    q, k = np.arange(128)[:, None], np.arange(128)[None, :]
    own = (k <= q) & (q <= k + window) & (q // window - k // window <= 1)
    before = (q <= np.arange(window)[None, :]) & (q < window)
    m = np.zeros((tiles, 128, 128 + window), np.float32)
    for t in range(tiles):
        m[t, :, :128] = np.where(own, 0, -1e30)
        m[t, :, 128:] = np.where(before & (t > 0), 0, -1e30)
    return m.astype(mybir.dt.np(BF16))


def shape_constants():
    p = np.arange(128)
    c = {"ident": np.eye(128, dtype=np.float32), "ident_bf": np.eye(128, dtype=np.float32).astype(mybir.dt.np(BF16)),
         "zeros": np.zeros((16, 128), np.float32), "block01": (p[:, None] // 8 == np.arange(16)[None, :]).astype(np.float32),
         "causal64": np.where(p[:, None] % 64 >= np.arange(64)[None, :], 0, -1e30).astype(mybir.dt.np(BF16)),
         "keep": (p[:, None] <= p[None, :]).astype(np.float32)}
    for w in (32, 64):
        c[f"rot{w}"], c[f"frame{w}"] = rotary_table(w)
        c[f"masks{w}"] = window_masks(w, 16)
    return c


def kernel(**inputs):
    import concourse.bacc as bacc
    from concourse.bass_utils import run_bass_kernel_spmd

    nc = bacc.Bacc("TRN2", target_bir_lowering=False, num_devices=1)
    transposed = {"L0_attn_Wq", "L0_attn_Wk", "L0_attn_Wv", "L0_attn_Wo", "L1_attn_q_w", "L1_attn_k_w", "L1_attn_v_w", "L1_attn_o_w", "L1_attn_f1_w", "L1_attn_f2_w"}
    arrays = {}
    for name, a in inputs.items():
        a = np.asarray(a)
        if name in transposed:
            name, a = name + "T", a.T
        arrays[name] = np.ascontiguousarray(a)
    arrays.update(shape_constants())
    t = {n: nc.dram_tensor("in_" + n, a.shape, mybir.dt.from_np(a.dtype), kind="ExternalInput").ap() for n, a in arrays.items()}
    out = nc.dram_tensor("out_x", (2, 2048, 128), F32, kind="ExternalOutput").ap()
    two_layer_kernel(nc, t, out)
    r = run_bass_kernel_spmd(nc, [{"in_" + n: a for n, a in arrays.items()}], core_ids=[0])
    return r.results[0]["out_x"]
```

```python
from contextlib import ExitStack, contextmanager

import numpy as np

import concourse.bass as bass
from concourse import mybir
from concourse.bass import ds

F32, BF16, I32 = mybir.dt.float32, mybir.dt.bfloat16, mybir.dt.int32
ACT = mybir.ActivationFunctionType
ALU = mybir.AluOpType
AX = mybir.AxisListType
LN_EPS = 1e-5
TILES = 32
ROWS = 2 * 2049


class Steps:

    def __init__(self, eng, sem):
        self.eng, self.sem, self.base, self.n = eng, sem, 0, 0

    def __call__(self, ins, settle=True):
        self.n += 1
        ins.then_inc(self.sem, 1)
        if settle:
            self.eng.wait_ge(self.sem, self.base + self.n)
        return self.base + self.n

    def settle(self):
        self.eng.wait_ge(self.sem, self.base + self.n)

    def turn(self, before, i, per):
        self.base, self.n = before + i * per, 0


@contextmanager
def stage_semaphores(nc, prefix):
    taken = []

    def take(name):
        taken.append(nc.alloc_semaphore(name=f"{prefix}_{name}"))
        return taken[-1]

    yield take
    nc.clear_and_free_semaphores(taken)
    nc.all_engine_barrier()


def wait(eng, sem, value):
    if not isinstance(value, int) or value > 0:
        eng.wait_ge(sem, value)


def pairs(eng, n, emit):
    emit(0, 0)
    emit(1, 1)
    with eng.Fori(1, n // 2) as p:
        emit(p * 2, 0)
        emit(p * 2 + 1, 1)


def inverse_root(step, nc, out, x, half, tmp, newtons=3):
    step(nc.vector.tensor_scalar(out.bitcast(I32), x.bitcast(I32), -0.5, 1597463007.0, ALU.mult, ALU.add))
    step(nc.vector.tensor_scalar(half, x, -0.5, None, ALU.mult))
    for _ in range(newtons):
        step(nc.vector.tensor_tensor(tmp, out, out, ALU.mult))
        step(nc.vector.tensor_tensor(tmp, tmp, half, ALU.mult))
        step(nc.vector.scalar_tensor_tensor(out, tmp, 1.5, out, ALU.add, ALU.mult))


def group_stats(nc, dve, step, x, mean, rstd, bufs):
    st, mv, var, half, tmp = bufs
    for g in range(8):
        for j in range(4):
            step(nc.vector.bn_stats(st[:, j, :], x[:, 4 * g + j, :]), settle=(j == 3))
        for j in range(4):
            step(nc.vector.bn_aggr(mv[:, j, :], st[:, j, :]), settle=(j == 3))
        step(nc.vector.tensor_copy(mean[:, 4 * g:4 * g + 4], mv[:, :, 0]))
        step(nc.vector.tensor_scalar(var[:, 4 * g:4 * g + 4], mv[:, :, 1], LN_EPS, None, ALU.add))
    inverse_root(step, nc, rstd[:, :], var[:, :], half[:, :], tmp[:, :])


def modulated_group(nc, step, x, mean, rstd, out, mods, g, layer, part, done):
    for j in range(4):
        T = 4 * g + j
        step(nc.vector.tensor_scalar(out[:, j, :], x[:, T, :], mean[:, T:T + 1], rstd[:, T:T + 1], ALU.subtract, ALU.mult), settle=(j == 3))
    k = g // 4 + 2 * layer
    vec = lambda i: mods[:, k:k + 1, 3 * part + i, :].to_broadcast([128, 4, 128])
    step(nc.vector.tensor_tensor(out, out, vec(1), ALU.mult))
    nc.vector.tensor_tensor(out, out, vec(0), ALU.add).then_inc(done, 1)


def modulation_stage(nc, mods, c_rows, w_mod):
    with ExitStack() as ctx:
        sb = lambda n, shape, dt=F32: ctx.enter_context(nc.sbuf_tensor(f"mod_{n}", shape, dt))
        sem = ctx.enter_context(stage_semaphores(nc, "mod"))
        c = sb("c", [128, 4])
        e = sb("e", [128, 4])
        silu = sb("silu", [128, 4])
        wide = sb("wide", [128, 4, 128])
        w = sb("w", [128, 2, 768])
        sign = sb("sign", [128, 128])
        mag = sb("mag", [128, 128])
        ps = [[ctx.enter_context(nc.psum_tensor(f"mod_ps{k}{j}", [128, 512], F32)) for j in range(2)] for k in range(4)]
        loaded, exped, wide_done, product, seq = sem("loaded"), sem("exped"), sem("wide_done"), sem("product"), sem("seq")
        with nc.Block() as block:
            @block.sync
            def _(sp):
                for l in range(2):
                    sp.dma_start(w[:, l, :], w_mod[l]).then_inc(loaded, 16)
                    for b in range(2):
                        sp.dma_start(c[:, 2 * l + b:2 * l + b + 1], c_rows[l][b, :].rearrange("(p o) -> p o", o=1)).then_inc(loaded, 16)

            @block.scalar
            def _(act):
                act.wait_ge(loaded, 96)
                nc.scalar.activation(e[:, :], c[:, :], ACT.Exp, scale=-1.0).then_inc(exped, 1)

            @block.tensor
            def _(pe):
                pe.wait_ge(loaded, 96)
                pe.wait_ge(wide_done, 1)
                for k in range(4):
                    for j in range(2):
                        last = nc.tensor.matmul(ps[k][j][:, 0:384], wide[:, k, :], w[:, k // 2, 384 * j:384 * j + 384], start=True, stop=True)
                last.then_inc(product, 1)

            @block.vector
            def _(dve):
                step = Steps(dve, seq)
                dve.wait_ge(exped, 1)
                step(nc.vector.tensor_scalar(e[:, :], e[:, :], 1.0, None, ALU.add))
                step(nc.vector.reciprocal(e[:, :], e[:, :]))
                step(nc.vector.tensor_tensor(silu[:, :], e[:, :], c[:, :], ALU.mult))
                nc.vector.tensor_copy(wide[:, :, :], silu[:, :].rearrange("p (k o) -> p k o", o=1).to_broadcast([128, 4, 128])).then_inc(wide_done, 1)
                dve.wait_ge(product, 1)
                for k in range(4):
                    for j in range(2):
                        src = ps[k][j]
                        out = mods[:, k, 3 * j:3 * j + 3, :]
                        step(nc.vector.tensor_copy(out[:, 0, :], src[:, 0:128]))
                        step(nc.vector.tensor_scalar(out[:, 1, :], src[:, 128:256], 1.0, None, ALU.add))
                        step(nc.vector.tensor_scalar(sign[:, :], src[:, 256:384], 0.0, 2.0, ALU.is_ge, ALU.mult))
                        step(nc.vector.tensor_scalar(mag[:, :], src[:, 256:384], -1.0, 0.25, ALU.mult, ALU.max))
                        step(nc.vector.scalar_tensor_tensor(mag[:, :], src[:, 256:384], 0.25, mag[:, :], ALU.max, ALU.max))
                        step(nc.vector.scalar_tensor_tensor(out[:, 2, :], sign[:, :], -1.0, mag[:, :], ALU.add, ALU.mult))


def delta_attention_stage(nc, x_dram, xr, mods, w_qkvT, w_oT, alpha_raw, beta_raw, tables, qkv_dram):
    H, DH, SUB, N_SUB = 16, 8, 32, 128
    with ExitStack() as ctx:
        sem = ctx.enter_context(stage_semaphores(nc, "da"))
        keep = lambda n, shape, dt=F32: ctx.enter_context(nc.sbuf_tensor(f"da_{n}", shape, dt))
        mem = keep("mem", [128, 64, 128])
        ident = keep("ident", [128, 128])
        block01 = keep("block01", [128, 16])
        trans_a = keep("trans_a", [128, DH, N_SUB])
        trans_b = keep("trans_b", [128, DH, N_SUB])

        with ExitStack() as c2:
            sb = lambda n, shape, dt=F32: c2.enter_context(nc.sbuf_tensor(f"da_{n}", shape, dt))
            ps = [c2.enter_context(nc.psum_tensor(f"da_psa{i}", [128, 512], F32)) for i in range(8)]
            hT = sb("hT", [128, 4096])
            st, mv = sb("st", [128, 4, 6]), sb("mv", [128, 4, 2])
            mean, var, rstd, half, tmp = (sb(n, [128, 32]) for n in ("mean", "var", "rstd", "half", "tmp"))
            h = sb("h", [128, 2, 4, 128])
            w3 = sb("w3", [128, 384])
            qs = sb("qs", [128, SUB, 128])
            ks = sb("ks", [128, SUB, 128])
            vs = sb("vs", [128, SUB, 128])
            state = sb("state", [128, H, 16, DH])
            prod = sb("prod", [128, H, 16, DH])
            dots = sb("dots", [128, H, 16])
            flat_state = prod[:, :, :, :].rearrange("p a b c -> p a (b c)")
            rk, rk_half, rk_tmp, rk_x = (sb(n, [128, SUB * H]) for n in ("rk", "rk_half", "rk_tmp", "rk_x"))
            alpha, beta = sb("alpha", [128, H]), sb("beta", [128, H])
            loaded, seq, h_ready, hT_ps, hT_done = (sem(n) for n in ("loaded", "seq", "h_ready", "hT_ps", "hT_done"))
            proj_ps, q_out, k_out, v_out, sig_exp = (sem(n) for n in ("proj_ps", "q_out", "k_out", "v_out", "sig_exp"))
            k_normed, stored, state_done, tr_ps, tr_done = (sem(n) for n in ("k_normed", "stored", "state_done", "tr_ps", "tr_done"))

            with nc.Block() as block:
                @block.sync
                def _(sp):
                    for b in range(2):
                        sp.dma_start(xr[:, 16 * b:16 * b + 16, :], x_dram[b].rearrange("(t p) d -> p t d", p=128)).then_inc(loaded, 16)
                    sp.dma_start(ident[:, :], tables["ident"]).then_inc(loaded, 16)
                    sp.dma_start(block01[:, :], tables["block01"]).then_inc(loaded, 16)
                    for j in range(3):
                        sp.dma_start(w3[:, 128 * j:128 * j + 128], w_qkvT[j]).then_inc(loaded, 16)
                    sp.dma_start(alpha[:, :], alpha_raw.rearrange("a h b c -> (a b c) h").partition_broadcast(128)).then_inc(loaded, 16)
                    sp.dma_start(beta[:, :], beta_raw.rearrange("a h b c -> (a b c) h").partition_broadcast(128)).then_inc(loaded, 16)
                    sp.wait_ge(q_out, SUB)
                    sp.dma_start(qkv_dram[0].rearrange("(s t) d -> s t d", t=SUB), qs[:, :, :]).then_inc(stored, 16)
                    sp.wait_ge(v_out, SUB)
                    sp.dma_start(qkv_dram[2].rearrange("(s t) d -> s t d", t=SUB), vs[:, :, :]).then_inc(stored, 16)
                    sp.wait_ge(stored, 32)
                    sp.wait_ge(k_normed, 1)
                    sp.dma_start(qkv_dram[1].rearrange("(s t) d -> s t d", t=SUB), ks[:, :, :]).then_inc(stored, 16)
                    sp.wait_ge(stored, 48)

                @block.tensor
                def _(pe):
                    pe.wait_ge(loaded, 144)
                    for g in range(8):
                        pe.wait_ge(h_ready, g + 1)
                        wait(pe, hT_done, g - 1)
                        for i in range(4):
                            last = nc.tensor.transpose(ps[g % 2][:, 128 * i:128 * i + 128], h[:, g % 2, i, :], ident[:, :])
                        last.then_inc(hT_ps, 1)
                    pe.wait_ge(hT_done, 8)
                    for t in range(SUB):
                        wait(pe, q_out, t - 3)
                        wait(pe, v_out, t - 3)
                        nc.tensor.matmul(ps[2 + t % 4][:, 0:384], hT[:, t:4096:SUB], w3[:, :], start=True, stop=True).then_inc(proj_ps, 1)
                    pe.wait_ge(state_done, 1)
                    pe.wait_ge(v_out, SUB)
                    for j in range(4):
                        wait(pe, tr_done, 2 * (j - 1))
                        for i in range(4):
                            n = 4 * j + i
                            last = nc.tensor.transpose(ps[j % 2][:, 128 * i:128 * i + 128], flat_state[:, n, :], ident[:, :])
                        last.then_inc(tr_ps, 1)

                @block.scalar
                def _(act):
                    act.wait_ge(loaded, 144)
                    nc.scalar.activation(alpha[:, :], alpha[:, :], ACT.Exp, scale=-1.0).then_inc(sig_exp, 1)
                    nc.scalar.activation(beta[:, :], beta[:, :], ACT.Exp, scale=-1.0).then_inc(sig_exp, 1)
                    for g in range(8):
                        act.wait_ge(hT_ps, g + 1)
                        nc.scalar.activation(hT[:, 512 * g:512 * g + 512], ps[g % 2][:, :], ACT.Copy).then_inc(hT_done, 1)
                    for t in range(SUB):
                        act.wait_ge(proj_ps, t + 1)
                        nc.scalar.activation(qs[:, t, :], ps[2 + t % 4][:, 0:128], ACT.Copy).then_inc(q_out, 1)
                        nc.scalar.activation(ks[:, t, :], ps[2 + t % 4][:, 128:256], ACT.Copy).then_inc(k_out, 1)
                        nc.scalar.activation(vs[:, t, :], ps[2 + t % 4][:, 256:384], ACT.Copy).then_inc(v_out, 1)
                    for j in range(4):
                        act.wait_ge(tr_ps, j + 1)
                        dst = (trans_a if j < 2 else trans_b)[:, 4 * (j % 2):4 * (j % 2) + 4, :]
                        nc.scalar.activation(dst, ps[j % 2][:, :].rearrange("p (i s) -> p i s", i=4), ACT.Copy).then_inc(tr_done, 2)

                @block.vector
                def _(dve):
                    step = Steps(dve, seq)
                    dve.wait_ge(loaded, 144)
                    group_stats(nc, dve, step, xr, mean, rstd, (st, mv, var, half, tmp))
                    for g in range(8):
                        wait(dve, hT_ps, g - 1)
                        modulated_group(nc, step, xr, mean, rstd, h[:, g % 2, :, :], mods, g, 0, 0, h_ready)
                    dve.wait_ge(sig_exp, 2)
                    for v, f in ((alpha, -0.5), (beta, 2.0)):
                        step(nc.vector.tensor_scalar(v[:, :], v[:, :], 1.0, None, ALU.add))
                        step(nc.vector.reciprocal(v[:, :], v[:, :]))
                        step(nc.vector.tensor_scalar(v[:, :], v[:, :], f, None, ALU.mult))
                    dve.wait_ge(k_out, SUB)
                    flat = prod[:, :, :, :].rearrange("p a b c -> p (a b c)")
                    kf = ks[:, :, :].rearrange("p t d -> p (t d)")
                    for j in range(2):
                        part = slice(2048 * j, 2048 * j + 2048)
                        step(nc.vector.tensor_tensor(flat, kf[:, part], kf[:, part], ALU.mult))
                        step(nc.vector.tensor_reduce(rk_x[:, 256 * j:256 * j + 256], flat.rearrange("p (g e) -> p g e", e=DH), AX.X, ALU.add))
                    step(nc.vector.tensor_scalar(rk_x[:, :], rk_x[:, :], 1e-24, None, ALU.max))
                    inverse_root(step, nc, rk[:, :], rk_x[:, :], rk_half[:, :], rk_tmp[:, :])
                    kg = kf.rearrange("p (g e) -> p g e", e=DH)
                    rkg = rk[:, :].rearrange("p (g o) -> p g o", o=1).to_broadcast([128, SUB * H, DH])
                    nc.vector.tensor_tensor(kg, kg, rkg, ALU.mult).then_inc(k_normed, 1)
                    dve.wait_ge(k_normed, 1)
                    dve.wait_ge(v_out, SUB)
                    dve.wait_ge(stored, 32)
                    for t in range(0, SUB, 8):
                        v4 = vs[:, t:t + 8, :].rearrange("p t (h e) -> p (t h) e", e=DH)
                        for i in range(8):
                            vi = vs[:, t + i, :].rearrange("p (h e) -> p h e", e=DH)
                            step(nc.vector.tensor_tensor(vi, vi, beta[:, :].rearrange("p (h o) -> p h o", o=1).to_broadcast([128, H, DH]), ALU.mult), settle=(i == 7))
                    step(nc.vector.memset(state[:, :, :, :], 0.0))
                    step(nc.vector.memset(state[:, :, :, :].rearrange("p h r e -> p h (r e)")[:, :, 0:64:9], 1.0))
                    before = step.base + step.n
                    with dve.Fori(0, SUB) as t:
                        step.turn(before, t, 6)
                        k_t = ks[:, ds(t, 1), :].rearrange("p o (h e) -> p (o h) e", e=DH)
                        v_t = vs[:, ds(t, 1), :].rearrange("p o (h e) -> p (o h) e", e=DH)
                        kb = k_t.rearrange("p h (o e) -> p h o e", o=1).to_broadcast([128, H, 16, DH])
                        step(nc.vector.tensor_tensor(prod[:, :, :, :], state[:, :, :, :], kb, ALU.mult))
                        step(nc.vector.tensor_reduce(dots[:, :, :], prod[:, :, :, :], AX.X, ALU.add))
                        step(nc.vector.tensor_tensor(dots[:, :, :], dots[:, :, :], alpha[:, :].rearrange("p (h o) -> p h o", o=1).to_broadcast([128, H, 16]), ALU.mult))
                        step(nc.vector.tensor_tensor(dots[:, :, DH:16], dots[:, :, DH:16], v_t, ALU.add))
                        ub = dots[:, :, :].rearrange("p h (r o) -> p h r o", o=1).to_broadcast([128, H, 16, DH])
                        step(nc.vector.tensor_tensor(prod[:, :, :, :], ub, kb, ALU.mult))
                        step(nc.vector.tensor_tensor(state[:, :, :, :], state[:, :, :, :], prod[:, :, :, :], ALU.add))
                    step.turn(before, SUB, 6)
                    step(nc.vector.tensor_copy(flat_state[:, 0:DH, :].rearrange("p e (h r) -> p h r e", r=DH), state[:, :, 0:DH, :]))
                    step(nc.vector.tensor_copy(flat_state[:, DH:16, :].rearrange("p d (h e) -> p h d e", e=DH), state[:, :, DH:16, :]))
                    dve.sem_inc(state_done, 1)

        with ExitStack() as c3:
            sb = lambda n, shape, dt=F32: c3.enter_context(nc.sbuf_tensor(f"da_{n}", shape, dt))
            ps = [c3.enter_context(nc.psum_tensor(f"da_psb{i}", [128, 512], F32)) for i in range(4)]
            mT = sb("mT", [128, 2, 65, DH])
            a_bd = sb("a_bd", [128, 2, 2, 128])
            m_bd = sb("m_bd", [128, 2, 4, 128])
            tenth = sb("tenth", [128, 16])
            m_init, a_built, m_ps, m_done, wide, wide_ps, mem_done, seq = (sem("c_" + n) for n in ("m_init", "a_built", "m_ps", "m_done", "wide", "wide_ps", "mem_done", "seq"))
            with nc.Block() as block:
                @block.gpsimd
                def _(pool):
                    def emit(s, par):
                        wait(pool, m_ps, 2 * (s - 1))
                        for b in range(2):
                            src = trans_a[:, :, ds(64 * b + s, 1)].rearrange("p e (o n) -> p (n o) e", o=1).to_broadcast([128, 16, DH])
                            nc.gpsimd.tensor_tensor(a_bd[:, par, b, :].rearrange("p (h e) -> p h e", e=DH), src,
                                                    block01[:, :].rearrange("p (h o) -> p h o", o=1).to_broadcast([128, 16, DH]), ALU.mult).then_inc(a_built, 1)
                    pairs(pool, 64, emit)

                @block.tensor
                def _(pe):
                    pe.wait_ge(m_init, 1)

                    def emit(s, par):
                        for b in range(2):
                            pe.wait_ge(a_built, 2 * s + b + 1)
                            wait(pe, m_done, 2 * (s - 1) + b + 1)
                            nc.tensor.matmul(ps[b][:, 0:DH], a_bd[:, par, b, :], mT[:, b, ds(s, 1), :].rearrange("p o d -> p (o d)"),
                                             start=True, stop=True).then_inc(m_ps, 1)
                    pairs(pe, 64, emit)
                    for n in range(16):
                        pe.wait_ge(wide, n + 1)
                        wait(pe, mem_done, n - 1)
                        for i in range(4):
                            last = nc.tensor.transpose(ps[2 + n % 2][:, 128 * i:128 * i + 128], m_bd[:, n % 2, i, :], ident[:, :])
                        last.then_inc(wide_ps, 1)

                @block.scalar
                def _(act):
                    for n in range(16):
                        act.wait_ge(wide_ps, n + 1)
                        nc.scalar.activation(mem[:, 4 * n:4 * n + 4, :], ps[2 + n % 2][:, :].rearrange("p (i c) -> p i c", i=4), ACT.Copy).then_inc(mem_done, 1)

                @block.vector
                def _(dve):
                    step = Steps(dve, seq)
                    step(nc.vector.tensor_scalar(tenth[:, :], block01[:, :], 0.1, None, ALU.mult))
                    nc.vector.memset(mT[:, :, 0:1, :], 0.0).then_inc(m_init, 1)

                    def emit(s, par):
                        for b in range(2):
                            dve.wait_ge(m_ps, 2 * s + b + 1)
                            nc.vector.tensor_tensor(mT[:, b, ds(s + 1, 1), :].rearrange("p o d -> p (o d)"), ps[b][:, 0:DH],
                                                    trans_b[:, :, ds(64 * b + s, 1)].rearrange("p d n -> p (d n)"), ALU.add).then_inc(m_done, 1)
                    pairs(dve, 64, emit)
                    dve.wait_ge(m_done, 128)
                    dve.wait_ge(m_init, 1)
                    for n in range(16):
                        wait(dve, wide_ps, n - 1)
                        for i in range(4):
                            c = 4 * n + i
                            src = mT[:, c // 32, 2 * (c % 32), :]
                            last = nc.vector.tensor_tensor(m_bd[:, n % 2, i, :].rearrange("p (h d) -> p h d", d=DH),
                                                           src.rearrange("p (o d) -> p o d", o=1).to_broadcast([128, 16, DH]),
                                                           tenth[:, :].rearrange("p (h o) -> p h o", o=1).to_broadcast([128, 16, DH]), ALU.mult)
                        last.then_inc(wide, 1)

        with ExitStack() as c4:
            sb = lambda n, shape, dt=F32: c4.enter_context(nc.sbuf_tensor(f"da_{n}", shape, dt))
            pb = lambda n: c4.enter_context(nc.psum_tensor(f"da_{n}", [128, 512], F32))
            q_t, k_t = sb("q_t", [128, 2, 128]), sb("k_t", [128, 2, 128])
            v_t = sb("v_t", [128, 2, 2, 128])
            q_pad, k_pad = sb("q_pad", [128, 2, 16, 32]), sb("k_pad", [128, 2, 16, 32])
            q_T, k_T, q_c = sb("q_T", [128, 512]), sb("k_T", [128, 512]), sb("q_c", [128, 128])
            p = sb("p", [128, 4, 4, 64])
            neg_max, p_sum = sb("neg_max", [128, 4, 4]), sb("p_sum", [128, 4, 4])
            p_T = sb("p_T", [128, 8, 128])
            att, att_T, gated = sb("att", [128, 128]), sb("att_T", [128, 128]), sb("gated", [128, 128])
            w_o = sb("w_o", [128, 128])
            causal = sb("causal", [128, 64], BF16)
            ident_bf = sb("ident_bf", [128, 128], BF16)
            mem_t = sb("mem_t", [128, 2, 2, 128])
            s_ps = [pb(f"s_ps{i}") for i in range(4)]
            t_ps = [pb(f"t_ps{i}") for i in range(2)]
            o_ps = [pb(f"o_ps{i}") for i in range(2)]
            names = ("const", "mem_ready", "padded", "zeroed", "qkT_ps", "qT_done", "kT_done", "s_done", "shifted", "exped", "p_done",
                     "pT_ps", "pTa", "pTb", "o_done", "att_done", "attT_ps", "attT_done", "y_done", "x_done", "seq")
            S = {n: sem("t_" + n) for n in names}
            tile_in = [sem("t_in0"), sem("t_in1")]
            with nc.Block() as block:
                @block.sync
                def _(sp):
                    sp.dma_start(w_o[:, :], w_oT).then_inc(S["const"], 16)
                    sp.dma_start(causal[:, :], tables["causal64"]).then_inc(S["const"], 16)
                    sp.dma_start(ident_bf[:, :], tables["ident_bf"]).then_inc(S["const"], 16)

                    def emit(T, par):
                        wait(sp, S["padded"], 2 * (T - 1))
                        wait(sp, S["qkT_ps"], T - 1)
                        wait(sp, S["o_done"], T - 1)
                        r = T * 128
                        sp.dma_start(q_t[:, par, :], qkv_dram[0][ds(r, 128), :]).then_inc(tile_in[par], 16)
                        sp.dma_start(k_t[:, par, :], qkv_dram[1][ds(r, 128), :]).then_inc(tile_in[par], 16)
                        for half_ in range(2):
                            sp.dma_start(v_t[64 * half_:64 * half_ + 64, par, :, :],
                                         qkv_dram[2][ds(r, 128), :].rearrange("(c k) d -> k c d", c=2)).then_inc(tile_in[par], 16)
                    pairs(sp, 32, emit)

                @block.tensor
                def _(pe):
                    pe.wait_ge(S["const"], 48)
                    pe.wait_ge(S["zeroed"], 2)

                    def emit(T, par):
                        pe.wait_ge(tile_in[par], 64 * (T // 2 + 1))
                        pe.wait_ge(S["padded"], 2 * T + 2)
                        wait(pe, S["pTa"], T)
                        wait(pe, S["pTb"], T)
                        wait(pe, S["attT_done"], T)
                        wait(pe, S["x_done"], T)
                        for src, dst in ((q_pad, t_ps[0]), (k_pad, t_ps[1])):
                            for g in range(4):
                                nc.tensor.transpose(dst[:, 128 * g:128 * g + 128], src[:, par, 4 * g:4 * g + 4, :].rearrange("p h e -> p (h e)"), ident[:, :])
                        wait(pe, S["att_done"], T)
                        nc.tensor.transpose(o_ps[1][:, 0:128], q_t[:, par, :], ident[:, :]).then_inc(S["qkT_ps"], 1)
                        wait(pe, S["exped"], 4 * T)
                        for hh in range(4):
                            nc.tensor.matmul(s_ps[hh][:, 0:256].rearrange("p (g k) -> p g k", g=4), ident_bf[:, :],
                                             causal[:, :].rearrange("p (o k) -> p o k", o=1).to_broadcast([128, 4, 64]), start=True, stop=False)
                        pe.wait_ge(S["qT_done"], 2 * T + 2)
                        pe.wait_ge(S["kT_done"], T + 1)
                        for g in range(4):
                            for hh in range(4):
                                for c in range(2):
                                    rows, cols = slice(32 * hh, 32 * hh + 32), slice(128 * g + 64 * c, 128 * g + 64 * c + 64)
                                    last = nc.tensor.matmul(s_ps[hh][64 * c:64 * c + 64, 64 * g:64 * g + 64], q_T[rows, cols], k_T[rows, cols], start=False, stop=(g == 3))
                        last.then_inc(S["s_done"], 1)
                        pe.wait_ge(S["mem_ready"], T + 1)
                        for c in range(2):
                            nc.tensor.matmul(o_ps[0][64 * c:64 * c + 64, 0:128], q_c[:, 64 * c:64 * c + 64], mem_t[:, par, c, :], start=True, stop=False)
                        for hh in range(4):
                            pe.wait_ge(S["p_done"], 4 * T + hh + 1)
                            for j in range(2):
                                n = 2 * hh + j
                                last = nc.tensor.transpose(t_ps[n // 4][:, 128 * (n % 4):128 * (n % 4) + 128],
                                                           p[:, hh, 2 * j:2 * j + 2, :].rearrange("p g k -> p (g k)"), ident[:, :])
                            if hh % 2:
                                last.then_inc(S["pT_ps"], 1)
                        pe.wait_ge(S["pTb"], 1)
                        pe.wait_ge(S["pTa"], T + 1)
                        pe.wait_ge(S["pTb"], T + 1)
                        for n in range(8):
                            for gp in range(2):
                                g = 2 * (n % 2) + gp
                                head = 4 * g + n // 2
                                for c in range(2):
                                    rows = slice(64 * gp, 64 * gp + 64)
                                    last = nc.tensor.matmul(o_ps[gp][64 * c:64 * c + 64, DH * head:DH * head + DH], p_T[rows, n, 64 * c:64 * c + 64],
                                                            v_t[rows, par, c, DH * head:DH * head + DH], start=(gp == 1), stop=(gp == 1 or n == 7))
                        last.then_inc(S["o_done"], 1)
                        pe.wait_ge(S["att_done"], T + 1)
                        nc.tensor.transpose(t_ps[0][:, 0:128], att[:, :], ident[:, :]).then_inc(S["attT_ps"], 1)
                        pe.wait_ge(S["attT_done"], T + 1)
                        nc.tensor.matmul(t_ps[1][:, 0:128], att_T[:, :], w_o[:, :], start=True, stop=True).then_inc(S["y_done"], 1)
                    pairs(pe, 32, emit)

                @block.gpsimd
                def _(pool):
                    def emit(T, par):
                        wait(pool, S["o_done"], T - 1)
                        nc.gpsimd.tensor_copy(mem_t[:, par, :, :], mem[:, ds(2 * T, 2), :]).then_inc(S["mem_ready"], 1)
                    pairs(pool, 32, emit)

                @block.scalar
                def _(act):
                    act.wait_ge(S["zeroed"], 2)

                    def emit(T, par):
                        act.wait_ge(tile_in[par], 64 * (T // 2 + 1))
                        wait(act, S["qkT_ps"], T - 1)
                        nc.scalar.activation(q_pad[:, par, :, 0:DH], q_t[:, par, :].rearrange("p (h e) -> p h e", e=DH), ACT.Copy, scale=float(DH) ** -0.5).then_inc(S["padded"], 1)
                        nc.scalar.activation(k_pad[:, par, :, 0:DH], k_t[:, par, :].rearrange("p (h e) -> p h e", e=DH), ACT.Copy).then_inc(S["padded"], 1)
                        act.wait_ge(S["qkT_ps"], T + 1)
                        wait(act, S["s_done"], T)
                        wait(act, S["o_done"], T)
                        nc.scalar.activation(q_T[:, :], t_ps[0][:, :], ACT.Copy).then_inc(S["qT_done"], 1)
                        nc.scalar.activation(q_c[:, :], o_ps[1][:, 0:128], ACT.Copy).then_inc(S["qT_done"], 1)
                        for hh in range(4):
                            act.wait_ge(S["shifted"], 4 * T + hh + 1)
                            nc.scalar.activation(p[:, hh, :, :], p[:, hh, :, :], ACT.Exp).then_inc(S["exped"], 1)
                        act.wait_ge(S["pT_ps"], 2 * T + 1)
                        wait(act, S["o_done"], T)
                        nc.scalar.activation(p_T[:, 0:4, :], t_ps[0][:, :].rearrange("p (n q) -> p n q", n=4), ACT.Copy).then_inc(S["pTa"], 1)
                        act.wait_ge(S["attT_ps"], T + 1)
                        nc.scalar.activation(att_T[:, :], t_ps[0][:, 0:128], ACT.Copy).then_inc(S["attT_done"], 1)
                    pairs(act, 32, emit)

                @block.vector
                def _(dve):
                    step = Steps(dve, S["seq"])
                    nc.vector.memset(q_pad[:, :, :, :], 0.0).then_inc(S["zeroed"], 1)
                    nc.vector.memset(k_pad[:, :, :, :], 0.0).then_inc(S["zeroed"], 1)
                    PER = 4 * 3 + 2

                    def emit(T, par):
                        step.turn(0, T, PER)
                        dve.wait_ge(S["qkT_ps"], T + 1)
                        wait(dve, S["s_done"], T)
                        nc.vector.tensor_copy(k_T[:, :], t_ps[1][:, :]).then_inc(S["kT_done"], 1)
                        dve.wait_ge(S["s_done"], T + 1)
                        wait(dve, S["pT_ps"], 2 * T)
                        for hh in range(4):
                            sc = s_ps[hh][:, 0:256].rearrange("p (g k) -> p g k", g=4)
                            step(nc.vector.tensor_reduce(neg_max[:, hh, :], sc, AX.X, ALU.max, negate=True))
                            nc.vector.tensor_tensor(p[:, hh, :, :], sc, neg_max[:, hh, :].rearrange("p (g o) -> p g o", o=1).to_broadcast([128, 4, 64]), ALU.add).then_inc(S["shifted"], 1)
                        for hh in range(4):
                            dve.wait_ge(S["exped"], 4 * T + hh + 1)
                            step(nc.vector.tensor_reduce(p_sum[:, hh, :], p[:, hh, :, :], AX.X, ALU.add))
                            step(nc.vector.reciprocal(p_sum[:, hh, :], p_sum[:, hh, :]))
                            nc.vector.tensor_tensor(p[:, hh, :, :], p[:, hh, :, :], p_sum[:, hh, :].rearrange("p (g o) -> p g o", o=1).to_broadcast([128, 4, 64]), ALU.mult).then_inc(S["p_done"], 1)
                        dve.wait_ge(S["pT_ps"], 2 * T + 2)
                        nc.vector.tensor_copy(p_T[:, 4:8, :], t_ps[1][:, :].rearrange("p (n q) -> p n q", n=4)).then_inc(S["pTb"], 1)
                        dve.wait_ge(S["o_done"], T + 1)
                        wait(dve, S["attT_ps"], T)
                        step(nc.vector.tensor_copy(att[:, :], o_ps[0][:, 0:128]))
                        odd = att[:, :].rearrange("p (a x) -> p a x", a=2)[:, :, 32:64]
                        nc.vector.tensor_tensor(odd, odd, o_ps[1][:, 0:128].rearrange("p (a x) -> p a x", a=2)[:, :, 32:64], ALU.add).then_inc(S["att_done"], 1)
                        dve.wait_ge(S["y_done"], T + 1)
                        gate = mods[:, ds(T // 16, 1), 2, :].rearrange("p o d -> p (o d)")
                        step(nc.vector.tensor_tensor(gated[:, :], t_ps[1][:, 0:128], gate, ALU.mult))
                        x_t = xr[:, ds(T, 1), :].rearrange("p o d -> p (o d)")
                        nc.vector.tensor_tensor(x_t, x_t, gated[:, :], ALU.add).then_inc(S["x_done"], 1)
                    pairs(dve, 32, emit)


def feed_stage(nc, name, xr, mods, layer, z, x_rows):
    with ExitStack() as ctx:
        sb = lambda n, shape, dt=F32: ctx.enter_context(nc.sbuf_tensor(f"{name}_{n}", shape, dt))
        sem = ctx.enter_context(stage_semaphores(nc, name))
        st, mv = sb("st", [128, 4, 6]), sb("mv", [128, 4, 2])
        mean, var, rstd, half, tmp = (sb(n, [128, 32]) for n in ("mean", "var", "rstd", "half", "tmp"))
        seq, h_ready = sem("seq"), sem("h_ready")
        stored = [sem("stored0"), sem("stored1")]
        with nc.Block() as block:
            @block.vector
            def _(dve):
                step = Steps(dve, seq)
                group_stats(nc, dve, step, xr, mean, rstd, (st, mv, var, half, tmp))
                for g in range(8):
                    modulated_group(nc, step, xr, mean, rstd, z[:, 4 * g:4 * g + 4, :], mods, g, layer, 1, h_ready)

            @block.sync
            def _(sp):
                for g in range(8):
                    sp.wait_ge(h_ready, g + 1)
                    r = 512 * g + g // 4 + 1
                    sp.dma_start(x_rows[r:r + 512, :].rearrange("(t p) d -> p t d", p=128), z[:, 4 * g:4 * g + 4, :]).then_inc(stored[g % 2], 16)
                for j in range(2):
                    sp.wait_ge(stored[j], 64)


def residual_stage(nc, name, xr, mods, k0, z, out=None):
    with ExitStack() as ctx:
        sem = ctx.enter_context(stage_semaphores(nc, name))
        scaled, added, stored = sem("scaled"), sem("added"), sem("stored")
        with nc.Block() as block:
            @block.sync
            def _(sp):
                if out is not None:
                    for g in range(8):
                        sp.wait_ge(added, g + 1)
                        t = 4 * (g % 4)
                        sp.dma_start(out[g // 4].rearrange("(t p) d -> p t d", p=128)[:, t:t + 4, :], xr[:, 4 * g:4 * g + 4, :]).then_inc(stored, 16)
                    sp.wait_ge(stored, 128)

            @block.vector
            def _(dve):
                for g in range(8):
                    k = k0 + g // 4
                    z4 = z[:, 4 * g:4 * g + 4, :]
                    nc.vector.tensor_tensor(z4, z4, mods[:, k:k + 1, 5, :].to_broadcast([128, 4, 128]), ALU.mult).then_inc(scaled, 1)
                for g in range(8):
                    dve.wait_ge(scaled, g + 1)
                    x4 = xr[:, 4 * g:4 * g + 4, :]
                    nc.vector.tensor_tensor(x4, x4, z[:, 4 * g:4 * g + 4, :], ALU.add).then_inc(added, 1)


def linear_attention_stage(nc, xr, mods, W, tables):
    F, N_CONST = 64, 21
    with ExitStack() as ctx:
        sb = lambda n, shape, dt=F32: ctx.enter_context(nc.sbuf_tensor(f"la_{n}", shape, dt))
        pb = lambda n: ctx.enter_context(nc.psum_tensor(f"la_{n}", [128, 512], F32))
        sem = ctx.enter_context(stage_semaphores(nc, "la"))
        st, mv = sb("st", [128, 4, 6]), sb("mv", [128, 4, 2])
        mean, var, rstd, half, tmp = (sb(n, [128, 32]) for n in ("mean", "var", "rstd", "half", "tmp"))
        mean2, rstd2 = sb("mean2", [128, 32]), sb("rstd2", [128, 32])
        h = sb("h", [128, 32, 128])
        xn = sb("xn", [128, 2, 128])
        xnT = sb("xnT", [128, 2, 128])
        qT, kT = sb("qT", [64, 2, 128]), sb("kT", [64, 2, 128])
        low = sb("low", [64, 2, 128])
        high = sb("high", [64, 2, 128])
        k_tok = sb("k_tok", [128, 2, 64])
        v1 = sb("v1", [128, 2, 129])
        sT = sb("sT", [128, 128])
        kv = sb("kv", [64, 129])
        rden = sb("rden", [128, 1])
        att, attT = sb("att", [128, 128]), sb("attT", [128, 128])
        x_mid = sb("x_mid", [128, 2, 128])
        s6, m2, v_eps, hf, tp_, r2 = sb("s6", [128, 6]), sb("m2", [128, 2]), sb("v_eps", [128, 1]), sb("hf", [128, 1]), sb("tp", [128, 1]), sb("r2", [128, 1])
        y_n, y_T = sb("y_n", [128, 128]), sb("y_T", [128, 128])
        g_T = sb("g_T", [128, 4, 128])
        res = sb("res", [128, 128])
        w_qk, w_v, w_o, w_f1, w_f2 = sb("w_qk", [128, 128]), sb("w_v", [128, 128]), sb("w_o", [128, 128]), sb("w_f1", [128, 512]), sb("w_f2", [128, 4, 128])
        b_qk = sb("b_qk", [64, 2])
        b_v, b_o, b_f2 = sb("b_v", [128, 128]), sb("b_o", [128, 128]), sb("b_f2", [128, 128])
        b_f1 = sb("b_f1", [128, 4])
        ln = sb("ln", [128, 4])
        ident, keep_mask = sb("ident", [128, 128]), sb("keep_mask", [128, 128])
        p_t, p_q, p_k, p_v, p_s, p_n, p_kv, p_f = (pb(n) for n in ("p_t", "p_q", "p_k", "p_v", "p_s", "p_n", "p_kv", "p_f"))
        names = ("const", "seq", "h_ready", "xn_done", "xT_ps", "xT_done", "qk_ps", "v_ps", "low_done", "exped", "feat", "ktok_ps", "ktok_done", "v_done",
                 "s_ps", "s_done", "n_ps", "kv_ps", "kv_done", "att_done", "attT_ps", "attT_done", "o_ps", "yn_done", "yT_ps", "yT_done",
                 "f1_ps", "gelu", "f2_ps", "x_done")
        S = {n: sem(n) for n in names}
        with nc.Block() as block:
            @block.sync
            def _(sp):
                loads = [(ident[:, :], tables["ident"]), (keep_mask[:, :], tables["keep"]), (w_qk[:, 0:F], W["q_wT"]), (w_qk[:, F:2 * F], W["k_wT"]),
                         (w_v[:, :], W["v_wT"]), (w_o[:, :], W["o_wT"]), (w_f1[:, :], W["f1_wT"]), (w_f2[:, :, :], W["f2_wT"].rearrange("(c p) n -> p c n", p=128))]
                col = lambda a: a.rearrange("(p o) -> p o", o=1)
                loads += [(b_qk[:, 0:1], col(W["q_b"])), (b_qk[:, 1:2], col(W["k_b"]))]
                loads += [(b_f1[:, c:c + 1], col(W["f1_b"][128 * c:128 * c + 128])) for c in range(4)]
                loads += [(ln[:, i:i + 1], col(W[n])) for i, n in enumerate(("ln1_w", "ln1_b", "ln2_w", "ln2_b"))]
                loads += [(dst, W[n].rearrange("(o n) -> o n", o=1).partition_broadcast(128)) for dst, n in ((b_v[:, :], "v_b"), (b_o[:, :], "o_b"), (b_f2[:, :], "f2_b"))]
                assert len(loads) == N_CONST
                for dst, src in loads:
                    sp.dma_start(dst, src).then_inc(S["const"], 16)

            @block.tensor
            def _(pe):
                pe.wait_ge(S["const"], 16 * N_CONST)

                def emit(T, par):
                    n = T + 1
                    pe.wait_ge(S["xn_done"], n)
                    wait(pe, S["attT_done"], T)
                    wait(pe, S["yT_done"], T)
                    nc.tensor.transpose(p_t[:, 0:128], xn[:, par, :], ident[:, :]).then_inc(S["xT_ps"], 1)
                    pe.wait_ge(S["xT_done"], n)
                    wait(pe, S["feat"], 2 * T)
                    nc.tensor.matmul(p_q[0:F, 0:128], w_qk[:, 0:F], xnT[:, par, :], start=True, stop=True)
                    nc.tensor.matmul(p_k[0:F, 0:128], w_qk[:, F:2 * F], xnT[:, par, :], start=True, stop=True).then_inc(S["qk_ps"], 1)
                    wait(pe, S["v_done"], T)
                    nc.tensor.matmul(p_v[:, 0:128], xnT[:, par, :], w_v[:, :], start=True, stop=True).then_inc(S["v_ps"], 1)
                    pe.wait_ge(S["feat"], 2 * n)
                    wait(pe, S["s_done"], T)
                    nc.tensor.matmul(p_s[:, 0:128], kT[:, par, :], qT[:, par, :], start=True, stop=True).then_inc(S["s_ps"], 1)
                    nc.tensor.transpose(p_t[:, 0:F], kT[:, par, :], ident[0:F, 0:F]).then_inc(S["ktok_ps"], 1)
                    pe.wait_ge(S["s_done"], n)
                    pe.wait_ge(S["v_done"], n)
                    wait(pe, S["x_done"], T)
                    nc.tensor.matmul(p_n[:, 0:129], sT[:, :], v1[:, par, :], start=True, stop=False)
                    wait(pe, S["kv_done"], n)
                    nc.tensor.matmul(p_n[:, 0:129], qT[:, par, :], kv[:, :], start=False, stop=True).then_inc(S["n_ps"], 1)
                    pe.wait_ge(S["ktok_done"], n)
                    nc.tensor.matmul(p_kv[0:F, 0:129], k_tok[:, par, :], v1[:, par, :], start=True, stop=True).then_inc(S["kv_ps"], 1)
                    pe.wait_ge(S["att_done"], n)
                    nc.tensor.transpose(p_t[:, 0:128], att[:, :], ident[:, :]).then_inc(S["attT_ps"], 1)
                    pe.wait_ge(S["attT_done"], n)
                    nc.tensor.matmul(p_n[:, 0:128], attT[:, :], w_o[:, :], start=True, stop=True).then_inc(S["o_ps"], 1)
                    pe.wait_ge(S["yn_done"], n)
                    nc.tensor.transpose(p_t[:, 0:128], y_n[:, :], ident[:, :]).then_inc(S["yT_ps"], 1)
                    pe.wait_ge(S["yT_done"], n)
                    for c in range(4):
                        last = nc.tensor.matmul(p_f[:, 128 * c:128 * c + 128], w_f1[:, 128 * c:128 * c + 128], y_T[:, :], start=True, stop=True)
                    last.then_inc(S["f1_ps"], 1)
                    pe.wait_ge(S["gelu"], n)
                    for c in range(4):
                        last = nc.tensor.matmul(p_n[:, 0:128], g_T[:, c, :], w_f2[:, c, :], start=(c == 0), stop=(c == 3))
                    last.then_inc(S["f2_ps"], 1)
                pairs(pe, 32, emit)

            @block.scalar
            def _(act):
                act.wait_ge(S["const"], 16 * N_CONST)

                def emit(T, par):
                    n = T + 1
                    act.wait_ge(S["xT_ps"], n)
                    nc.scalar.activation(xnT[:, par, :], p_t[:, 0:128], ACT.Identity, bias=ln[:, 1:2], scale=ln[:, 0:1]).then_inc(S["xT_done"], 1)
                    act.wait_ge(S["low_done"], n)
                    nc.scalar.activation(low[:, :, :], low[:, :, :], ACT.Exp).then_inc(S["exped"], 1)
                    act.wait_ge(S["ktok_ps"], n)
                    nc.scalar.activation(k_tok[:, par, :], p_t[:, 0:F], ACT.Copy).then_inc(S["ktok_done"], 1)
                    act.wait_ge(S["attT_ps"], n)
                    nc.scalar.activation(attT[:, :], p_t[:, 0:128], ACT.Copy).then_inc(S["attT_done"], 1)
                    act.wait_ge(S["yT_ps"], n)
                    nc.scalar.activation(y_T[:, :], p_t[:, 0:128], ACT.Identity, bias=ln[:, 3:4], scale=ln[:, 2:3]).then_inc(S["yT_done"], 1)
                    act.wait_ge(S["f1_ps"], n)
                    for c in range(4):
                        last = nc.scalar.activation(g_T[:, c, :], p_f[:, 128 * c:128 * c + 128], ACT.Gelu, bias=b_f1[:, c:c + 1], scale=1.0)
                    last.then_inc(S["gelu"], 1)
                pairs(act, 32, emit)

            @block.vector
            def _(dve):
                step = Steps(dve, S["seq"])
                dve.wait_ge(S["const"], 16 * N_CONST)
                group_stats(nc, dve, step, xr, mean, rstd, (st, mv, var, half, tmp))
                for g in range(8):
                    modulated_group(nc, step, xr, mean, rstd, h[:, 4 * g:4 * g + 4, :], mods, g, 1, 0, S["h_ready"])
                dve.wait_ge(S["h_ready"], 8)
                group_stats(nc, dve, step, h, mean2, rstd2, (st, mv, var, half, tmp))
                step(nc.vector.memset(v1[:, :, :], 1.0))
                before = step.base + step.n
                nc.vector.memset(kv[:, :], 0.0).then_inc(S["kv_done"], 1)
                PER = 25

                def emit(T, par, batch_ends=False):
                    n = T + 1
                    step.turn(before, T, PER)
                    one = lambda a: a[:, ds(T, 1)]
                    h_t = h[:, ds(T, 1), :].rearrange("p o d -> p (o d)")
                    wait(dve, S["xT_ps"], T - 1)
                    nc.vector.tensor_scalar(xn[:, par, :], h_t, one(mean2), one(rstd2), ALU.subtract, ALU.mult).then_inc(S["xn_done"], 1)
                    dve.wait_ge(S["qk_ps"], n)
                    wait(dve, S["feat"], 2 * T)
                    for j, src in enumerate((p_q, p_k)):
                        step(nc.vector.tensor_scalar(high[:, j, :], src[0:F, 0:128], b_qk[:, j:j + 1], 0.0, ALU.add, ALU.max), settle=False)
                        last = nc.vector.tensor_scalar(low[:, j, :], src[0:F, 0:128], b_qk[:, j:j + 1], 0.0, ALU.add, ALU.min)
                        if j:
                            last.then_inc(S["low_done"], 1)
                    dve.wait_ge(S["v_ps"], n)
                    nc.vector.tensor_tensor(v1[:, par, 0:128], p_v[:, 0:128], b_v[:, :], ALU.add).then_inc(S["v_done"], 1)
                    dve.wait_ge(S["exped"], n)
                    step.settle()
                    for j, dst in enumerate((qT, kT)):
                        nc.vector.tensor_tensor(dst[:, par, :], high[:, j, :], low[:, j, :], ALU.add).then_inc(S["feat"], 1)
                    dve.wait_ge(S["s_ps"], n)
                    wait(dve, S["n_ps"], T)
                    nc.vector.tensor_tensor(sT[:, :], p_s[:, 0:128], keep_mask[:, :], ALU.mult).then_inc(S["s_done"], 1)
                    dve.wait_ge(S["n_ps"], n)
                    wait(dve, S["attT_ps"], T)
                    step(nc.vector.tensor_scalar(rden[:, :], p_n[:, 128:129], 1e-6, None, ALU.add))
                    step(nc.vector.reciprocal(rden[:, :], rden[:, :]))
                    nc.vector.tensor_scalar(att[:, :], p_n[:, 0:128], rden[:, 0:1], None, ALU.mult).then_inc(S["att_done"], 1)
                    dve.wait_ge(S["kv_ps"], n)
                    dve.wait_ge(S["kv_done"], n)
                    if batch_ends:
                        nc.vector.memset(kv[:, :], 0.0).then_inc(S["kv_done"], 1)
                    else:
                        nc.vector.tensor_tensor(kv[:, :], kv[:, :], p_kv[0:F, 0:129], ALU.add).then_inc(S["kv_done"], 1)
                    dve.wait_ge(S["o_ps"], n)
                    step(nc.vector.tensor_tensor(x_mid[:, par, :], p_n[:, 0:128], h_t, ALU.add))
                    step(nc.vector.tensor_tensor(x_mid[:, par, :], x_mid[:, par, :], b_o[:, :], ALU.add))
                    step(nc.vector.bn_stats(s6[:, :], x_mid[:, par, :]))
                    step(nc.vector.memset(v_eps[:, :], LN_EPS), settle=False)
                    step(nc.vector.bn_aggr(m2[:, :], s6[:, :]))
                    step(nc.vector.tensor_tensor(v_eps[:, :], m2[:, 1:2], v_eps[:, :], ALU.add))
                    inverse_root(step, nc, r2[:, :], v_eps[:, :], hf[:, :], tp_[:, :])
                    nc.vector.tensor_scalar(y_n[:, :], x_mid[:, par, :], m2[:, 0:1], r2[:, 0:1], ALU.subtract, ALU.mult).then_inc(S["yn_done"], 1)
                    dve.wait_ge(S["f2_ps"], n)
                    step(nc.vector.tensor_tensor(res[:, :], p_n[:, 0:128], x_mid[:, par, :], ALU.add))
                    dve.sem_inc(S["x_done"], 1)
                    step(nc.vector.tensor_tensor(res[:, :], res[:, :], b_f2[:, :], ALU.add))
                    step(nc.vector.tensor_tensor(res[:, :], res[:, :], mods[:, ds(T // 16 + 2, 1), 2, :].rearrange("p o d -> p (o d)"), ALU.mult))
                    x_t = xr[:, ds(T, 1), :].rearrange("p o d -> p (o d)")
                    step(nc.vector.tensor_tensor(x_t, x_t, res[:, :], ALU.add))
                    assert step.n == PER, step.n
                emit(0, 0)
                emit(1, 1)
                with dve.Fori(1, 7) as p:
                    emit(p * 2, 0)
                    emit(p * 2 + 1, 1)
                emit(14, 0)
                emit(15, 1, batch_ends=True)
                with dve.Fori(8, 16) as p:
                    emit(p * 2, 0)
                    emit(p * 2 + 1, 1)


def local_block_stage(nc, name, depth, heads, window, x, x_rows, mid_rows, weights, tables):
    U = heads // 2
    W = window
    KW = 128 + W
    NT = TILES
    TPB = NT // 2
    HID = 341
    CH = [(0, 128), (128, 128), (256, HID - 256)]
    AT_SCORE, AT_MAX, AT_EXP, AT_NORM, AT_PT, AT_PV, AT_OUT = 1, 1, 2, 3, 4, 5, 6
    LAG_OUT = (U - 1 + AT_OUT) // U
    NEWTONS = 3
    CHAIN = 3 + 3 * NEWTONS
    if U == 8:
        project = [(1, s + 4) if s < 4 else (2, s - 4) for s in range(8)]
        take_up = [(1, s + 3) if s < 5 else (2, s - 5) for s in range(8)]
        normalise = [[(0, s + 2)] if s < 6 else [(1, 0), (1, 1)] if s == 7 else [] for s in range(8)]
        link_spots = [(4, 4), (4, 4)] + [(s, spot) for s in (5, 6) for spot in range(5)]
        AHEAD, XT_STEP, ROT_STEP = 2, 3, 2
    else:
        project = [(2, s + 1) if s < 3 else (3, 0) for s in range(4)]
        take_up = [(2, s) for s in range(4)]
        normalise = [[(0, 2)], [(0, 3)], [], [(1, 0), (1, 1)]]
        link_spots = [(s, spot) for s in range(3) for spot in range(4)]
        AHEAD, XT_STEP, ROT_STEP = 3, 2, 2
    R = {8: 2, 4: 4}[U]
    links_at = lambda s, spot: [k for k in range(CHAIN) if link_spots[k] == (s, spot)]
    first_full = {2: 2, 4: 4}[R]
    last_full = NT - 2 if R == 2 else NT - 4

    with ExitStack() as ctx:
        sb = lambda n, shape, dt=F32: ctx.enter_context(nc.sbuf_tensor(f"{name}_{n}", shape, dt))
        pb = lambda n, shape=(128, 512), dt=F32: ctx.enter_context(nc.psum_tensor(f"{name}_{n}", list(shape), dt))
        once = ctx.enter_context(stage_semaphores(nc, name + "_once"))
        sem = ctx.enter_context(stage_semaphores(nc, name))
        taken = []

        def layer_sem(n):
            taken.append(sem(n))
            return taken[-1]

        w_qkv = sb("w_qkv", [128, U, 3, 128])
        w_out = sb("w_out", [128, U, 128])
        w_up = sb("w_up", [128, 2 * HID])
        w_down = sb("w_down", [128, 3, 128])
        b_up = sb("b_up", [128, 2, 3])
        ln_gb = sb("ln_gb", [128, 2])
        qk_scales = sb("qk_scales", [128, 4, 64])
        rot_base = sb("rot_base", [128, TPB, 256])
        rot = sb("rot", [128, 2, 4, 64])
        frame = sb("frame", [128, 1])
        masks = sb("masks", [128, TPB, KW], BF16)
        ident = sb("ident", [128, 128])
        ident_bf = sb("ident_bf", [128, 128], BF16)
        x_in = sb("x_in", [128, 2, 128])
        xT = sb("xT", [128, 2, 128])
        squares = sb("squares", [128, 2, 256])
        sumsq = sb("sumsq", [128, 4 * U])
        cos_part = sb("cos_part", [128, 2, 256])
        sin_part = sb("sin_part", [128, 2, 256])
        qk = sb("qk", [128, 2, U, 256])
        val = sb("val", [128, R, U, 128])
        qkT = sb("qkT", [128, 2, 256])
        k_prev = sb("k_prev", [128, 2, U, W])
        v_prev = sb("v_prev", [128, R, U, 128])
        probs = sb("probs", [128, 4, 2, KW])
        neg_max = sb("neg_max", [128, 4, 2])
        p_sum = sb("p_sum", [128, 4, 2])
        p_rec = sb("p_rec", [128, 2])
        probsT = sb("probsT", [128, 2, 256 + 2 * W])
        outT = sb("outT", [128, 2, 128])
        nw_x = sb("nw_x", [128, 4 * U])
        nw_h = sb("nw_h", [128, 4 * U])
        nw_a = sb("nw_a", [128, 4 * U])
        rnorm = sb("rnorm", [128, 2, 4 * U])
        f_in = sb("f_in", [128, 2, 4, 128])
        f_norm = sb("f_norm", [128, 4, 128])
        f_normT = sb("f_normT", [128, 512])
        gate = sb("gate", [128, 3, 512])
        hidden = sb("hidden", [128, 2, 3, 512])
        stats = sb("stats", [128, 4, 6])
        mean_var = sb("mean_var", [128, 4, 2])
        f_var, f_half, f_tmp, f_rstd = (sb(n, [128, 4]) for n in ("f_var", "f_half", "f_tmp", "f_rstd"))

        ps_q = [pb("ps_q0"), pb("ps_q1")]
        ps_s = [pb("ps_s0"), pb("ps_s1")]
        ps_t, ps_pt, ps_o, ps_y = pb("ps_t"), pb("ps_pt"), pb("ps_o"), pb("ps_y")
        ps_gate, ps_fact = [ps_q[0], ps_q[1], ps_s[0]], [ps_s[1], ps_pt, ps_o]

        consts_in = once("consts_in")
        zeroed = once("zeroed")

        S = {n: layer_sem(n) for n in (
            "rep_in", "wq_in", "wo_in", "wf_in", "xin_in0", "xin_in1", "fin_in0", "fin_in1", "mid_stored", "new_stored0", "new_stored1",
            "xT_ps", "proj_ps", "qkT_ps", "score_half", "score_ps", "pT_ps", "pv_ps", "wo_used", "fT_ps", "gate_ps", "up_ps", "down_ps",
            "sq_done", "val_done", "xT_done", "qkT_done", "exp_done", "pT_done", "outT_done", "fT_done", "gelu_done",
            "ss_done", "rotated", "max_done", "rec_done", "probs_done", "kprev_done", "vprev_done", "chain", "mid_done",
            "ln_steps", "fnorm_done", "hidden_done", "new_done",
            "rot_done", "added", "normed")}
        xin_in = [S["xin_in0"], S["xin_in1"]]
        fin_in = [S["fin_in0"], S["fin_in1"]]
        new_stored = [S["new_stored0"], S["new_stored1"]]

        def unit(T, s, lag):
            d, u = divmod(s - lag, U)
            return T + d, d, u

        def nth(T, u, per=U):
            return T * per + (u + 1)

        def loads(T):
            return T // 2 + 1

        def live(T):
            return not isinstance(T, int) or 0 <= T < NT

        def bodies(eng, emit):
            for T in range(-AHEAD, first_full):
                emit(T, T % R)
            with eng.Fori(0, (last_full - first_full) // R) as p:
                for r in range(R):
                    emit(p * R + (first_full + r), r)
            for T in range(last_full, NT + LAG_OUT):
                emit(T, T % R)

        NG = NT // 4

        def groups(eng, emit):
            emit(0, 0)
            emit(1, 1)
            with eng.Fori(1, NG // 2 - 1) as p:
                emit(p * 2, 0)
                emit(p * 2 + 1, 1)
            emit(NG - 2, 0)
            emit(NG - 1, 1)

        exists = lambda g: not isinstance(g, int) or 0 <= g < NG

        with nc.Block() as block:
            @block.sync
            def _(sp):
                sp.dma_start(ident[:, :], tables["ident"]).then_inc(consts_in, 16)
                sp.dma_start(ident_bf[:, :], tables["ident_bf"]).then_inc(consts_in, 16)
                sp.dma_start(masks[:, :, :], tables[f"masks{W}"].rearrange("t p k -> p t k")).then_inc(consts_in, 16)
                sp.dma_start(rot_base[:, :, :], tables[f"rot{W}"].rearrange("(t p) d -> p t d", p=128)).then_inc(consts_in, 16)
                sp.dma_start(frame[:, :], tables[f"frame{W}"]).then_inc(consts_in, 16)
                sp.wait_ge(consts_in, 80)

            @block.vector
            def _(dve):
                nc.vector.memset(hidden[:, :, :, :], 1.0).then_inc(zeroed, 1)
                nc.vector.memset(k_prev[:, 1, :, :], 0.0).then_inc(zeroed, 1)
                nc.vector.memset(v_prev[:, R - 1, :, :], 0.0).then_inc(zeroed, 1)
                dve.wait_ge(zeroed, 3)

        loop = ExitStack()
        layer = loop.enter_context(nc.Fori(0, depth))
        with nc.Block() as block:

            @block.sync
            def _(sp):
                l, W_ = layer, weights

                def load_input(T, par):
                    r = T * 128 + T // TPB
                    sp.dma_start(x_in[:, par, 0:64], x_rows[ds(r + 1, 128), 0:64]).then_inc(xin_in[par], 16)
                    sp.dma_start(x_in[:, par, 64:128], x_rows[ds(r, 128), 64:128]).then_inc(xin_in[par], 16)

                load_input(0, 0)
                for u in range(U):
                    for j in range(3):
                        sp.dma_start(w_qkv[:, u, j, :], W_["qkv"][l, :, (j * U + u) * 128:(j * U + u + 1) * 128]).then_inc(S["wq_in"], 16)
                    if u == 0:
                        for j, nm in enumerate(("q_scale", "k_scale")):
                            src = W_[nm]
                            sp.dma_start(qk_scales[:, 2 * j, :], src[ds(l, 1), :].partition_broadcast(128)).then_inc(S["rep_in"], 16)
                            sp.dma_start(qk_scales[:, 2 * j + 1, 0:32], src[ds(l, 1), 32:64].partition_broadcast(128)).then_inc(S["rep_in"], 16)
                            sp.dma_start(qk_scales[:, 2 * j + 1, 32:64], src[ds(l, 1), 0:32].partition_broadcast(128)).then_inc(S["rep_in"], 16)
                load_input(1, 1)
                for u in range(U):
                    sp.dma_start(w_out[:, u, :], W_["out"][l, u * 128:(u + 1) * 128, :]).then_inc(S["wo_in"], 16)
                sp.dma_start(w_up[:, :], W_["w1"][l, :, :]).then_inc(S["wf_in"], 16)
                for c, (c0, cn) in enumerate(CH):
                    sp.dma_start(w_down[0:cn, c, :], W_["w2"][l, c0:c0 + cn, :]).then_inc(S["wf_in"], 16)
                    for j in range(2):
                        sp.dma_start(b_up[0:cn, j, c:c + 1], W_["b1"][l, j * HID + c0:j * HID + c0 + cn].rearrange("(p o) -> p o", o=1)).then_inc(S["wf_in"], 16)
                sp.dma_start(w_down[HID - 256:HID - 255, 2, :], W_["b2"][ds(l, 1), :]).then_inc(S["wf_in"], 16)
                sp.dma_start(ln_gb[:, 0:1], W_["ln_g"][l, :].rearrange("(p o) -> p o", o=1)).then_inc(S["wf_in"], 16)
                sp.dma_start(ln_gb[:, 1:2], W_["ln_b"][l, :].rearrange("(p o) -> p o", o=1)).then_inc(S["wf_in"], 16)

                def load_group(g, par):
                    r = g * 512 + g // (NG // 2)
                    rows = lambda at, half: mid_rows[ds(at, 512), half].rearrange("(t p) d -> p t d", p=128)
                    sp.dma_start(f_in[:, par, :, 0:64], rows(r + 1, slice(0, 64))).then_inc(fin_in[par], 16)
                    sp.dma_start(f_in[:, par, :, 64:128], rows(r, slice(64, 128))).then_inc(fin_in[par], 16)

                def emit(T, slot):
                    t = T + AHEAD
                    if live(t) and live(t - 2):
                        wait(sp, S["xT_ps"], nth(t - 2, 0, 1))
                        load_input(t, (slot + AHEAD) % 2)
                    if isinstance(T, int) and T == NT - 1:
                        sp.wait_ge(S["mid_stored"], 16 * 8)
                        load_group(0, 0)
                        load_group(1, 1)
                    if live(T - LAG_OUT):
                        t = T - LAG_OUT
                        wait(sp, S["mid_done"], nth(t, 0, 1))
                        wait(sp, S["mid_stored"], T * 16 - 16 * LAG_OUT)
                        sp.dma_start(mid_rows[ds(t * 128 + t // TPB + 1, 128), :], x[:, ds(t, 1), :].rearrange("p o d -> p (o d)")).then_inc(S["mid_stored"], 16)

                bodies(sp, emit)
                sp.wait_ge(S["mid_stored"], 16 * NT)

                def emit_group(g, par):
                    if exists(g + 2):
                        sp.wait_ge(S["fnorm_done"], g + 1)
                        load_group(g + 2, par)
                    sp.wait_ge(S["new_done"], g + 1)
                    wait(sp, new_stored[par], (g // 2) * 16)
                    r = g * 512 + g // (NG // 2) + 1
                    sp.dma_start(x_rows[ds(r, 512), :].rearrange("(t p) d -> p t d", p=128), x[:, ds(g * 4, 4), :]).then_inc(new_stored[par], 16)

                groups(sp, emit_group)
                sp.wait_ge(new_stored[0], 16 * NG // 2)
                sp.wait_ge(new_stored[1], 16 * NG // 2)

            @block.tensor
            def _(pe):
                def score_head(t, tp, u, h):
                    rows = slice(64 * h, 64 * h + 64)
                    c0 = h * KW
                    nc.tensor.matmul(ps_s[u % 2][0:W, c0 + 128:c0 + KW], qkT[rows, u % 2, 0:W], k_prev[rows, (tp + 1) % 2, u, :],
                                     start=False, stop=False)
                    nc.tensor.matmul(ps_s[u % 2][:, c0:c0 + 128], qkT[rows, u % 2, 0:128], qkT[rows, u % 2, 128:256],
                                     start=False, stop=(h == 1)).then_inc(S["score_ps"] if h else S["score_half"], 1)

                def emit(T, slot):
                    par = slot % 2
                    for s in range(U):
                        if live(T):
                            pe.wait_ge(S["normed"], nth(T, s))
                            wait(pe, S["qkT_done"], nth(T, s - 1))
                            if s == XT_STEP + 1:
                                wait(pe, S["xT_done"], nth(T + AHEAD, 0, 1) if live(T + AHEAD) else NT)
                            nc.tensor.transpose(ps_t[:, 0:128], qk[:, par, s, 0:128], ident[:, :])
                            nc.tensor.transpose(ps_t[:, 128:256], qk[:, par, s, 128:256], ident[:, :]).then_inc(S["qkT_ps"], 1)
                        t, d, u = unit(T, s, AT_PT)
                        if live(t):
                            wait(pe, S["pT_done"], nth(t, u - 1))
                            pe.wait_ge(S["probs_done"], nth(t, u))
                            pr = probs[:, u % 4, :, :]
                            for h in range(2):
                                nc.tensor.transpose(ps_pt[:, 128 * h:128 * h + 128], pr[:, h, 0:128], ident[:, :])
                            for h in range(2):
                                last = nc.tensor.transpose(ps_pt[:, 256 + W * h:256 + W * h + W], pr[0:W, h, W:KW], ident[0:W, 0:W])
                            last.then_inc(S["pT_ps"], 1)
                        t, d, u = unit(T, s, AT_SCORE)
                        if live(t):
                            tp = (par + d) % 2
                            sc = ps_s[u % 2][:, 0:2 * KW].rearrange("p (h k) -> p h k", h=2)
                            wait(pe, S["exp_done"], nth(t, u - 2))
                            pe.wait_ge(S["qkT_done"], nth(t, u))
                            wait(pe, S["kprev_done"], nth(t - 1, u))
                            nc.tensor.matmul(sc, ident_bf[:, :], masks[:, ds(t % TPB, 1), :].to_broadcast([128, 2, KW]), start=True, stop=False)
                            score_head(t, tp, u, 0)
                        t, d, u = unit(T, s, AT_PV)
                        if live(t):
                            wait(pe, S["outT_done"], nth(t, u - 1))
                            pe.wait_ge(S["pT_done"], nth(t, u))
                            pe.wait_ge(S["val_done"], nth(t, u))
                            wait(pe, S["vprev_done"], nth(t - 1, u))
                            for h in range(2):
                                nc.tensor.matmul(ps_o[64 * h:64 * h + 64, 0:128], val[:, (slot + d) % R, u, 64 * h:64 * h + 64],
                                                 probsT[:, u % 2, 128 * h:128 * h + 128], start=True, stop=False)
                                last = nc.tensor.matmul(ps_o[64 * h:64 * h + 64, 0:W], v_prev[128 - W:128, (slot + d - 1) % R, u, 64 * h:64 * h + 64],
                                                        probsT[128 - W:128, u % 2, 256 + W * h:256 + W * h + W], start=False, stop=True)
                            last.then_inc(S["pv_ps"], 1)
                        t, d, u = unit(T, s, AT_SCORE)
                        if live(t):
                            pe.wait_ge(consts_in, 80)
                            pe.wait_ge(S["score_half"], nth(t, u))
                            score_head(t, (par + d) % 2, u, 1)
                        t, d, u = unit(T, s, AT_OUT)
                        if live(t):
                            pe.wait_ge(S["outT_done"], nth(t, u))
                            pe.wait_ge(S["wo_in"], 16 * U)
                            if u == 0:
                                wait(pe, S["mid_done"], nth(t - 1, 0, 1))
                            nc.tensor.matmul(ps_y[:, 0:128], outT[:, u % 2, :], w_out[:, u, :], start=(u == 0), stop=(u == U - 1)).then_inc(S["wo_used"], 1)
                        d, u = project[s]
                        if live(T + d):
                            pe.wait_ge(S["xT_done"], nth(T + d, 0, 1))
                            pe.wait_ge(S["wq_in"], 16 * 3 * U)
                            n = nth(T + d, u - 2)
                            wait(pe, S["sq_done"], n)
                            wait(pe, S["val_done"], n)
                            wait(pe, S["rotated"], n)
                            nc.tensor.matmul(ps_q[u % 2][:, 0:384], xT[:, (par + d) % 2, :], w_qkv[:, u, :, :].rearrange("p j n -> p (j n)"),
                                             start=True, stop=True).then_inc(S["proj_ps"], 1)
                        t = T + AHEAD
                        if s == XT_STEP and live(t):
                            pe.wait_ge(xin_in[(par + AHEAD) % 2], 32 * loads(t))
                            wait(pe, S["qkT_done"], nth(T, s))
                            wait(pe, S["xT_done"], nth(t - 1, 0, 1))
                            nc.tensor.transpose(ps_t[:, 0:128], x_in[:, (par + AHEAD) % 2, :], ident[:, :]).then_inc(S["xT_ps"], 1)

                bodies(pe, emit)

                for n in ("exp_done", "pT_done", "outT_done", "qkT_done", "rotated", "sq_done", "val_done"):
                    pe.wait_ge(S[n], NT * U)
                pe.wait_ge(S["mid_done"], NT)
                pe.wait_ge(S["wf_in"], 16 * 13)

                def transpose_group(g):
                    pe.wait_ge(S["fnorm_done"], g + 1)
                    wait(pe, S["fT_done"], g)
                    for j in range(4):
                        last = nc.tensor.transpose(ps_t[:, 128 * j:128 * j + 128], f_norm[:, j, :], ident[:, :])
                    last.then_inc(S["fT_ps"], 1)

                def down_group(g, par):
                    pe.wait_ge(S["hidden_done"], g * 3 + 3)
                    wait(pe, S["new_done"], g)
                    for j in range(4):
                        for c, (c0, cn) in enumerate(CH):
                            k = cn + (c == 2)
                            last = nc.tensor.matmul(ps_y[:, 128 * j:128 * j + 128], hidden[0:k, par, c, 128 * j:128 * j + 128], w_down[0:k, c, :],
                                                    start=(c == 0), stop=(c == 2))
                    last.then_inc(S["down_ps"], 1)

                def emit_group(g, par):
                    pe.wait_ge(S["fT_done"], g + 1)
                    for j, banks, freed, made in ((1, ps_gate, "gelu_done", "gate_ps"), (0, ps_fact, "hidden_done", "up_ps")):
                        for c, (c0, cn) in enumerate(CH):
                            wait(pe, S[freed], g * 3 - 2 + c if exists(g - 1) else 0)
                            nc.tensor.matmul(banks[c][0:cn, :], w_up[:, j * HID + c0:j * HID + c0 + cn], f_normT[:, :],
                                             start=True, stop=True).then_inc(S[made], 1)
                    if exists(g + 1):
                        transpose_group(g + 1)
                    if exists(g - 1):
                        down_group(g - 1, 1 - par)

                transpose_group(0)
                groups(pe, emit_group)
                down_group(NG - 1, 1)

            @block.scalar
            def _(act):
                def squares_and_values(T, slot, s):
                    d, u = take_up[s]
                    if live(T + d):
                        act.wait_ge(S["proj_ps"], nth(T + d, u))
                        wait(act, S["ss_done"], nth(T + d, u - 2))
                        nc.scalar.activation(squares[:, u % 2, :], ps_q[u % 2][:, 0:256], ACT.Square).then_inc(S["sq_done"], 1)
                        wait(act, S["pv_ps"], nth(T + d - R, u))
                        wait(act, S["vprev_done"], nth(T + d - R, u))
                        nc.scalar.activation(val[:, (slot + d) % R, u, :], ps_q[u % 2][:, 256:384], ACT.Copy).then_inc(S["val_done"], 1)

                def output_copy(T, s):
                    t, d, u = unit(T, s, AT_PV)
                    if live(t):
                        act.wait_ge(S["pv_ps"], nth(t, u))
                        wait(act, S["wo_used"], nth(t, u - 2))
                        nc.scalar.activation(outT[:, u % 2, :], ps_o[:, 0:128], ACT.Copy).then_inc(S["outT_done"], 1)

                def exponentials(T, s):
                    t, d, u = unit(T, s, AT_EXP)
                    if live(t):
                        act.wait_ge(S["max_done"], nth(t, u))
                        wait(act, S["pT_ps"], nth(t, u - 4))
                        sc = ps_s[u % 2][:, 0:2 * KW].rearrange("p (h k) -> p h k", h=2)
                        for h in range(2):
                            last = nc.scalar.activation(probs[:, u % 4, h, :], sc[:, h, :], ACT.Exp, bias=neg_max[:, u % 4, h:h + 1], scale=1.0,
                                                        accum_out=p_sum[:, u % 4, h:h + 1])
                        last.then_inc(S["exp_done"], 1)

                def emit(T, slot):
                    for s in range(U):
                        if live(T):
                            act.wait_ge(S["qkT_ps"], nth(T, s))
                            wait(act, S["score_ps"], nth(T, s - 2))
                            wait(act, S["kprev_done"], nth(T, s - 2))
                            nc.scalar.activation(qkT[:, s % 2, :], ps_t[:, 0:256], ACT.Copy).then_inc(S["qkT_done"], 1)
                        t, d, u = unit(T, s, AT_PT)
                        if live(t):
                            act.wait_ge(S["pT_ps"], nth(t, u))
                            wait(act, S["pv_ps"], nth(t, u - 2))
                            nc.scalar.activation(probsT[:, u % 2, :], ps_pt[:, 0:256 + 2 * W], ACT.Copy).then_inc(S["pT_done"], 1)
                        exponentials(T, s)
                        output_copy(T, s)
                        squares_and_values(T, slot, s)
                        t = T + AHEAD
                        if s == XT_STEP and live(t):
                            act.wait_ge(S["xT_ps"], nth(t, 0, 1))
                            wait(act, S["proj_ps"], nth(t - 2, U - 1))
                            nc.scalar.activation(xT[:, (slot + AHEAD) % 2, :], ps_t[:, 0:128], ACT.Copy).then_inc(S["xT_done"], 1)

                bodies(act, emit)
                act.wait_ge(S["wf_in"], 16 * 13)

                def affine_group(g):
                    act.wait_ge(S["fT_ps"], g + 1)
                    wait(act, S["up_ps"], g * 3)
                    nc.scalar.activation(f_normT[:, :], ps_t[:, :], ACT.Identity, bias=ln_gb[:, 1:2], scale=ln_gb[:, 0:1]).then_inc(S["fT_done"], 1)

                def emit_group(g, par):
                    for c, (c0, cn) in enumerate(CH):
                        act.wait_ge(S["gate_ps"], g * 3 + (c + 1))
                        wait(act, S["hidden_done"], g * 3 - 2 + c if exists(g - 1) else 0)
                        nc.scalar.activation(gate[0:cn, c, :], ps_gate[c][0:cn, :], ACT.Gelu, bias=b_up[0:cn, 1, c:c + 1], scale=1.0).then_inc(S["gelu_done"], 1)
                    if exists(g + 1):
                        affine_group(g + 1)

                affine_group(0)
                groups(act, emit_group)

            @block.vector
            def _(dve):
                R4 = lambda ap: ap.rearrange("p (a h t x) -> p a h t x", a=2, h=2, t=2)

                def newton_link(T, np_, k):
                    r = rnorm[:, np_, :]
                    if k == 0:
                        dve.wait_ge(S["ss_done"], nth(T + 1, U - 1))
                        wait(dve, S["normed"], nth(T - 1, U - 1) if live(T - 1) else 0)
                        ins = nc.vector.tensor_scalar(nw_x[:, :], sumsq[:, :], 1e-24, None, ALU.max)
                    else:
                        dve.wait_ge(S["chain"], (T + 1) * CHAIN + k)
                        if k == 1:
                            ins = nc.vector.tensor_scalar(r.bitcast(I32), nw_x[:, :].bitcast(I32), -0.5, 1597463007.0, ALU.mult, ALU.add)
                        elif k == 2:
                            ins = nc.vector.tensor_scalar(nw_h[:, :], nw_x[:, :], -0.5, None, ALU.mult)
                        elif k % 3 == 0:
                            ins = nc.vector.tensor_tensor(nw_a[:, :], r, r, ALU.mult)
                        elif k % 3 == 1:
                            ins = nc.vector.tensor_tensor(nw_a[:, :], nw_a[:, :], nw_h[:, :], ALU.mult)
                        else:
                            ins = nc.vector.scalar_tensor_tensor(r, nw_a[:, :], 1.5, r, ALU.add, ALU.mult)
                    ins.then_inc(S["chain"], 1)

                def rotate(T, par, s):
                    d, u = take_up[s]
                    if not live(T + d):
                        return
                    dve.wait_ge(S["val_done"], nth(T + d, u))
                    if u == 0:
                        dve.wait_ge(S["rot_done"], nth(T + d, 0, 1))
                        wait(dve, S["chain"], (T + d - 1) * CHAIN + 1)
                    wait(dve, S["added"], nth(T + d, u - 2))
                    qkp = R4(ps_q[u % 2][:, 0:256])
                    cs = rot[:, (par + d) % 2, :, :].rearrange("p (a c) (o t x) -> p a c o t x", a=2, c=2, o=1, t=2)
                    nc.vector.tensor_tensor(R4(cos_part[:, u % 2, :]), qkp, cs[:, :, 0, :, :, :].to_broadcast([128, 2, 2, 2, 32]), ALU.mult)
                    nc.vector.tensor_tensor(R4(sin_part[:, u % 2, :]), qkp[:, :, :, ::-1, :], cs[:, :, 1, :, :, :].to_broadcast([128, 2, 2, 2, 32]), ALU.mult).then_inc(S["rotated"], 1)
                    nc.vector.tensor_reduce(sumsq[:, 4 * u:4 * u + 4], squares[:, u % 2, :].rearrange("p (g d) -> p g d", g=4), AX.X, ALU.add).then_inc(S["ss_done"], 1)

                def emit(T, slot):
                    par = slot % 2
                    for s in range(U):
                        def newton(spot):
                            if live(T + 1):
                                for k in links_at(s, spot):
                                    newton_link(T, (par + 1) % 2, k)
                        t, d, u = unit(T, s, AT_NORM)
                        if live(t):
                            dve.wait_ge(S["exp_done"], nth(t, u))
                            wait(dve, S["probs_done"], nth(t, u - 1))
                            nc.vector.reciprocal(p_rec[:, :], p_sum[:, u % 4, :]).then_inc(S["rec_done"], 1)
                            newton(0)
                            dve.wait_ge(S["rec_done"], nth(t, u))
                            pr = probs[:, u % 4, :, :]
                            nc.vector.tensor_tensor(pr, pr, p_rec[:, :].rearrange("p (h o) -> p h o", o=1).to_broadcast([128, 2, KW]), ALU.mult).then_inc(S["probs_done"], 1)
                        else:
                            newton(0)
                        if live(T):
                            newton(1)
                            dve.wait_ge(S["qkT_done"], nth(T, s))
                            wait(dve, S["score_ps"], nth(T - 1, s))
                            nc.vector.tensor_scalar(k_prev[:, par, s, :], qkT[:, s % 2, 256 - W:256], frame[:, 0:1], None, ALU.mult).then_inc(S["kprev_done"], 1)
                            newton(2)
                            dve.wait_ge(S["val_done"], nth(T, s))
                            wait(dve, S["pv_ps"], nth(T - R + 1, s))
                            nc.vector.tensor_copy(v_prev[128 - W:128, slot, s, :], val[128 - W:128, slot, s, :]).then_inc(S["vprev_done"], 1)
                        else:
                            newton(1)
                            newton(2)
                        t, d, u = unit(T, s, AT_MAX)
                        if live(t):
                            dve.wait_ge(S["score_ps"], nth(t, u))
                            wait(dve, S["exp_done"], nth(t, u - 4))
                            sc = ps_s[u % 2][:, 0:2 * KW].rearrange("p (h k) -> p h k", h=2)
                            nc.vector.tensor_reduce(neg_max[:, u % 4, :], sc, AX.X, ALU.max, negate=True).then_inc(S["max_done"], 1)
                        newton(3)
                        t, d, u = unit(T, s, AT_OUT)
                        if live(t) and u == U - 1:
                            dve.wait_ge(S["wo_used"], nth(t, u))
                            x_t = x[:, ds(t, 1), :].rearrange("p o d -> p (o d)")
                            nc.vector.tensor_tensor(x_t, ps_y[:, 0:128], x_t, ALU.add).then_inc(S["mid_done"], 1)
                        rotate(T, par, s)
                        newton(4)

                bodies(dve, emit)
                dve.wait_ge(S["mid_stored"], 16 * NT)
                step = Steps(dve, S["ln_steps"])
                PER = 7 + 2 + 3 * NEWTONS

                def normalise_group(g, par):
                    step.turn(0, g, PER)
                    dve.wait_ge(fin_in[par], (g // 2) * 32 + 32)
                    for j in range(4):
                        last = nc.vector.bn_stats(stats[:, j, :], f_in[:, par, j, :])
                    step(last)
                    step(nc.vector.memset(f_var[:, :], LN_EPS), settle=False)
                    for j in range(4):
                        step(nc.vector.bn_aggr(mean_var[:, j, :], stats[:, j, :]), settle=(j == 3))
                    step(nc.vector.tensor_tensor(f_var[:, :], f_var[:, :], mean_var[:, :, 1], ALU.add))
                    inverse_root(step, nc, f_rstd[:, :], f_var[:, :], f_half[:, :], f_tmp[:, :], NEWTONS)
                    wait(dve, S["fT_ps"], g)
                    for j in range(4):
                        last = nc.vector.tensor_scalar(f_norm[:, j, :], f_in[:, par, j, :], mean_var[:, j, 0:1], f_rstd[:, j:j + 1], ALU.subtract, ALU.mult)
                    last.then_inc(S["fnorm_done"], 1)

                def add_group(g):
                    dve.wait_ge(S["down_ps"], g + 1)
                    x_g = x[:, ds(g * 4, 4), :].rearrange("p t d -> p (t d)")
                    nc.vector.tensor_tensor(x_g, ps_y[:, :], x_g, ALU.add).then_inc(S["new_done"], 1)

                def emit_group(g, par):
                    if exists(g + 1):
                        normalise_group(g + 1, 1 - par)
                    wait(dve, S["down_ps"], g - 1 if exists(g - 2) else 0)
                    for c, (c0, cn) in enumerate(CH):
                        dve.wait_ge(S["up_ps"], g * 3 + (c + 1))
                        dve.wait_ge(S["gelu_done"], g * 3 + (c + 1))
                        nc.vector.scalar_tensor_tensor(hidden[0:cn, par, c, :], ps_fact[c][0:cn, :], b_up[0:cn, 0, c:c + 1],
                                                       gate[0:cn, c, :], ALU.add, ALU.mult).then_inc(S["hidden_done"], 1)
                    if exists(g - 1):
                        add_group(g - 1)

                normalise_group(0, 0)
                groups(dve, emit_group)
                add_group(NG - 1)

            @block.gpsimd
            def _(pool):
                def to_unit_length(T, par, s):
                    for d, u in normalise[s]:
                        if live(T + d):
                            pool.wait_ge(S["chain"], (T + d + 1) * CHAIN)
                            pool.wait_ge(S["added"], nth(T + d, u))
                            v = qk[:, (par + d) % 2, u, :].rearrange("p (g d) -> p g d", g=4)
                            rr = rnorm[:, (par + d) % 2, 4 * u:4 * u + 4].rearrange("p (g o) -> p g o", o=1).to_broadcast([128, 4, 64])
                            nc.gpsimd.tensor_tensor(v, v, rr, ALU.mult).then_inc(S["normed"], 1)

                def emit(T, slot):
                    par = slot % 2
                    for s in range(U):
                        to_unit_length(T, par, s)
                        d, u = take_up[s]
                        if live(T + d):
                            pool.wait_ge(S["rotated"], nth(T + d, u))
                            wait(pool, S["qkT_ps"], nth(T + d - 2, u))
                            nc.gpsimd.tensor_tensor(qk[:, (par + d) % 2, u, :], cos_part[:, u % 2, :], sin_part[:, u % 2, :], ALU.add).then_inc(S["added"], 1)
                        t = T + AHEAD
                        if s == ROT_STEP and live(t):
                            pool.wait_ge(S["rep_in"], 16 * 6)
                            wait(pool, S["rotated"], nth(t - 2, U - 1))
                            nc.gpsimd.tensor_tensor(rot[:, (par + AHEAD) % 2, :, :].rearrange("p a d -> p (a d)"), rot_base[:, ds(t % TPB, 1), :].rearrange("p o d -> p (o d)"),
                                                    qk_scales[:, :, :].rearrange("p a d -> p (a d)"), ALU.mult).then_inc(S["rot_done"], 1)

                bodies(pool, emit)

        for s in taken:
            nc.gpsimd.sem_clear(s)
        nc.all_engine_barrier()
        loop.close()


def two_layer_kernel(nc, t, out):
    dram = lambda n, shape: nc.dram_tensor(n, shape, F32, kind="Internal").ap()
    qkv = [dram(f"l0_{n}", [4096, 128]) for n in "qkv"]
    x_rows, mid_rows = dram("x_rows", [ROWS, 128]), dram("mid_rows", [ROWS, 128])
    with ExitStack() as ctx:
        mods = ctx.enter_context(nc.sbuf_tensor("mods", [128, 4, 6, 128], F32))
        xr = ctx.enter_context(nc.sbuf_tensor("xr", [128, TILES, 128], F32))
        z = ctx.enter_context(nc.sbuf_tensor("z", [128, TILES, 128], F32))
        zero_rows(nc, (x_rows, mid_rows), t["zeros"])
        modulation_stage(nc, mods, [t["L0_c"], t["L1_c"]], [t["L0_wmod"], t["L1_wmod"]])
        delta_attention_stage(nc, t["L0_attn_x"], xr, mods, [t["L0_attn_WqT"], t["L0_attn_WkT"], t["L0_attn_WvT"]], t["L0_attn_WoT"],
                              t["L0_attn_alpha_raw"], t["L0_attn_beta_raw"], t, qkv)
        feed_stage(nc, "feed0", xr, mods, 0, z, x_rows)
        names = dict(qkv="Wqkv", out="Wo", w1="W1", w2="W2", b1="b1", b2="b2", ln_g="ln_g", ln_b="ln_b", q_scale="q_scale", k_scale="k_scale")
        local_block_stage(nc, "L0", 6, 16, 32, z, x_rows, mid_rows, {k: t["L0_ffn_" + v] for k, v in names.items()}, t)
        residual_stage(nc, "res0", xr, mods, 0, z)
        linear_attention_stage(nc, xr, mods, {k[8:]: v for k, v in t.items() if k.startswith("L1_attn_")}, t)
        feed_stage(nc, "feed1", xr, mods, 1, z, x_rows)
        local_block_stage(nc, "L1", 2, 8, 64, z, x_rows, mid_rows, {k: t["L1_ffn_" + v.lower()] for k, v in names.items()}, t)
        residual_stage(nc, "res1", xr, mods, 2, z, out)


def zero_rows(nc, arrays, zeros):
    with stage_semaphores(nc, "zr") as sem, nc.Block() as block:
        stored = sem("stored")

        @block.sync
        def _(sp):
            total = 0
            for a in arrays:
                n = a.shape[0] // 2049
                sp.dma_start(a.rearrange("(n r) d -> n r d", r=2049)[:, 0, :], zeros[0:n, :]).then_inc(stored, 16)
                total += 16
            sp.wait_ge(stored, total)


def rotary_table(window, n=2048, dim=64):
    half = np.arange(0, dim, 2, dtype=np.float32)
    inv = (np.float32(1.0) / np.float32(10000.0) ** (half / np.float32(dim))).astype(np.float32)
    angle = (np.arange(n, dtype=np.float32)[:, None] * inv[None, :]).astype(np.float32).astype(np.float64)
    base = (half.astype(np.float64) + 0.4 * dim) / (1.4 * dim)
    scale = base[None, :] ** ((np.arange(n) % 128 - 64) / (window // 2))[:, None]
    out = np.zeros((n, 2, 2, dim))
    for a, f in ((0, 8.0 * scale), (1, 1.0 / scale)):
        out[:, a, 0, :] = np.tile(np.cos(angle) * f, 2)
        out[:, a, 1, :] = np.concatenate([-np.sin(angle) * f, np.sin(angle) * f], 1)
    frame = np.tile(base, 4) ** (128 / (window // 2))
    return out.reshape(n, 256).astype(np.float32), frame.reshape(128, 1).astype(np.float32)


def window_masks(window, tiles):
    q, k = np.arange(128)[:, None], np.arange(128)[None, :]
    own = (k <= q) & (q <= k + window) & (q // window - k // window <= 1)
    before = (q <= np.arange(window)[None, :]) & (q < window)
    m = np.zeros((tiles, 128, 128 + window), np.float32)
    for t in range(tiles):
        m[t, :, :128] = np.where(own, 0, -1e30)
        m[t, :, 128:] = np.where(before & (t > 0), 0, -1e30)
    return m.astype(mybir.dt.np(BF16))


def shape_constants():
    p = np.arange(128)
    c = {"ident": np.eye(128, dtype=np.float32), "ident_bf": np.eye(128, dtype=np.float32).astype(mybir.dt.np(BF16)),
         "zeros": np.zeros((16, 128), np.float32), "block01": (p[:, None] // 8 == np.arange(16)[None, :]).astype(np.float32),
         "causal64": np.where(p[:, None] % 64 >= np.arange(64)[None, :], 0, -1e30).astype(mybir.dt.np(BF16)),
         "keep": (p[:, None] <= p[None, :]).astype(np.float32)}
    for w in (32, 64):
        c[f"rot{w}"], c[f"frame{w}"] = rotary_table(w)
        c[f"masks{w}"] = window_masks(w, 16)
    return c


def kernel(**inputs):
    import concourse.bacc as bacc
    from concourse.bass_utils import run_bass_kernel_spmd

    nc = bacc.Bacc("TRN2", target_bir_lowering=False, num_devices=1)
    transposed = {"L0_attn_Wq", "L0_attn_Wk", "L0_attn_Wv", "L0_attn_Wo", "L1_attn_q_w", "L1_attn_k_w", "L1_attn_v_w", "L1_attn_o_w", "L1_attn_f1_w", "L1_attn_f2_w"}
    arrays = {}
    for name, a in inputs.items():
        a = np.asarray(a)
        if name in transposed:
            name, a = name + "T", a.T
        arrays[name] = np.ascontiguousarray(a)
    arrays.update(shape_constants())
    t = {n: nc.dram_tensor("in_" + n, a.shape, mybir.dt.from_np(a.dtype), kind="ExternalInput").ap() for n, a in arrays.items()}
    out = nc.dram_tensor("out_x", (2, 2048, 128), F32, kind="ExternalOutput").ap()
    two_layer_kernel(nc, t, out)
    r = run_bass_kernel_spmd(nc, [{"in_" + n: a for n, a in arrays.items()}], core_ids=[0])
    return r.results[0]["out_x"]
```

```python
from contextlib import ExitStack, contextmanager

import numpy as np

import concourse.bass as bass
from concourse import mybir
from concourse.bass import ds

F32, BF16, I32 = mybir.dt.float32, mybir.dt.bfloat16, mybir.dt.int32
ACT = mybir.ActivationFunctionType
ALU = mybir.AluOpType
AX = mybir.AxisListType
LN_EPS = 1e-5
TILES = 32
ROWS = 2 * 2049


class Steps:

    def __init__(self, eng, sem):
        self.eng, self.sem, self.base, self.n = eng, sem, 0, 0

    def __call__(self, ins, settle=True):
        self.n += 1
        ins.then_inc(self.sem, 1)
        if settle:
            self.eng.wait_ge(self.sem, self.base + self.n)
        return self.base + self.n

    def settle(self):
        self.eng.wait_ge(self.sem, self.base + self.n)

    def turn(self, before, i, per):
        self.base, self.n = before + i * per, 0


@contextmanager
def stage_semaphores(nc, prefix):
    taken = []

    def take(name):
        taken.append(nc.alloc_semaphore(name=f"{prefix}_{name}"))
        return taken[-1]

    yield take
    nc.clear_and_free_semaphores(taken)
    nc.all_engine_barrier()


def wait(eng, sem, value):
    if not isinstance(value, int) or value > 0:
        eng.wait_ge(sem, value)


def pairs(eng, n, emit):
    emit(0, 0)
    emit(1, 1)
    with eng.Fori(1, n // 2) as p:
        emit(p * 2, 0)
        emit(p * 2 + 1, 1)


def inverse_root(step, nc, out, x, half, tmp, newtons=3):
    step(nc.vector.tensor_scalar(out.bitcast(I32), x.bitcast(I32), -0.5, 1597463007.0, ALU.mult, ALU.add))
    step(nc.vector.tensor_scalar(half, x, -0.5, None, ALU.mult))
    for _ in range(newtons):
        step(nc.vector.tensor_tensor(tmp, out, out, ALU.mult))
        step(nc.vector.tensor_tensor(tmp, tmp, half, ALU.mult))
        step(nc.vector.scalar_tensor_tensor(out, tmp, 1.5, out, ALU.add, ALU.mult))


def group_stats(nc, dve, step, x, mean, rstd, bufs):
    st, mv, var, half, tmp = bufs
    for g in range(8):
        for j in range(4):
            step(nc.vector.bn_stats(st[:, j, :], x[:, 4 * g + j, :]), settle=(j == 3))
        for j in range(4):
            step(nc.vector.bn_aggr(mv[:, j, :], st[:, j, :]), settle=(j == 3))
        step(nc.vector.tensor_copy(mean[:, 4 * g:4 * g + 4], mv[:, :, 0]))
        step(nc.vector.tensor_scalar(var[:, 4 * g:4 * g + 4], mv[:, :, 1], LN_EPS, None, ALU.add))
    inverse_root(step, nc, rstd[:, :], var[:, :], half[:, :], tmp[:, :])


def modulated_group(nc, step, x, mean, rstd, out, mods, g, layer, part, done):
    for j in range(4):
        T = 4 * g + j
        step(nc.vector.tensor_scalar(out[:, j, :], x[:, T, :], mean[:, T:T + 1], rstd[:, T:T + 1], ALU.subtract, ALU.mult), settle=(j == 3))
    k = g // 4 + 2 * layer
    vec = lambda i: mods[:, k:k + 1, 3 * part + i, :].to_broadcast([128, 4, 128])
    step(nc.vector.tensor_tensor(out, out, vec(1), ALU.mult))
    nc.vector.tensor_tensor(out, out, vec(0), ALU.add).then_inc(done, 1)


def modulation_stage(nc, mods, c_rows, w_mod):
    with ExitStack() as ctx:
        sb = lambda n, shape, dt=F32: ctx.enter_context(nc.sbuf_tensor(f"mod_{n}", shape, dt))
        sem = ctx.enter_context(stage_semaphores(nc, "mod"))
        c = sb("c", [128, 4])
        e = sb("e", [128, 4])
        silu = sb("silu", [128, 4])
        wide = sb("wide", [128, 4, 128])
        w = sb("w", [128, 2, 768])
        sign = sb("sign", [128, 128])
        mag = sb("mag", [128, 128])
        ps = [[ctx.enter_context(nc.psum_tensor(f"mod_ps{k}{j}", [128, 512], F32)) for j in range(2)] for k in range(4)]
        loaded, exped, wide_done, product, seq = sem("loaded"), sem("exped"), sem("wide_done"), sem("product"), sem("seq")
        with nc.Block() as block:
            @block.sync
            def _(sp):
                for l in range(2):
                    sp.dma_start(w[:, l, :], w_mod[l]).then_inc(loaded, 16)
                    for b in range(2):
                        sp.dma_start(c[:, 2 * l + b:2 * l + b + 1], c_rows[l][b, :].rearrange("(p o) -> p o", o=1)).then_inc(loaded, 16)

            @block.scalar
            def _(act):
                act.wait_ge(loaded, 96)
                nc.scalar.activation(e[:, :], c[:, :], ACT.Exp, scale=-1.0).then_inc(exped, 1)

            @block.tensor
            def _(pe):
                pe.wait_ge(loaded, 96)
                pe.wait_ge(wide_done, 1)
                for k in range(4):
                    for j in range(2):
                        last = nc.tensor.matmul(ps[k][j][:, 0:384], wide[:, k, :], w[:, k // 2, 384 * j:384 * j + 384], start=True, stop=True)
                last.then_inc(product, 1)

            @block.vector
            def _(dve):
                step = Steps(dve, seq)
                dve.wait_ge(exped, 1)
                step(nc.vector.tensor_scalar(e[:, :], e[:, :], 1.0, None, ALU.add))
                step(nc.vector.reciprocal(e[:, :], e[:, :]))
                step(nc.vector.tensor_tensor(silu[:, :], e[:, :], c[:, :], ALU.mult))
                nc.vector.tensor_copy(wide[:, :, :], silu[:, :].rearrange("p (k o) -> p k o", o=1).to_broadcast([128, 4, 128])).then_inc(wide_done, 1)
                dve.wait_ge(product, 1)
                for k in range(4):
                    for j in range(2):
                        src = ps[k][j]
                        out = mods[:, k, 3 * j:3 * j + 3, :]
                        step(nc.vector.tensor_copy(out[:, 0, :], src[:, 0:128]))
                        step(nc.vector.tensor_scalar(out[:, 1, :], src[:, 128:256], 1.0, None, ALU.add))
                        step(nc.vector.tensor_scalar(sign[:, :], src[:, 256:384], 0.0, 2.0, ALU.is_ge, ALU.mult))
                        step(nc.vector.tensor_scalar(mag[:, :], src[:, 256:384], -1.0, 0.25, ALU.mult, ALU.max))
                        step(nc.vector.scalar_tensor_tensor(mag[:, :], src[:, 256:384], 0.25, mag[:, :], ALU.max, ALU.max))
                        step(nc.vector.scalar_tensor_tensor(out[:, 2, :], sign[:, :], -1.0, mag[:, :], ALU.add, ALU.mult))


def delta_attention_stage(nc, x_dram, xr, mods, w_qkvT, w_oT, alpha_raw, beta_raw, tables, qkv_dram):
    H, DH, SUB, N_SUB = 16, 8, 32, 128
    with ExitStack() as ctx:
        sem = ctx.enter_context(stage_semaphores(nc, "da"))
        keep = lambda n, shape, dt=F32: ctx.enter_context(nc.sbuf_tensor(f"da_{n}", shape, dt))
        mem = keep("mem", [128, 64, 128])
        ident = keep("ident", [128, 128])
        block01 = keep("block01", [128, 16])
        trans_a = keep("trans_a", [128, DH, N_SUB])
        trans_b = keep("trans_b", [128, DH, N_SUB])

        with ExitStack() as c2:
            sb = lambda n, shape, dt=F32: c2.enter_context(nc.sbuf_tensor(f"da_{n}", shape, dt))
            ps = [c2.enter_context(nc.psum_tensor(f"da_psa{i}", [128, 512], F32)) for i in range(8)]
            hT = sb("hT", [128, 4096])
            st, mv = sb("st", [128, 4, 6]), sb("mv", [128, 4, 2])
            mean, var, rstd, half, tmp = (sb(n, [128, 32]) for n in ("mean", "var", "rstd", "half", "tmp"))
            h = sb("h", [128, 2, 4, 128])
            w3 = sb("w3", [128, 384])
            qs = sb("qs", [128, SUB, 128])
            ks = sb("ks", [128, SUB, 128])
            vs = sb("vs", [128, SUB, 128])
            state = sb("state", [128, H, 16, DH])
            prod = sb("prod", [128, H, 16, DH])
            dots = sb("dots", [128, H, 16])
            flat_state = prod[:, :, :, :].rearrange("p a b c -> p a (b c)")
            rk, rk_half, rk_tmp, rk_x = (sb(n, [128, SUB * H]) for n in ("rk", "rk_half", "rk_tmp", "rk_x"))
            alpha, beta = sb("alpha", [128, H]), sb("beta", [128, H])
            loaded, seq, h_ready, hT_ps, hT_done = (sem(n) for n in ("loaded", "seq", "h_ready", "hT_ps", "hT_done"))
            proj_ps, q_out, k_out, v_out, sig_exp = (sem(n) for n in ("proj_ps", "q_out", "k_out", "v_out", "sig_exp"))
            k_normed, stored, state_done, tr_ps, tr_done = (sem(n) for n in ("k_normed", "stored", "state_done", "tr_ps", "tr_done"))

            state_init, pool_state_done, pool_seq = sem("state_init"), sem("pool_state_done"), sem("pool_seq")
            H_DVE = 12
            key = sb("key", [128, DH * (H - H_DVE)])

            def recurrence_operands(t, hs):
                k_t = ks[:, ds(t, 1), :].rearrange("p o (h e) -> p (o h) e", e=DH)[:, hs, :]
                v_t = vs[:, ds(t, 1), :].rearrange("p o (h e) -> p (o h) e", e=DH)[:, hs, :]
                n = hs.stop - hs.start
                kb = k_t.rearrange("p h (o e) -> p h o e", o=1).to_broadcast([128, n, 16, DH])
                ub = dots[:, hs, :].rearrange("p h (r o) -> p h r o", o=1).to_broadcast([128, n, 16, DH])
                return kb, ub, v_t, alpha[:, hs].rearrange("p (h o) -> p h o", o=1).to_broadcast([128, n, 16])

            with nc.Block() as block:
                @block.sync
                def _(sp):
                    for b in range(2):
                        sp.dma_start(xr[:, 16 * b:16 * b + 16, :], x_dram[b].rearrange("(t p) d -> p t d", p=128)).then_inc(loaded, 16)
                    sp.dma_start(ident[:, :], tables["ident"]).then_inc(loaded, 16)
                    sp.dma_start(block01[:, :], tables["block01"]).then_inc(loaded, 16)
                    for j in range(3):
                        sp.dma_start(w3[:, 128 * j:128 * j + 128], w_qkvT[j]).then_inc(loaded, 16)
                    sp.dma_start(alpha[:, :], alpha_raw.rearrange("a h b c -> (a b c) h").partition_broadcast(128)).then_inc(loaded, 16)
                    sp.dma_start(beta[:, :], beta_raw.rearrange("a h b c -> (a b c) h").partition_broadcast(128)).then_inc(loaded, 16)
                    sp.wait_ge(q_out, SUB)
                    sp.dma_start(qkv_dram[0].rearrange("(s t) d -> s t d", t=SUB), qs[:, :, :]).then_inc(stored, 16)
                    sp.wait_ge(v_out, SUB)
                    sp.dma_start(qkv_dram[2].rearrange("(s t) d -> s t d", t=SUB), vs[:, :, :]).then_inc(stored, 16)
                    sp.wait_ge(stored, 32)
                    sp.wait_ge(k_normed, 1)
                    sp.dma_start(qkv_dram[1].rearrange("(s t) d -> s t d", t=SUB), ks[:, :, :]).then_inc(stored, 16)
                    sp.wait_ge(stored, 48)

                @block.tensor
                def _(pe):
                    pe.wait_ge(loaded, 144)
                    for g in range(8):
                        pe.wait_ge(h_ready, g + 1)
                        wait(pe, hT_done, g - 1)
                        for i in range(4):
                            last = nc.tensor.transpose(ps[g % 2][:, 128 * i:128 * i + 128], h[:, g % 2, i, :], ident[:, :])
                        last.then_inc(hT_ps, 1)
                    pe.wait_ge(hT_done, 8)
                    for t in range(SUB):
                        wait(pe, q_out, t - 3)
                        wait(pe, v_out, t - 3)
                        nc.tensor.matmul(ps[2 + t % 4][:, 0:384], hT[:, t:4096:SUB], w3[:, :], start=True, stop=True).then_inc(proj_ps, 1)
                    pe.wait_ge(state_done, 1)
                    pe.wait_ge(v_out, SUB)
                    for j in range(4):
                        wait(pe, tr_done, 2 * (j - 1))
                        for i in range(4):
                            n = 4 * j + i
                            last = nc.tensor.transpose(ps[j % 2][:, 128 * i:128 * i + 128], flat_state[:, n, :], ident[:, :])
                        last.then_inc(tr_ps, 1)

                @block.scalar
                def _(act):
                    act.wait_ge(loaded, 144)
                    nc.scalar.activation(alpha[:, :], alpha[:, :], ACT.Exp, scale=-1.0).then_inc(sig_exp, 1)
                    nc.scalar.activation(beta[:, :], beta[:, :], ACT.Exp, scale=-1.0).then_inc(sig_exp, 1)
                    for g in range(8):
                        act.wait_ge(hT_ps, g + 1)
                        nc.scalar.activation(hT[:, 512 * g:512 * g + 512], ps[g % 2][:, :], ACT.Copy).then_inc(hT_done, 1)
                    for t in range(SUB):
                        act.wait_ge(proj_ps, t + 1)
                        nc.scalar.activation(qs[:, t, :], ps[2 + t % 4][:, 0:128], ACT.Copy).then_inc(q_out, 1)
                        nc.scalar.activation(ks[:, t, :], ps[2 + t % 4][:, 128:256], ACT.Copy).then_inc(k_out, 1)
                        nc.scalar.activation(vs[:, t, :], ps[2 + t % 4][:, 256:384], ACT.Copy).then_inc(v_out, 1)
                    for j in range(4):
                        act.wait_ge(tr_ps, j + 1)
                        dst = (trans_a if j < 2 else trans_b)[:, 4 * (j % 2):4 * (j % 2) + 4, :]
                        nc.scalar.activation(dst, ps[j % 2][:, :].rearrange("p (i s) -> p i s", i=4), ACT.Copy).then_inc(tr_done, 2)

                @block.gpsimd
                def _(pool):
                    step = Steps(pool, pool_seq)
                    pool.wait_ge(state_init, 1)
                    hs = slice(H_DVE, H)
                    with pool.Fori(0, SUB) as t:
                        step.turn(0, t, 9)
                        _, ub, v_t, alpha_b = recurrence_operands(t, hs)
                        k_t = ks[:, ds(t, 1), DH * H_DVE:DH * H].rearrange("p o d -> p (o d)")
                        step(nc.gpsimd.tensor_copy(key[:, :], k_t))
                        kb = key[:, :].rearrange("p (h o e) -> p h o e", o=1, e=DH).to_broadcast([128, H - H_DVE, 16, DH])
                        step(nc.gpsimd.tensor_tensor(prod[:, hs, :, :], state[:, hs, :, :], kb, ALU.mult))
                        step(nc.gpsimd.tensor_tensor(prod[:, hs, :, 0:4], prod[:, hs, :, 0:4], prod[:, hs, :, 4:8], ALU.add))
                        step(nc.gpsimd.tensor_tensor(prod[:, hs, :, 0:2], prod[:, hs, :, 0:2], prod[:, hs, :, 2:4], ALU.add))
                        step(nc.gpsimd.tensor_tensor(dots[:, hs, :], prod[:, hs, :, 0], prod[:, hs, :, 1], ALU.add))
                        step(nc.gpsimd.tensor_tensor(dots[:, hs, :], dots[:, hs, :], alpha_b, ALU.mult))
                        step(nc.gpsimd.tensor_tensor(dots[:, hs, DH:16], dots[:, hs, DH:16], v_t, ALU.add))
                        step(nc.gpsimd.tensor_tensor(prod[:, hs, :, :], ub, kb, ALU.mult))
                        step(nc.gpsimd.tensor_tensor(state[:, hs, :, :], state[:, hs, :, :], prod[:, hs, :, :], ALU.add))
                    pool.sem_inc(pool_state_done, 1)

                @block.vector
                def _(dve):
                    step = Steps(dve, seq)
                    dve.wait_ge(loaded, 144)
                    group_stats(nc, dve, step, xr, mean, rstd, (st, mv, var, half, tmp))
                    for g in range(8):
                        wait(dve, hT_ps, g - 1)
                        modulated_group(nc, step, xr, mean, rstd, h[:, g % 2, :, :], mods, g, 0, 0, h_ready)
                    dve.wait_ge(sig_exp, 2)
                    for v, f in ((alpha, -0.5), (beta, 2.0)):
                        step(nc.vector.tensor_scalar(v[:, :], v[:, :], 1.0, None, ALU.add))
                        step(nc.vector.reciprocal(v[:, :], v[:, :]))
                        step(nc.vector.tensor_scalar(v[:, :], v[:, :], f, None, ALU.mult))
                    dve.wait_ge(k_out, SUB)
                    flat = prod[:, :, :, :].rearrange("p a b c -> p (a b c)")
                    kf = ks[:, :, :].rearrange("p t d -> p (t d)")
                    for j in range(2):
                        part = slice(2048 * j, 2048 * j + 2048)
                        step(nc.vector.tensor_tensor(flat, kf[:, part], kf[:, part], ALU.mult))
                        step(nc.vector.tensor_reduce(rk_x[:, 256 * j:256 * j + 256], flat.rearrange("p (g e) -> p g e", e=DH), AX.X, ALU.add))
                    step(nc.vector.tensor_scalar(rk_x[:, :], rk_x[:, :], 1e-24, None, ALU.max))
                    inverse_root(step, nc, rk[:, :], rk_x[:, :], rk_half[:, :], rk_tmp[:, :])
                    kg = kf.rearrange("p (g e) -> p g e", e=DH)
                    rkg = rk[:, :].rearrange("p (g o) -> p g o", o=1).to_broadcast([128, SUB * H, DH])
                    nc.vector.tensor_tensor(kg, kg, rkg, ALU.mult).then_inc(k_normed, 1)
                    dve.wait_ge(k_normed, 1)
                    dve.wait_ge(v_out, SUB)
                    dve.wait_ge(stored, 32)
                    for t in range(0, SUB, 8):
                        v4 = vs[:, t:t + 8, :].rearrange("p t (h e) -> p (t h) e", e=DH)
                        for i in range(8):
                            vi = vs[:, t + i, :].rearrange("p (h e) -> p h e", e=DH)
                            step(nc.vector.tensor_tensor(vi, vi, beta[:, :].rearrange("p (h o) -> p h o", o=1).to_broadcast([128, H, DH]), ALU.mult), settle=(i == 7))
                    step(nc.vector.memset(state[:, :, :, :], 0.0))
                    step(nc.vector.memset(state[:, :, :, :].rearrange("p h r e -> p h (r e)")[:, :, 0:64:9], 1.0))
                    dve.sem_inc(state_init, 1)
                    before = step.base + step.n
                    hs = slice(0, H_DVE)
                    with dve.Fori(0, SUB) as t:
                        step.turn(before, t, 6)
                        kb, ub, v_t, alpha_b = recurrence_operands(t, hs)
                        step(nc.vector.tensor_tensor(prod[:, hs, :, :], state[:, hs, :, :], kb, ALU.mult))
                        step(nc.vector.tensor_reduce(dots[:, hs, :], prod[:, hs, :, :], AX.X, ALU.add))
                        step(nc.vector.tensor_tensor(dots[:, hs, :], dots[:, hs, :], alpha_b, ALU.mult))
                        step(nc.vector.tensor_tensor(dots[:, hs, DH:16], dots[:, hs, DH:16], v_t, ALU.add))
                        step(nc.vector.tensor_tensor(prod[:, hs, :, :], ub, kb, ALU.mult))
                        step(nc.vector.tensor_tensor(state[:, hs, :, :], state[:, hs, :, :], prod[:, hs, :, :], ALU.add))
                    step.turn(before, SUB, 6)
                    dve.wait_ge(pool_state_done, 1)
                    step(nc.vector.tensor_copy(flat_state[:, 0:DH, :].rearrange("p e (h r) -> p h r e", r=DH), state[:, :, 0:DH, :]))
                    step(nc.vector.tensor_copy(flat_state[:, DH:16, :].rearrange("p d (h e) -> p h d e", e=DH), state[:, :, DH:16, :]))
                    dve.sem_inc(state_done, 1)

        with ExitStack() as c3:
            sb = lambda n, shape, dt=F32: c3.enter_context(nc.sbuf_tensor(f"da_{n}", shape, dt))
            ps = [c3.enter_context(nc.psum_tensor(f"da_psb{i}", [128, 512], F32)) for i in range(4)]
            mT = sb("mT", [128, 2, 65, DH])
            a_bd = sb("a_bd", [128, 2, 2, 128])
            m_bd = sb("m_bd", [128, 2, 4, 128])
            tenth = sb("tenth", [128, 16])
            m_init, a_built, m_ps, m_done, wide, wide_ps, mem_done, seq = (sem("c_" + n) for n in ("m_init", "a_built", "m_ps", "m_done", "wide", "wide_ps", "mem_done", "seq"))
            with nc.Block() as block:
                @block.gpsimd
                def _(pool):
                    def emit(s, par):
                        wait(pool, m_ps, 2 * (s - 1))
                        for b in range(2):
                            src = trans_a[:, :, ds(64 * b + s, 1)].rearrange("p e (o n) -> p (n o) e", o=1).to_broadcast([128, 16, DH])
                            nc.gpsimd.tensor_tensor(a_bd[:, par, b, :].rearrange("p (h e) -> p h e", e=DH), src,
                                                    block01[:, :].rearrange("p (h o) -> p h o", o=1).to_broadcast([128, 16, DH]), ALU.mult).then_inc(a_built, 1)
                    pairs(pool, 64, emit)

                @block.tensor
                def _(pe):
                    pe.wait_ge(m_init, 1)

                    def emit(s, par):
                        for b in range(2):
                            pe.wait_ge(a_built, 2 * s + b + 1)
                            wait(pe, m_done, 2 * (s - 1) + b + 1)
                            nc.tensor.matmul(ps[b][:, 0:DH], a_bd[:, par, b, :], mT[:, b, ds(s, 1), :].rearrange("p o d -> p (o d)"),
                                             start=True, stop=True).then_inc(m_ps, 1)
                    pairs(pe, 64, emit)
                    for n in range(16):
                        pe.wait_ge(wide, n + 1)
                        wait(pe, mem_done, n - 1)
                        for i in range(4):
                            last = nc.tensor.transpose(ps[2 + n % 2][:, 128 * i:128 * i + 128], m_bd[:, n % 2, i, :], ident[:, :])
                        last.then_inc(wide_ps, 1)

                @block.scalar
                def _(act):
                    for n in range(16):
                        act.wait_ge(wide_ps, n + 1)
                        nc.scalar.activation(mem[:, 4 * n:4 * n + 4, :], ps[2 + n % 2][:, :].rearrange("p (i c) -> p i c", i=4), ACT.Copy).then_inc(mem_done, 1)

                @block.vector
                def _(dve):
                    step = Steps(dve, seq)
                    step(nc.vector.tensor_scalar(tenth[:, :], block01[:, :], 0.1, None, ALU.mult))
                    nc.vector.memset(mT[:, :, 0:1, :], 0.0).then_inc(m_init, 1)

                    def emit(s, par):
                        for b in range(2):
                            dve.wait_ge(m_ps, 2 * s + b + 1)
                            nc.vector.tensor_tensor(mT[:, b, ds(s + 1, 1), :].rearrange("p o d -> p (o d)"), ps[b][:, 0:DH],
                                                    trans_b[:, :, ds(64 * b + s, 1)].rearrange("p d n -> p (d n)"), ALU.add).then_inc(m_done, 1)
                    pairs(dve, 64, emit)
                    dve.wait_ge(m_done, 128)
                    dve.wait_ge(m_init, 1)
                    for n in range(16):
                        wait(dve, wide_ps, n - 1)
                        for i in range(4):
                            c = 4 * n + i
                            src = mT[:, c // 32, 2 * (c % 32), :]
                            last = nc.vector.tensor_tensor(m_bd[:, n % 2, i, :].rearrange("p (h d) -> p h d", d=DH),
                                                           src.rearrange("p (o d) -> p o d", o=1).to_broadcast([128, 16, DH]),
                                                           tenth[:, :].rearrange("p (h o) -> p h o", o=1).to_broadcast([128, 16, DH]), ALU.mult)
                        last.then_inc(wide, 1)

        with ExitStack() as c4:
            sb = lambda n, shape, dt=F32: c4.enter_context(nc.sbuf_tensor(f"da_{n}", shape, dt))
            pb = lambda n: c4.enter_context(nc.psum_tensor(f"da_{n}", [128, 512], F32))
            q_t, k_t = sb("q_t", [128, 2, 128]), sb("k_t", [128, 2, 128])
            v_t = sb("v_t", [128, 2, 2, 128])
            q_pad, k_pad = sb("q_pad", [128, 2, 16, 32]), sb("k_pad", [128, 2, 16, 32])
            q_T, k_T, q_c = sb("q_T", [128, 512]), sb("k_T", [128, 512]), sb("q_c", [128, 2, 128])
            p = sb("p", [128, 2, 4, 4, 64])
            neg_max, p_sum = sb("neg_max", [128, 4, 4]), sb("p_sum", [128, 4, 4])
            p_T = sb("p_T", [128, 8, 128])
            att, att_T, gated = sb("att", [128, 128]), sb("att_T", [128, 128]), sb("gated", [128, 128])
            w_o = sb("w_o", [128, 128])
            causal = sb("causal", [128, 64], BF16)
            ident_bf = sb("ident_bf", [128, 128], BF16)
            mem_t = sb("mem_t", [128, 2, 2, 128])
            s_ps = [pb(f"s_ps{i}") for i in range(4)]
            t_ps = [pb(f"t_ps{i}") for i in range(2)]
            o_ps = [pb(f"o_ps{i}") for i in range(2)]
            names = ("const", "mem_ready", "padded", "zeroed", "qkT_ps", "qT_done", "kT_done", "s_done", "shifted", "exped", "p_done",
                     "pT_ps", "pTa", "pTb", "o_done", "att_done", "attT_ps", "attT_done", "y_done", "x_done",
                     "max_steps", "sum_steps", "att_steps", "gate_steps")
            S = {n: sem("t_" + n) for n in names}
            qk_in = [sem("t_qk_in0"), sem("t_qk_in1")]
            v_in = [sem("t_v_in0"), sem("t_v_in1")]

            exists = lambda T: not isinstance(T, int) or 0 <= T < TILES

            def turns(eng, emit):
                for i in range(4):
                    emit(i, i % 2)
                with eng.Fori(2, TILES // 2 - 1) as r:
                    emit(r * 2, 0)
                    emit(r * 2 + 1, 1)
                for i in range(TILES - 2, TILES + 2):
                    emit(i, i % 2)

            with nc.Block() as block:
                @block.sync
                def _(sp):
                    sp.dma_start(w_o[:, :], w_oT).then_inc(S["const"], 16)
                    sp.dma_start(causal[:, :], tables["causal64"]).then_inc(S["const"], 16)
                    sp.dma_start(ident_bf[:, :], tables["ident_bf"]).then_inc(S["const"], 16)

                    def emit(i, par):
                        if exists(i):
                            wait(sp, S["qkT_ps"], i - 1)
                            sp.dma_start(q_t[:, par, :], qkv_dram[0][ds(i * 128, 128), :]).then_inc(qk_in[par], 16)
                            sp.dma_start(k_t[:, par, :], qkv_dram[1][ds(i * 128, 128), :]).then_inc(qk_in[par], 16)
                        t = i - 1
                        if exists(t):
                            wait(sp, S["o_done"], t - 1)
                            for half_ in range(2):
                                sp.dma_start(v_t[64 * half_:64 * half_ + 64, 1 - par, :, :],
                                             qkv_dram[2][ds(t * 128, 128), :].rearrange("(c k) d -> k c d", c=2)).then_inc(v_in[1 - par], 16)
                    turns(sp, emit)

                @block.tensor
                def _(pe):
                    pe.wait_ge(S["const"], 48)
                    pe.wait_ge(S["zeroed"], 2)

                    def emit(i, par):
                        t, w = i - 1, i - 2
                        if exists(i):
                            pe.wait_ge(S["padded"], i * 2 + 2)
                            wait(pe, S["pTa"], i - 1)
                            wait(pe, S["pTb"], i - 1)
                            for src, dst in ((q_pad, t_ps[0]), (k_pad, t_ps[1])):
                                for g in range(4):
                                    nc.tensor.transpose(dst[:, 128 * g:128 * g + 128], src[:, par, 4 * g:4 * g + 4, :].rearrange("p h e -> p (h e)"), ident[:, :])
                            pe.wait_ge(qk_in[par], (i // 2) * 32 + 32)
                            wait(pe, S["att_done"], i - 1)
                            wait(pe, S["x_done"], i - 2)
                            nc.tensor.transpose(o_ps[1][:, 0:128], q_t[:, par, :], ident[:, :]).then_inc(S["qkT_ps"], 1)
                        if exists(w):
                            pe.wait_ge(S["att_done"], w + 1)
                            wait(pe, S["attT_done"], w)
                            nc.tensor.transpose(o_ps[0][:, 128:256], att[:, :], ident[:, :]).then_inc(S["attT_ps"], 1)
                        if exists(i):
                            wait(pe, S["shifted"], i * 4)
                            for hh in range(4):
                                nc.tensor.matmul(s_ps[hh][:, 0:256].rearrange("p (g k) -> p g k", g=4), ident_bf[:, :],
                                                 causal[:, :].rearrange("p (o k) -> p o k", o=1).to_broadcast([128, 4, 64]), start=True, stop=False)
                            pe.wait_ge(S["qT_done"], i * 2 + 2)
                        if exists(w):
                            pe.wait_ge(S["attT_done"], w + 1)
                            nc.tensor.matmul(o_ps[1][:, 128:256], att_T[:, :], w_o[:, :], start=True, stop=True).then_inc(S["y_done"], 1)
                        if exists(i):
                            pe.wait_ge(S["qT_done"], i * 2 + 2)
                            pe.wait_ge(S["kT_done"], i + 1)
                            for g in range(4):
                                for hh in range(4):
                                    for c in range(2):
                                        rows, cols = slice(32 * hh, 32 * hh + 32), slice(128 * g + 64 * c, 128 * g + 64 * c + 64)
                                        last = nc.tensor.matmul(s_ps[hh][64 * c:64 * c + 64, 64 * g:64 * g + 64], q_T[rows, cols], k_T[rows, cols], start=False, stop=(g == 3))
                            last.then_inc(S["s_done"], 1)
                        if exists(t):
                            for hh in range(4):
                                pe.wait_ge(S["p_done"], t * 4 + (hh + 1))
                                for j in range(2):
                                    n = 2 * hh + j
                                    last = nc.tensor.transpose(t_ps[n // 4][:, 128 * (n % 4):128 * (n % 4) + 128],
                                                               p[:, 1 - par, hh, 2 * j:2 * j + 2, :].rearrange("p g k -> p (g k)"), ident[:, :])
                                if hh % 2:
                                    last.then_inc(S["pT_ps"], 1)
                            pe.wait_ge(v_in[1 - par], (t // 2) * 32 + 32)
                            wait(pe, S["x_done"], w + 1)
                            pe.wait_ge(S["mem_ready"], t + 1)
                            for c in range(2):
                                nc.tensor.matmul(o_ps[0][64 * c:64 * c + 64, 0:128], q_c[:, 1 - par, 64 * c:64 * c + 64], mem_t[:, 1 - par, c, :], start=True, stop=False)
                            pe.wait_ge(S["zeroed"], 2)
                            pe.wait_ge(S["pTa"], t + 1)
                            pe.wait_ge(S["pTb"], t + 1)
                            for n in range(8):
                                for gp in range(2):
                                    g = 2 * (n % 2) + gp
                                    head = 4 * g + n // 2
                                    for c in range(2):
                                        rows = slice(64 * gp, 64 * gp + 64)
                                        last = nc.tensor.matmul(o_ps[gp][64 * c:64 * c + 64, DH * head:DH * head + DH], p_T[rows, n, 64 * c:64 * c + 64],
                                                                v_t[rows, 1 - par, c, DH * head:DH * head + DH], start=(gp == 1), stop=(gp == 1 or n == 7))
                            last.then_inc(S["o_done"], 1)
                    turns(pe, emit)

                @block.gpsimd
                def _(pool):
                    def emit(T, par):
                        wait(pool, S["o_done"], T - 1)
                        nc.gpsimd.tensor_copy(mem_t[:, par, :, :], mem[:, ds(2 * T, 2), :]).then_inc(S["mem_ready"], 1)
                    pairs(pool, 32, emit)

                @block.scalar
                def _(act):
                    act.wait_ge(S["zeroed"], 2)

                    def pad(T, par):
                        act.wait_ge(qk_in[par], (T // 2) * 32 + 32)
                        wait(act, S["qkT_ps"], T - 1)
                        nc.scalar.activation(q_pad[:, par, :, 0:DH], q_t[:, par, :].rearrange("p (h e) -> p h e", e=DH), ACT.Copy, scale=float(DH) ** -0.5).then_inc(S["padded"], 1)
                        nc.scalar.activation(k_pad[:, par, :, 0:DH], k_t[:, par, :].rearrange("p (h e) -> p h e", e=DH), ACT.Copy).then_inc(S["padded"], 1)

                    def emit(i, par):
                        t, w = i - 1, i - 2
                        if exists(i):
                            act.wait_ge(S["qkT_ps"], i + 1)
                            wait(act, S["s_done"], i)
                            nc.scalar.activation(q_T[:, :], t_ps[0][:, :], ACT.Copy).then_inc(S["qT_done"], 1)
                            wait(act, S["o_done"], i - 1)
                            nc.scalar.activation(q_c[:, par, :], o_ps[1][:, 0:128], ACT.Copy).then_inc(S["qT_done"], 1)
                        if exists(w):
                            act.wait_ge(S["attT_ps"], w + 1)
                            wait(act, S["y_done"], w)
                            nc.scalar.activation(att_T[:, :], o_ps[0][:, 128:256], ACT.Copy).then_inc(S["attT_done"], 1)
                        for hh in range(4):
                            if exists(i):
                                act.wait_ge(S["shifted"], i * 4 + (hh + 1))
                                nc.scalar.activation(p[:, par, hh, :, :], p[:, par, hh, :, :], ACT.Exp).then_inc(S["exped"], 1)
                            if hh == 0 and exists(t):
                                act.wait_ge(S["pT_ps"], t * 2 + 1)
                                wait(act, S["o_done"], t)
                                nc.scalar.activation(p_T[:, 0:4, :], t_ps[0][:, :].rearrange("p (n q) -> p n q", n=4), ACT.Copy).then_inc(S["pTa"], 1)
                        if exists(i + 1):
                            pad(i + 1, 1 - par)
                    pad(0, 0)
                    turns(act, emit)

                @block.vector
                def _(dve):
                    max_step, sum_step, att_step, gate_step = (Steps(dve, S[n]) for n in ("max_steps", "sum_steps", "att_steps", "gate_steps"))
                    nc.vector.memset(q_pad[:, :, :, :], 0.0).then_inc(S["zeroed"], 1)
                    nc.vector.memset(k_pad[:, :, :, :], 0.0).then_inc(S["zeroed"], 1)
                    wide = lambda a: a.rearrange("p (g o) -> p g o", o=1).to_broadcast([128, 4, 64])

                    def shift(par, heads_):
                        for hh in heads_:
                            sc = s_ps[hh][:, 0:256].rearrange("p (g k) -> p g k", g=4)
                            max_step(nc.vector.tensor_reduce(neg_max[:, hh, :], sc, AX.X, ALU.max, negate=True))
                            nc.vector.tensor_tensor(p[:, par, hh, :, :], sc, wide(neg_max[:, hh, :]), ALU.add).then_inc(S["shifted"], 1)

                    def emit(i, par):
                        t, w = i - 1, i - 2
                        max_step.turn(0, i, 4)
                        if exists(i):
                            dve.wait_ge(S["qkT_ps"], i + 1)
                            wait(dve, S["s_done"], i)
                            nc.vector.tensor_copy(k_T[:, :], t_ps[1][:, :]).then_inc(S["kT_done"], 1)
                        if exists(t):
                            sum_step.turn(0, t, 8)
                            for hh in range(4):
                                dve.wait_ge(S["exped"], t * 4 + (hh + 1))
                                ph = p[:, 1 - par, hh, :, :]
                                sum_step(nc.vector.tensor_reduce(p_sum[:, hh, :], ph, AX.X, ALU.add))
                                sum_step(nc.vector.reciprocal(p_sum[:, hh, :], p_sum[:, hh, :]))
                                nc.vector.tensor_tensor(ph, ph, wide(p_sum[:, hh, :]), ALU.mult).then_inc(S["p_done"], 1)
                        if exists(w):
                            gate_step.turn(0, w, 1)
                            dve.wait_ge(S["y_done"], w + 1)
                            wait(dve, S["x_done"], w)
                            gate = mods[:, ds(w // 16, 1), 2, :].rearrange("p o d -> p (o d)")
                            gate_step(nc.vector.tensor_tensor(gated[:, :], o_ps[1][:, 128:256], gate, ALU.mult))
                            x_t = xr[:, ds(w, 1), :].rearrange("p o d -> p (o d)")
                            nc.vector.tensor_tensor(x_t, x_t, gated[:, :], ALU.add).then_inc(S["x_done"], 1)
                        if exists(i):
                            dve.wait_ge(S["s_done"], i + 1)
                            wait(dve, S["pT_ps"], i * 2 - 2)
                            shift(par, (0, 1))
                        if exists(t):
                            dve.wait_ge(S["pT_ps"], t * 2 + 2)
                            wait(dve, S["o_done"], t)
                            nc.vector.tensor_copy(p_T[:, 4:8, :], t_ps[1][:, :].rearrange("p (n q) -> p n q", n=4)).then_inc(S["pTb"], 1)
                        if exists(i):
                            shift(par, (2, 3))
                        if exists(t):
                            att_step.turn(0, t, 1)
                            dve.wait_ge(S["o_done"], t + 1)
                            wait(dve, S["attT_ps"], t)
                            att_step(nc.vector.tensor_copy(att[:, :], o_ps[0][:, 0:128]))
                            odd = att[:, :].rearrange("p (a x) -> p a x", a=2)[:, :, 32:64]
                            nc.vector.tensor_tensor(odd, odd, o_ps[1][:, 0:128].rearrange("p (a x) -> p a x", a=2)[:, :, 32:64], ALU.add).then_inc(S["att_done"], 1)
                    turns(dve, emit)


def feed_stage(nc, name, xr, mods, layer, z, x_rows):
    with ExitStack() as ctx:
        sb = lambda n, shape, dt=F32: ctx.enter_context(nc.sbuf_tensor(f"{name}_{n}", shape, dt))
        sem = ctx.enter_context(stage_semaphores(nc, name))
        st, mv = sb("st", [128, 4, 6]), sb("mv", [128, 4, 2])
        mean, var, rstd, half, tmp = (sb(n, [128, 32]) for n in ("mean", "var", "rstd", "half", "tmp"))
        seq, h_ready = sem("seq"), sem("h_ready")
        stored = [sem("stored0"), sem("stored1")]
        with nc.Block() as block:
            @block.vector
            def _(dve):
                step = Steps(dve, seq)
                group_stats(nc, dve, step, xr, mean, rstd, (st, mv, var, half, tmp))
                for g in range(8):
                    modulated_group(nc, step, xr, mean, rstd, z[:, 4 * g:4 * g + 4, :], mods, g, layer, 1, h_ready)

            @block.sync
            def _(sp):
                for g in range(8):
                    sp.wait_ge(h_ready, g + 1)
                    r = 512 * g + g // 4 + 1
                    sp.dma_start(x_rows[r:r + 512, :].rearrange("(t p) d -> p t d", p=128), z[:, 4 * g:4 * g + 4, :]).then_inc(stored[g % 2], 16)
                for j in range(2):
                    sp.wait_ge(stored[j], 64)


def residual_stage(nc, name, xr, mods, k0, z, out=None):
    with ExitStack() as ctx:
        sem = ctx.enter_context(stage_semaphores(nc, name))
        scaled, added, stored = sem("scaled"), sem("added"), sem("stored")
        with nc.Block() as block:
            @block.sync
            def _(sp):
                if out is not None:
                    for g in range(8):
                        sp.wait_ge(added, g + 1)
                        t = 4 * (g % 4)
                        sp.dma_start(out[g // 4].rearrange("(t p) d -> p t d", p=128)[:, t:t + 4, :], xr[:, 4 * g:4 * g + 4, :]).then_inc(stored, 16)
                    sp.wait_ge(stored, 128)

            @block.vector
            def _(dve):
                for g in range(8):
                    k = k0 + g // 4
                    z4 = z[:, 4 * g:4 * g + 4, :]
                    nc.vector.tensor_tensor(z4, z4, mods[:, k:k + 1, 5, :].to_broadcast([128, 4, 128]), ALU.mult).then_inc(scaled, 1)
                for g in range(8):
                    dve.wait_ge(scaled, g + 1)
                    x4 = xr[:, 4 * g:4 * g + 4, :]
                    nc.vector.tensor_tensor(x4, x4, z[:, 4 * g:4 * g + 4, :], ALU.add).then_inc(added, 1)


def linear_attention_stage(nc, xr, mods, W, tables):
    F, N_CONST, NT, NG = 64, 21, TILES, TILES // 4
    with ExitStack() as ctx:
        sb = lambda n, shape, dt=F32: ctx.enter_context(nc.sbuf_tensor(f"la_{n}", shape, dt))
        pb = lambda n: ctx.enter_context(nc.psum_tensor(f"la_{n}", [128, 512], F32))
        sem = ctx.enter_context(stage_semaphores(nc, "la"))
        st, mv = sb("st", [128, 4, 6]), sb("mv", [128, 4, 2])
        mean, var, rstd, half, tmp = (sb(n, [128, 32]) for n in ("mean", "var", "rstd", "half", "tmp"))
        mean2, rstd2 = sb("mean2", [128, 32]), sb("rstd2", [128, 32])
        h = sb("h", [128, 32, 128])
        xm = sb("xm", [128, 32, 128])
        xn = sb("xn", [128, 2, 128])
        xnT = sb("xnT", [128, 2, 128])
        qT, kT = sb("qT", [64, 2, 128]), sb("kT", [64, 2, 128])
        low = sb("low", [64, 2, 128])
        high = sb("high", [64, 2, 128])
        k_tok = sb("k_tok", [128, 2, 64])
        v1 = sb("v1", [128, 2, 129])
        sT = sb("sT", [128, 128])
        kv = sb("kv", [64, 129])
        rden = sb("rden", [128, 1])
        att, attT = sb("att", [128, 128]), sb("attT", [128, 128])
        f_mv, f_var, f_half, f_tmp, f_rstd = sb("f_mv", [128, 4, 2]), *(sb(n, [128, 4]) for n in ("f_var", "f_half", "f_tmp", "f_rstd"))
        f_stats = sb("f_stats", [128, 4, 6])
        y_n, y_T = sb("y_n", [128, 4, 128]), sb("y_T", [128, 512])
        g_T = sb("g_T", [128, 2, 4, 512])
        res = sb("res", [128, 4, 128])
        w_qk, w_v, w_o, w_f1, w_f2 = sb("w_qk", [128, 128]), sb("w_v", [128, 128]), sb("w_o", [128, 128]), sb("w_f1", [128, 512]), sb("w_f2", [128, 4, 128])
        b_qk = sb("b_qk", [64, 2])
        b_v, b_o, b_f2 = sb("b_v", [128, 128]), sb("b_o", [128, 128]), sb("b_f2", [128, 128])
        b_f1 = sb("b_f1", [128, 4])
        ln = sb("ln", [128, 4])
        ident, keep_mask = sb("ident", [128, 128]), sb("keep_mask", [128, 128])
        p_t, p_qk, p_v, p_s, p_n, p_kv, p_kt, p_at = (pb(n) for n in ("p_t", "p_qk", "p_v", "p_s", "p_n", "p_kv", "p_kt", "p_at"))
        p_up = [p_qk, p_v, p_s, p_n]
        names = ("const", "seq", "h_ready", "h_bias", "xn_done", "xT_ps", "xT_done", "qk_ps", "v_ps", "high_done", "low_done", "exped", "feat", "ktok_ps", "ktok_done",
                 "v_done", "s_ps", "s_done", "n_ps", "den_steps", "kv_ps", "kv_done", "att_done", "attT_ps", "attT_done", "o_ps", "mid_done",
                 "ln_steps", "yn_done", "yT_ps", "yT_done", "up_ps", "gelu", "down_ps", "freed", "res_steps")
        S = {n: sem(n) for n in names}

        exists = lambda T, n=NT: not isinstance(T, int) or 0 <= T < n

        def turns(eng, emit):
            for i in range(4):
                emit(i, i % 2)
            with eng.Fori(2, NT // 4) as p:
                emit(p * 2, 0)
                emit(p * 2 + 1, 1)
            emit(NT // 2, 0)
            emit(NT // 2 + 1, 1)
            with eng.Fori(NT // 4 + 1, NT // 2 - 1) as p:
                emit(p * 2, 0)
                emit(p * 2 + 1, 1)
            for i in range(NT - 2, NT + 2):
                emit(i, i % 2)

        def groups(eng, emit):
            emit(0, 0)
            emit(1, 1)
            with eng.Fori(1, NG // 2 - 1) as p:
                emit(p * 2, 0)
                emit(p * 2 + 1, 1)
            emit(NG - 2, 0)
            emit(NG - 1, 1)

        with nc.Block() as block:
            @block.sync
            def _(sp):
                loads = [(ident[:, :], tables["ident"]), (keep_mask[:, :], tables["keep"]), (w_qk[:, 0:F], W["q_wT"]), (w_qk[:, F:2 * F], W["k_wT"]),
                         (w_v[:, :], W["v_wT"]), (w_o[:, :], W["o_wT"]), (w_f1[:, :], W["f1_wT"]), (w_f2[:, :, :], W["f2_wT"].rearrange("(c p) n -> p c n", p=128))]
                col = lambda a: a.rearrange("(p o) -> p o", o=1)
                loads += [(b_qk[:, 0:1], col(W["q_b"])), (b_qk[:, 1:2], col(W["k_b"]))]
                loads += [(b_f1[:, c:c + 1], col(W["f1_b"][128 * c:128 * c + 128])) for c in range(4)]
                loads += [(ln[:, i:i + 1], col(W[n])) for i, n in enumerate(("ln1_w", "ln1_b", "ln2_w", "ln2_b"))]
                loads += [(dst, W[n].rearrange("(o n) -> o n", o=1).partition_broadcast(128)) for dst, n in ((b_v[:, :], "v_b"), (b_o[:, :], "o_b"), (b_f2[:, :], "f2_b"))]
                assert len(loads) == N_CONST
                for dst, src in loads:
                    sp.dma_start(dst, src).then_inc(S["const"], 16)

            @block.tensor
            def _(pe):
                pe.wait_ge(S["const"], 16 * N_CONST)

                def emit(i, par):
                    t = i - 2
                    if exists(t):
                        pe.wait_ge(S["att_done"], t + 1)
                        wait(pe, S["mid_done"], t)
                        nc.tensor.transpose(p_at[:, 0:128], att[:, :], ident[:, :]).then_inc(S["attT_ps"], 1)
                    if exists(i):
                        pe.wait_ge(S["xn_done"], i + 1)
                        wait(pe, S["xT_done"], i)
                        nc.tensor.transpose(p_t[:, 0:128], xn[:, par, :], ident[:, :]).then_inc(S["xT_ps"], 1)
                    if exists(i - 1):
                        pe.wait_ge(S["feat"], i * 2)
                        wait(pe, S["s_done"], i - 1)
                        wait(pe, S["ktok_done"], i - 1)
                        nc.tensor.matmul(p_s[:, 0:128], kT[:, 1 - par, :], qT[:, 1 - par, :], start=True, stop=True).then_inc(S["s_ps"], 1)
                        nc.tensor.transpose(p_kt[:, 0:F], kT[:, 1 - par, :], ident[0:F, 0:F]).then_inc(S["ktok_ps"], 1)
                    if exists(t):
                        pe.wait_ge(S["attT_done"], t + 1)
                        nc.tensor.matmul(p_at[:, 128:256], attT[:, :], w_o[:, :], start=True, stop=True).then_inc(S["o_ps"], 1)
                    if exists(i):
                        pe.wait_ge(S["xT_done"], i + 1)
                        wait(pe, S["low_done"], i)
                        nc.tensor.matmul(p_qk[0:F, 0:128], w_qk[:, 0:F], xnT[:, par, :], start=True, stop=True)
                        nc.tensor.matmul(p_qk[0:F, 128:256], w_qk[:, F:2 * F], xnT[:, par, :], start=True, stop=True).then_inc(S["qk_ps"], 1)
                        wait(pe, S["v_done"], i)
                        nc.tensor.matmul(p_v[:, 0:128], xnT[:, par, :], w_v[:, :], start=True, stop=True).then_inc(S["v_ps"], 1)
                    if exists(i - 1):
                        pe.wait_ge(S["s_done"], i)
                        pe.wait_ge(S["v_done"], i)
                        wait(pe, S["att_done"], i - 1)
                        nc.tensor.matmul(p_n[:, 0:129], sT[:, :], v1[:, 1 - par, :], start=True, stop=False)
                        pe.wait_ge(S["kv_done"], i)
                        nc.tensor.matmul(p_n[:, 0:129], qT[:, 1 - par, :], kv[:, :], start=False, stop=True).then_inc(S["n_ps"], 1)
                        pe.wait_ge(S["ktok_done"], i)
                        nc.tensor.matmul(p_kv[0:F, 0:129], k_tok[:, 1 - par, :], v1[:, 1 - par, :], start=True, stop=True).then_inc(S["kv_ps"], 1)

                turns(pe, emit)

                pe.wait_ge(S["kv_done"], NT + 1)
                pe.wait_ge(S["mid_done"], NT)

                def transpose_group(g):
                    pe.wait_ge(S["yn_done"], g + 1)
                    wait(pe, S["yT_done"], g)
                    for j in range(4):
                        last = nc.tensor.transpose(p_t[:, 128 * j:128 * j + 128], y_n[:, j, :], ident[:, :])
                    last.then_inc(S["yT_ps"], 1)

                def down_group(g, par):
                    pe.wait_ge(S["gelu"], g * 4 + 4)
                    wait(pe, S["freed"], g)
                    for j in range(4):
                        for c in range(4):
                            last = nc.tensor.matmul(p_kv[:, 128 * j:128 * j + 128], g_T[:, par, c, 128 * j:128 * j + 128], w_f2[:, c, :], start=(c == 0), stop=(c == 3))
                    last.then_inc(S["down_ps"], 1)

                def emit_group(g, par):
                    pe.wait_ge(S["yT_done"], g + 1)
                    for c in range(4):
                        wait(pe, S["gelu"], g * 4 - 3 + c if exists(g - 1, NG) else 0)
                        nc.tensor.matmul(p_up[c][:, :], w_f1[:, 128 * c:128 * c + 128], y_T[:, :], start=True, stop=True).then_inc(S["up_ps"], 1)
                    if exists(g + 1, NG):
                        transpose_group(g + 1)
                    if exists(g - 1, NG):
                        down_group(g - 1, 1 - par)

                transpose_group(0)
                groups(pe, emit_group)
                down_group(NG - 1, 1)

            @block.scalar
            def _(act):
                act.wait_ge(S["const"], 16 * N_CONST)

                def emit(i, par):
                    t = i - 2
                    if exists(i):
                        act.wait_ge(S["xT_ps"], i + 1)
                        wait(act, S["v_ps"], i - 1)
                        nc.scalar.activation(xnT[:, par, :], p_t[:, 0:128], ACT.Identity, bias=ln[:, 1:2], scale=ln[:, 0:1]).then_inc(S["xT_done"], 1)
                    if exists(t):
                        act.wait_ge(S["attT_ps"], t + 1)
                        wait(act, S["o_ps"], t)
                        nc.scalar.activation(attT[:, :], p_at[:, 0:128], ACT.Copy).then_inc(S["attT_done"], 1)
                    if exists(i - 1):
                        act.wait_ge(S["ktok_ps"], i)
                        wait(act, S["kv_ps"], i - 2)
                        nc.scalar.activation(k_tok[:, 1 - par, :], p_kt[:, 0:F], ACT.Copy).then_inc(S["ktok_done"], 1)
                    if exists(i):
                        act.wait_ge(S["low_done"], i + 1)
                        nc.scalar.activation(low[:, :, :], low[:, :, :], ACT.Exp).then_inc(S["exped"], 1)

                turns(act, emit)

                def affine_group(g):
                    act.wait_ge(S["yT_ps"], g + 1)
                    wait(act, S["up_ps"], g * 4)
                    nc.scalar.activation(y_T[:, :], p_t[:, :], ACT.Identity, bias=ln[:, 3:4], scale=ln[:, 2:3]).then_inc(S["yT_done"], 1)

                def emit_group(g, par):
                    wait(act, S["down_ps"], g - 1 if exists(g - 2, NG) else 0)
                    for c in range(4):
                        act.wait_ge(S["up_ps"], g * 4 + (c + 1))
                        nc.scalar.activation(g_T[:, par, c, :], p_up[c][:, :], ACT.Gelu, bias=b_f1[:, c:c + 1], scale=1.0).then_inc(S["gelu"], 1)
                    if exists(g + 1, NG):
                        affine_group(g + 1)

                affine_group(0)
                groups(act, emit_group)

            @block.gpsimd
            def _(pool):
                pool.wait_ge(S["const"], 16 * N_CONST)
                for g in range(NG):
                    pool.wait_ge(S["h_ready"], g + 1)
                    nc.gpsimd.tensor_tensor(xm[:, 4 * g:4 * g + 4, :], h[:, 4 * g:4 * g + 4, :], b_o[:, :].rearrange("p (o d) -> p o d", o=1).to_broadcast([128, 4, 128]),
                                            ALU.add).then_inc(S["h_bias"], 1)

            @block.vector
            def _(dve):
                step = Steps(dve, S["seq"])
                dve.wait_ge(S["const"], 16 * N_CONST)
                group_stats(nc, dve, step, xr, mean, rstd, (st, mv, var, half, tmp))
                for g in range(8):
                    modulated_group(nc, step, xr, mean, rstd, h[:, 4 * g:4 * g + 4, :], mods, g, 1, 0, S["h_ready"])
                dve.wait_ge(S["h_ready"], 8)
                group_stats(nc, dve, step, h, mean2, rstd2, (st, mv, var, half, tmp))
                step(nc.vector.memset(v1[:, :, :], 1.0))
                nc.vector.memset(kv[:, :], 0.0).then_inc(S["kv_done"], 1)
                dve.wait_ge(S["h_bias"], NG)
                den_step = Steps(dve, S["den_steps"])
                row = lambda a, T: a[:, ds(T, 1), :].rearrange("p o d -> p (o d)")

                def normalise(T, par):
                    wait(dve, S["xT_ps"], T - 1)
                    nc.vector.tensor_scalar(xn[:, par, :], row(h, T), mean2[:, ds(T, 1)], rstd2[:, ds(T, 1)], ALU.subtract, ALU.mult).then_inc(S["xn_done"], 1)

                def emit(i, par):
                    t = i - 1
                    if exists(t):
                        dve.wait_ge(S["s_ps"], i)
                        wait(dve, S["n_ps"], t)
                        nc.vector.tensor_tensor(sT[:, :], p_s[:, 0:128], keep_mask[:, :], ALU.mult).then_inc(S["s_done"], 1)
                    if exists(i):
                        dve.wait_ge(S["qk_ps"], i + 1)
                        wait(dve, S["feat"], i * 2)
                        for j in range(2):
                            src = p_qk[0:F, 128 * j:128 * j + 128]
                            high_last = nc.vector.tensor_scalar(high[:, j, :], src, b_qk[:, j:j + 1], 0.0, ALU.add, ALU.max)
                            if j:
                                high_last.then_inc(S["high_done"], 1)
                            low_last = nc.vector.tensor_scalar(low[:, j, :], src, b_qk[:, j:j + 1], 0.0, ALU.add, ALU.min)
                        low_last.then_inc(S["low_done"], 1)
                        dve.wait_ge(S["v_ps"], i + 1)
                        wait(dve, S["kv_ps"], i - 1)
                        nc.vector.tensor_tensor(v1[:, par, 0:128], p_v[:, 0:128], b_v[:, :], ALU.add).then_inc(S["v_done"], 1)
                    if exists(t):
                        den_step.turn(0, t, 2)
                        dve.wait_ge(S["n_ps"], i)
                        wait(dve, S["attT_ps"], t)
                        den_step(nc.vector.tensor_scalar(rden[:, :], p_n[:, 128:129], 1e-6, None, ALU.add))
                        den_step(nc.vector.reciprocal(rden[:, :], rden[:, :]))
                        nc.vector.tensor_scalar(att[:, :], p_n[:, 0:128], rden[:, 0:1], None, ALU.mult).then_inc(S["att_done"], 1)
                        dve.wait_ge(S["kv_ps"], i)
                        dve.wait_ge(S["kv_done"], i)
                        if isinstance(i, int) and i == NT // 2:
                            nc.vector.memset(kv[:, :], 0.0).then_inc(S["kv_done"], 1)
                        else:
                            nc.vector.tensor_tensor(kv[:, :], kv[:, :], p_kv[0:F, 0:129], ALU.add).then_inc(S["kv_done"], 1)
                    if exists(i):
                        dve.wait_ge(S["exped"], i + 1)
                        dve.wait_ge(S["high_done"], i + 1)
                        wait(dve, S["n_ps"], i - 1)
                        wait(dve, S["ktok_ps"], i - 1)
                        for j, dst in enumerate((qT, kT)):
                            nc.vector.tensor_tensor(dst[:, par, :], high[:, j, :], low[:, j, :], ALU.add).then_inc(S["feat"], 1)
                    if exists(i - 2):
                        dve.wait_ge(S["o_ps"], i - 1)
                        nc.vector.tensor_tensor(row(xm, i - 2), p_at[:, 128:256], row(xm, i - 2), ALU.add).then_inc(S["mid_done"], 1)
                    if exists(i + 1):
                        normalise(i + 1, 1 - par)

                normalise(0, 0)
                turns(dve, emit)

                dve.wait_ge(S["mid_done"], NT)
                ln_step, res_step = Steps(dve, S["ln_steps"]), Steps(dve, S["res_steps"])
                four = lambda a, g: a[:, ds(g * 4, 4), :]

                def normalise_group(g):
                    ln_step.turn(0, g, 18)
                    for j in range(4):
                        last = nc.vector.bn_stats(f_stats[:, j, :], row(xm, g * 4 + j))
                    ln_step(last)
                    ln_step(nc.vector.memset(f_var[:, :], LN_EPS), settle=False)
                    for j in range(4):
                        ln_step(nc.vector.bn_aggr(f_mv[:, j, :], f_stats[:, j, :]), settle=(j == 3))
                    ln_step(nc.vector.tensor_tensor(f_var[:, :], f_var[:, :], f_mv[:, :, 1], ALU.add))
                    inverse_root(ln_step, nc, f_rstd[:, :], f_var[:, :], f_half[:, :], f_tmp[:, :])
                    wait(dve, S["yT_ps"], g)
                    for j in range(4):
                        last = nc.vector.tensor_scalar(y_n[:, j, :], row(xm, g * 4 + j), f_mv[:, j, 0:1], f_rstd[:, j:j + 1], ALU.subtract, ALU.mult)
                    last.then_inc(S["yn_done"], 1)

                def add_group(g):
                    res_step.turn(0, g, 4)
                    wide = lambda a: a.to_broadcast([128, 4, 128])
                    dve.wait_ge(S["down_ps"], g + 1)
                    res_step(nc.vector.tensor_tensor(res[:, :, :], p_kv[:, :].rearrange("p (t d) -> p t d", t=4), four(xm, g), ALU.add))
                    dve.sem_inc(S["freed"], 1)
                    res_step(nc.vector.tensor_tensor(res[:, :, :], res[:, :, :], wide(b_f2[:, :].rearrange("p (o d) -> p o d", o=1)), ALU.add))
                    res_step(nc.vector.tensor_tensor(res[:, :, :], res[:, :, :], wide(mods[:, ds(g // (NG // 2) + 2, 1), 2, :]), ALU.mult))
                    res_step(nc.vector.tensor_tensor(four(xr, g), four(xr, g), res[:, :, :], ALU.add))

                def emit_group(g, par):
                    if exists(g + 1, NG):
                        normalise_group(g + 1)
                    if exists(g - 1, NG):
                        add_group(g - 1)

                normalise_group(0)
                groups(dve, emit_group)
                add_group(NG - 1)


def local_block_stage(nc, name, depth, heads, window, x, x_rows, mid_rows, weights, tables):
    U = heads // 2
    W = window
    KW = 128 + W
    NT = TILES
    TPB = NT // 2
    HID = 341
    CH = [(0, 128), (128, 128), (256, HID - 256)]
    AT_SCORE, AT_MAX, AT_EXP, AT_NORM, AT_PT, AT_PV, AT_OUT = 1, 1, 2, 3, 4, 5, 6
    LAG_OUT = (U - 1 + AT_OUT) // U
    NEWTONS = 3
    CHAIN = 3 + 3 * NEWTONS
    if U == 8:
        project = [(1, s + 4) if s < 4 else (2, s - 4) for s in range(8)]
        take_up = [(1, s + 3) if s < 5 else (2, s - 5) for s in range(8)]
        normalise = [[(0, s + 2)] if s < 6 else [(1, 0), (1, 1)] if s == 7 else [] for s in range(8)]
        link_spots = [(4, 4), (4, 4)] + [(s, spot) for s in (5, 6) for spot in range(5)]
        AHEAD, XT_STEP, ROT_STEP = 2, 3, 2
    else:
        project = [(2, s + 1) if s < 3 else (3, 0) for s in range(4)]
        take_up = [(2, s) for s in range(4)]
        normalise = [[(0, 2)], [(0, 3)], [], [(1, 0), (1, 1)]]
        link_spots = [(s, spot) for s in range(3) for spot in range(4)]
        AHEAD, XT_STEP, ROT_STEP = 3, 2, 2
    R = {8: 2, 4: 4}[U]
    links_at = lambda s, spot: [k for k in range(CHAIN) if link_spots[k] == (s, spot)]
    first_full = {2: 2, 4: 4}[R]
    last_full = NT - 2 if R == 2 else NT - 4

    with ExitStack() as ctx:
        sb = lambda n, shape, dt=F32: ctx.enter_context(nc.sbuf_tensor(f"{name}_{n}", shape, dt))
        pb = lambda n, shape=(128, 512), dt=F32: ctx.enter_context(nc.psum_tensor(f"{name}_{n}", list(shape), dt))
        once = ctx.enter_context(stage_semaphores(nc, name + "_once"))
        sem = ctx.enter_context(stage_semaphores(nc, name))
        taken = []

        def layer_sem(n):
            taken.append(sem(n))
            return taken[-1]

        w_qkv = sb("w_qkv", [128, U, 3, 128])
        w_out = sb("w_out", [128, U, 128])
        w_up = sb("w_up", [128, 2 * HID])
        w_down = sb("w_down", [128, 3, 128])
        b_up = sb("b_up", [128, 2, 3])
        ln_gb = sb("ln_gb", [128, 2])
        qk_scales = sb("qk_scales", [128, 4, 64])
        rot_base = sb("rot_base", [128, TPB, 256])
        rot = sb("rot", [128, 2, 4, 64])
        frame = sb("frame", [128, 1])
        masks = sb("masks", [128, TPB, KW], BF16)
        ident = sb("ident", [128, 128])
        ident_bf = sb("ident_bf", [128, 128], BF16)
        x_in = sb("x_in", [128, 2, 128])
        xT = sb("xT", [128, 2, 128])
        squares = sb("squares", [128, 2, 256])
        sumsq = sb("sumsq", [128, 4 * U])
        cos_part = sb("cos_part", [128, 2, 256])
        sin_part = sb("sin_part", [128, 2, 256])
        qk = sb("qk", [128, 2, U, 256])
        val = sb("val", [128, R, U, 128])
        qkT = sb("qkT", [128, 2, 256])
        k_prev = sb("k_prev", [128, 2, U, W])
        v_prev = sb("v_prev", [128, R, U, 128])
        probs = sb("probs", [128, 4, 2, KW])
        neg_max = sb("neg_max", [128, 4, 2])
        p_sum = sb("p_sum", [128, 4, 2])
        p_rec = sb("p_rec", [128, 2])
        probsT = sb("probsT", [128, 2, 256 + 2 * W])
        outT = sb("outT", [128, 2, 128])
        nw_x = sb("nw_x", [128, 4 * U])
        nw_h = sb("nw_h", [128, 4 * U])
        nw_a = sb("nw_a", [128, 4 * U])
        rnorm = sb("rnorm", [128, 2, 4 * U])
        f_in = sb("f_in", [128, 2, 4, 128])
        f_norm = sb("f_norm", [128, 4, 128])
        f_normT = sb("f_normT", [128, 512])
        gate = sb("gate", [128, 3, 512])
        hidden = sb("hidden", [128, 2, 3, 512])
        stats = sb("stats", [128, 4, 6])
        mean_var = sb("mean_var", [128, 4, 2])
        f_var, f_half, f_tmp, f_rstd = (sb(n, [128, 4]) for n in ("f_var", "f_half", "f_tmp", "f_rstd"))

        ps_q = [pb("ps_q0"), pb("ps_q1")]
        ps_s = [pb("ps_s0"), pb("ps_s1")]
        ps_t, ps_pt, ps_o, ps_y = pb("ps_t"), pb("ps_pt"), pb("ps_o"), pb("ps_y")
        ps_gate, ps_fact = [ps_q[0], ps_q[1], ps_s[0]], [ps_s[1], ps_pt, ps_o]

        consts_in = once("consts_in")
        zeroed = once("zeroed")

        S = {n: layer_sem(n) for n in (
            "rep_in", "wq_in", "wo_in", "wf_in", "xin_in0", "xin_in1", "fin_in0", "fin_in1", "mid_stored", "new_stored0", "new_stored1",
            "xT_ps", "proj_ps", "qkT_ps", "score_half", "score_ps", "pT_ps", "pv_ps", "wo_used", "fT_ps", "gate_ps", "up_ps", "down_ps",
            "sq_done", "val_done", "xT_done", "qkT_done", "exp_done", "pT_done", "outT_done", "fT_done", "gelu_done",
            "ss_done", "rotated", "max_done", "rec_done", "probs_done", "kprev_done", "vprev_done", "chain", "mid_done",
            "ln_steps", "fnorm_done", "hidden_done", "new_done",
            "rot_done", "added", "normed")}
        xin_in = [S["xin_in0"], S["xin_in1"]]
        fin_in = [S["fin_in0"], S["fin_in1"]]
        new_stored = [S["new_stored0"], S["new_stored1"]]

        def unit(T, s, lag):
            d, u = divmod(s - lag, U)
            return T + d, d, u

        def nth(T, u, per=U):
            return T * per + (u + 1)

        def loads(T):
            return T // 2 + 1

        def live(T):
            return not isinstance(T, int) or 0 <= T < NT

        def bodies(eng, emit):
            for T in range(-AHEAD, first_full):
                emit(T, T % R)
            with eng.Fori(0, (last_full - first_full) // R) as p:
                for r in range(R):
                    emit(p * R + (first_full + r), r)
            for T in range(last_full, NT + LAG_OUT):
                emit(T, T % R)

        NG = NT // 4

        def groups(eng, emit):
            emit(0, 0)
            emit(1, 1)
            with eng.Fori(1, NG // 2 - 1) as p:
                emit(p * 2, 0)
                emit(p * 2 + 1, 1)
            emit(NG - 2, 0)
            emit(NG - 1, 1)

        exists = lambda g: not isinstance(g, int) or 0 <= g < NG

        with nc.Block() as block:
            @block.sync
            def _(sp):
                sp.dma_start(ident[:, :], tables["ident"]).then_inc(consts_in, 16)
                sp.dma_start(ident_bf[:, :], tables["ident_bf"]).then_inc(consts_in, 16)
                sp.dma_start(masks[:, :, :], tables[f"masks{W}"].rearrange("t p k -> p t k")).then_inc(consts_in, 16)
                sp.dma_start(rot_base[:, :, :], tables[f"rot{W}"].rearrange("(t p) d -> p t d", p=128)).then_inc(consts_in, 16)
                sp.dma_start(frame[:, :], tables[f"frame{W}"]).then_inc(consts_in, 16)
                sp.wait_ge(consts_in, 80)

            @block.vector
            def _(dve):
                nc.vector.memset(hidden[:, :, :, :], 1.0).then_inc(zeroed, 1)
                nc.vector.memset(k_prev[:, 1, :, :], 0.0).then_inc(zeroed, 1)
                nc.vector.memset(v_prev[:, R - 1, :, :], 0.0).then_inc(zeroed, 1)
                dve.wait_ge(zeroed, 3)

        loop = ExitStack()
        layer = loop.enter_context(nc.Fori(0, depth))
        with nc.Block() as block:

            @block.sync
            def _(sp):
                l, W_ = layer, weights

                def load_input(T, par):
                    r = T * 128 + T // TPB
                    sp.dma_start(x_in[:, par, 0:64], x_rows[ds(r + 1, 128), 0:64]).then_inc(xin_in[par], 16)
                    sp.dma_start(x_in[:, par, 64:128], x_rows[ds(r, 128), 64:128]).then_inc(xin_in[par], 16)

                load_input(0, 0)
                load_input(1, 1)
                for j, nm in enumerate(("q_scale", "k_scale")):
                    src = W_[nm]
                    sp.dma_start(qk_scales[:, 2 * j, :], src[ds(l, 1), :].partition_broadcast(128)).then_inc(S["rep_in"], 16)
                    sp.dma_start(qk_scales[:, 2 * j + 1, 0:32], src[ds(l, 1), 32:64].partition_broadcast(128)).then_inc(S["rep_in"], 16)
                    sp.dma_start(qk_scales[:, 2 * j + 1, 32:64], src[ds(l, 1), 0:32].partition_broadcast(128)).then_inc(S["rep_in"], 16)
                sp.dma_start(w_out[:, :, :], W_["out"][l, :, :].rearrange("(u p) n -> p u n", p=128)).then_inc(S["wo_in"], 16)
                sp.dma_start(w_up[:, :], W_["w1"][l, :, :]).then_inc(S["wf_in"], 16)
                for c, (c0, cn) in enumerate(CH):
                    sp.dma_start(w_down[0:cn, c, :], W_["w2"][l, c0:c0 + cn, :]).then_inc(S["wf_in"], 16)
                    for j in range(2):
                        sp.dma_start(b_up[0:cn, j, c:c + 1], W_["b1"][l, j * HID + c0:j * HID + c0 + cn].rearrange("(p o) -> p o", o=1)).then_inc(S["wf_in"], 16)
                sp.dma_start(w_down[HID - 256:HID - 255, 2, :], W_["b2"][ds(l, 1), :]).then_inc(S["wf_in"], 16)
                sp.dma_start(ln_gb[:, 0:1], W_["ln_g"][l, :].rearrange("(p o) -> p o", o=1)).then_inc(S["wf_in"], 16)
                sp.dma_start(ln_gb[:, 1:2], W_["ln_b"][l, :].rearrange("(p o) -> p o", o=1)).then_inc(S["wf_in"], 16)

                def load_group(g, par):
                    r = g * 512 + g // (NG // 2)
                    rows = lambda at, half: mid_rows[ds(at, 512), half].rearrange("(t p) d -> p t d", p=128)
                    sp.dma_start(f_in[:, par, :, 0:64], rows(r + 1, slice(0, 64))).then_inc(fin_in[par], 16)
                    sp.dma_start(f_in[:, par, :, 64:128], rows(r, slice(64, 128))).then_inc(fin_in[par], 16)

                def emit(T, slot):
                    t = T + AHEAD
                    if live(t) and live(t - 2):
                        wait(sp, S["xT_ps"], nth(t - 2, 0, 1))
                        load_input(t, (slot + AHEAD) % 2)
                    if isinstance(T, int) and T == NT - 1:
                        sp.wait_ge(S["mid_stored"], 16 * 8)
                        load_group(0, 0)
                        load_group(1, 1)
                    if live(T - LAG_OUT):
                        t = T - LAG_OUT
                        wait(sp, S["mid_done"], nth(t, 0, 1))
                        wait(sp, S["mid_stored"], T * 16 - 16 * LAG_OUT)
                        sp.dma_start(mid_rows[ds(t * 128 + t // TPB + 1, 128), :], x[:, ds(t, 1), :].rearrange("p o d -> p (o d)")).then_inc(S["mid_stored"], 16)

                bodies(sp, emit)
                sp.wait_ge(S["mid_stored"], 16 * NT)

                def store_group(g, par):
                    sp.wait_ge(S["new_done"], g + 1)
                    wait(sp, new_stored[par], (g // 2) * 16)
                    r = g * 512 + g // (NG // 2) + 1
                    sp.dma_start(x_rows[ds(r, 512), :].rearrange("(t p) d -> p t d", p=128), x[:, ds(g * 4, 4), :]).then_inc(new_stored[par], 16)

                def emit_group(g, par):
                    if exists(g + 2):
                        sp.wait_ge(S["fnorm_done"], g + 1)
                        load_group(g + 2, par)
                    if exists(g - 1):
                        store_group(g - 1, 1 - par)

                groups(sp, emit_group)
                store_group(NG - 1, 1)
                sp.wait_ge(new_stored[0], 16 * NG // 2)
                sp.wait_ge(new_stored[1], 16 * NG // 2)

            @block.tensor
            def _(pe):
                def score_head(t, tp, u, h):
                    rows = slice(64 * h, 64 * h + 64)
                    c0 = h * KW
                    nc.tensor.matmul(ps_s[u % 2][0:W, c0 + 128:c0 + KW], qkT[rows, u % 2, 0:W], k_prev[rows, (tp + 1) % 2, u, :],
                                     start=False, stop=False)
                    nc.tensor.matmul(ps_s[u % 2][:, c0:c0 + 128], qkT[rows, u % 2, 0:128], qkT[rows, u % 2, 128:256],
                                     start=False, stop=(h == 1)).then_inc(S["score_ps"] if h else S["score_half"], 1)

                def emit(T, slot):
                    par = slot % 2
                    for s in range(U):
                        if live(T):
                            pe.wait_ge(S["normed"], nth(T, s))
                            wait(pe, S["qkT_done"], nth(T, s - 1))
                            if s == XT_STEP + 1:
                                wait(pe, S["xT_done"], nth(T + AHEAD, 0, 1) if live(T + AHEAD) else NT)
                            nc.tensor.transpose(ps_t[:, 0:128], qk[:, par, s, 0:128], ident[:, :])
                            nc.tensor.transpose(ps_t[:, 128:256], qk[:, par, s, 128:256], ident[:, :]).then_inc(S["qkT_ps"], 1)
                        t, d, u = unit(T, s, AT_PT)
                        if live(t):
                            wait(pe, S["pT_done"], nth(t, u - 1))
                            pe.wait_ge(S["probs_done"], nth(t, u))
                            pr = probs[:, u % 4, :, :]
                            for h in range(2):
                                nc.tensor.transpose(ps_pt[:, 128 * h:128 * h + 128], pr[:, h, 0:128], ident[:, :])
                            for h in range(2):
                                last = nc.tensor.transpose(ps_pt[:, 256 + W * h:256 + W * h + W], pr[0:W, h, W:KW], ident[0:W, 0:W])
                            last.then_inc(S["pT_ps"], 1)
                        t, d, u = unit(T, s, AT_SCORE)
                        if live(t):
                            tp = (par + d) % 2
                            sc = ps_s[u % 2][:, 0:2 * KW].rearrange("p (h k) -> p h k", h=2)
                            wait(pe, S["exp_done"], nth(t, u - 2))
                            pe.wait_ge(S["qkT_done"], nth(t, u))
                            wait(pe, S["kprev_done"], nth(t - 1, u))
                            nc.tensor.matmul(sc, ident_bf[:, :], masks[:, ds(t % TPB, 1), :].to_broadcast([128, 2, KW]), start=True, stop=False)
                            score_head(t, tp, u, 0)
                        t, d, u = unit(T, s, AT_PV)
                        if live(t):
                            wait(pe, S["outT_done"], nth(t, u - 1))
                            pe.wait_ge(S["pT_done"], nth(t, u))
                            pe.wait_ge(S["val_done"], nth(t, u))
                            wait(pe, S["vprev_done"], nth(t - 1, u))
                            for h in range(2):
                                nc.tensor.matmul(ps_o[64 * h:64 * h + 64, 0:128], val[:, (slot + d) % R, u, 64 * h:64 * h + 64],
                                                 probsT[:, u % 2, 128 * h:128 * h + 128], start=True, stop=False)
                                last = nc.tensor.matmul(ps_o[64 * h:64 * h + 64, 0:W], v_prev[128 - W:128, (slot + d - 1) % R, u, 64 * h:64 * h + 64],
                                                        probsT[128 - W:128, u % 2, 256 + W * h:256 + W * h + W], start=False, stop=True)
                            last.then_inc(S["pv_ps"], 1)
                        t, d, u = unit(T, s, AT_SCORE)
                        if live(t):
                            pe.wait_ge(consts_in, 80)
                            pe.wait_ge(S["score_half"], nth(t, u))
                            score_head(t, (par + d) % 2, u, 1)
                        t = T + AHEAD
                        if s == XT_STEP and live(t):
                            pe.wait_ge(xin_in[(par + AHEAD) % 2], 32 * loads(t))
                            wait(pe, S["qkT_done"], nth(T, s))
                            wait(pe, S["xT_done"], nth(t - 1, 0, 1))
                            nc.tensor.transpose(ps_t[:, 0:128], x_in[:, (par + AHEAD) % 2, :], ident[:, :]).then_inc(S["xT_ps"], 1)
                        t, d, u = unit(T, s, AT_OUT)
                        if live(t):
                            pe.wait_ge(S["outT_done"], nth(t, u))
                            pe.wait_ge(S["wo_in"], 16)
                            if u == 0:
                                wait(pe, S["mid_done"], nth(t - 1, 0, 1))
                            nc.tensor.matmul(ps_y[:, 0:128], outT[:, u % 2, :], w_out[:, u, :], start=(u == 0), stop=(u == U - 1)).then_inc(S["wo_used"], 1)
                        d, u = project[s]
                        if live(T + d):
                            pe.wait_ge(S["xT_done"], nth(T + d, 0, 1))
                            pe.wait_ge(S["wq_in"], 16 * 3)
                            n = nth(T + d, u - 2)
                            wait(pe, S["sq_done"], n)
                            wait(pe, S["val_done"], n)
                            wait(pe, S["rotated"], n)
                            nc.tensor.matmul(ps_q[u % 2][:, 0:384], xT[:, (par + d) % 2, :], w_qkv[:, u, :, :].rearrange("p j n -> p (j n)"),
                                             start=True, stop=True).then_inc(S["proj_ps"], 1)

                bodies(pe, emit)

                for n in ("exp_done", "pT_done", "outT_done", "qkT_done", "rotated", "sq_done", "val_done"):
                    pe.wait_ge(S[n], NT * U)
                pe.wait_ge(S["mid_done"], NT)
                pe.wait_ge(S["wf_in"], 16 * 13)

                def transpose_group(g):
                    pe.wait_ge(S["fnorm_done"], g + 1)
                    wait(pe, S["fT_done"], g)
                    for j in range(4):
                        last = nc.tensor.transpose(ps_t[:, 128 * j:128 * j + 128], f_norm[:, j, :], ident[:, :])
                    last.then_inc(S["fT_ps"], 1)

                def down_group(g, par):
                    pe.wait_ge(S["hidden_done"], g * 3 + 3)
                    wait(pe, S["new_done"], g)
                    for j in range(4):
                        for c, (c0, cn) in enumerate(CH):
                            k = cn + (c == 2)
                            last = nc.tensor.matmul(ps_y[:, 128 * j:128 * j + 128], hidden[0:k, par, c, 128 * j:128 * j + 128], w_down[0:k, c, :],
                                                    start=(c == 0), stop=(c == 2))
                    last.then_inc(S["down_ps"], 1)

                def emit_group(g, par):
                    pe.wait_ge(S["fT_done"], g + 1)
                    for j, banks, freed, made in ((1, ps_gate, "gelu_done", "gate_ps"), (0, ps_fact, "hidden_done", "up_ps")):
                        for c, (c0, cn) in enumerate(CH):
                            wait(pe, S[freed], g * 3 - 2 + c if exists(g - 1) else 0)
                            nc.tensor.matmul(banks[c][0:cn, :], w_up[:, j * HID + c0:j * HID + c0 + cn], f_normT[:, :],
                                             start=True, stop=True).then_inc(S[made], 1)
                    if exists(g + 1):
                        transpose_group(g + 1)
                    if exists(g - 1):
                        down_group(g - 1, 1 - par)

                transpose_group(0)
                groups(pe, emit_group)
                down_group(NG - 1, 1)

            @block.scalar
            def _(act):
                for j in range(3):
                    act.dma_start(w_qkv[:, :, j, :], weights["qkv"][layer, :, j * U * 128:(j + 1) * U * 128].rearrange("p (u n) -> p u n", u=U)).then_inc(S["wq_in"], 16)

                def squares_and_values(T, slot, s):
                    d, u = take_up[s]
                    if live(T + d):
                        act.wait_ge(S["proj_ps"], nth(T + d, u))
                        wait(act, S["ss_done"], nth(T + d, u - 2))
                        nc.scalar.activation(squares[:, u % 2, :], ps_q[u % 2][:, 0:256], ACT.Square).then_inc(S["sq_done"], 1)
                        wait(act, S["pv_ps"], nth(T + d - R, u))
                        wait(act, S["vprev_done"], nth(T + d - R, u))
                        nc.scalar.activation(val[:, (slot + d) % R, u, :], ps_q[u % 2][:, 256:384], ACT.Copy).then_inc(S["val_done"], 1)

                def output_copy(T, s):
                    t, d, u = unit(T, s, AT_PV)
                    if live(t):
                        act.wait_ge(S["pv_ps"], nth(t, u))
                        wait(act, S["wo_used"], nth(t, u - 2))
                        nc.scalar.activation(outT[:, u % 2, :], ps_o[:, 0:128], ACT.Copy).then_inc(S["outT_done"], 1)

                def exponentials(T, s):
                    t, d, u = unit(T, s, AT_EXP)
                    if live(t):
                        act.wait_ge(S["max_done"], nth(t, u))
                        wait(act, S["pT_ps"], nth(t, u - 4))
                        sc = ps_s[u % 2][:, 0:2 * KW].rearrange("p (h k) -> p h k", h=2)
                        for h in range(2):
                            last = nc.scalar.activation(probs[:, u % 4, h, :], sc[:, h, :], ACT.Exp, bias=neg_max[:, u % 4, h:h + 1], scale=1.0,
                                                        accum_out=p_sum[:, u % 4, h:h + 1])
                        last.then_inc(S["exp_done"], 1)

                def emit(T, slot):
                    for s in range(U):
                        if live(T):
                            act.wait_ge(S["qkT_ps"], nth(T, s))
                            wait(act, S["score_ps"], nth(T, s - 2))
                            wait(act, S["kprev_done"], nth(T, s - 2))
                            nc.scalar.activation(qkT[:, s % 2, :], ps_t[:, 0:256], ACT.Copy).then_inc(S["qkT_done"], 1)
                        t, d, u = unit(T, s, AT_PT)
                        if live(t):
                            act.wait_ge(S["pT_ps"], nth(t, u))
                            wait(act, S["pv_ps"], nth(t, u - 2))
                            nc.scalar.activation(probsT[:, u % 2, :], ps_pt[:, 0:256 + 2 * W], ACT.Copy).then_inc(S["pT_done"], 1)
                        exponentials(T, s)
                        output_copy(T, s)
                        t = T + AHEAD
                        if s == XT_STEP and live(t):
                            act.wait_ge(S["xT_ps"], nth(t, 0, 1))
                            wait(act, S["proj_ps"], nth(t - 2, U - 1))
                            nc.scalar.activation(xT[:, (slot + AHEAD) % 2, :], ps_t[:, 0:128], ACT.Copy).then_inc(S["xT_done"], 1)
                        squares_and_values(T, slot, s)

                bodies(act, emit)
                act.wait_ge(S["wf_in"], 16 * 13)

                def affine_group(g):
                    act.wait_ge(S["fT_ps"], g + 1)
                    wait(act, S["up_ps"], g * 3)
                    nc.scalar.activation(f_normT[:, :], ps_t[:, :], ACT.Identity, bias=ln_gb[:, 1:2], scale=ln_gb[:, 0:1]).then_inc(S["fT_done"], 1)

                def emit_group(g, par):
                    for c, (c0, cn) in enumerate(CH):
                        act.wait_ge(S["gate_ps"], g * 3 + (c + 1))
                        wait(act, S["hidden_done"], g * 3 - 2 + c if exists(g - 1) else 0)
                        nc.scalar.activation(gate[0:cn, c, :], ps_gate[c][0:cn, :], ACT.Gelu, bias=b_up[0:cn, 1, c:c + 1], scale=1.0).then_inc(S["gelu_done"], 1)
                    if exists(g + 1):
                        affine_group(g + 1)

                affine_group(0)
                groups(act, emit_group)

            @block.vector
            def _(dve):
                R4 = lambda ap: ap.rearrange("p (a h t x) -> p a h t x", a=2, h=2, t=2)

                def newton_link(T, np_, k):
                    r = rnorm[:, np_, :]
                    if k == 0:
                        dve.wait_ge(S["ss_done"], nth(T + 1, U - 1))
                        wait(dve, S["normed"], nth(T - 1, U - 1) if live(T - 1) else 0)
                        ins = nc.vector.tensor_scalar(nw_x[:, :], sumsq[:, :], 1e-24, None, ALU.max)
                    else:
                        dve.wait_ge(S["chain"], (T + 1) * CHAIN + k)
                        if k == 1:
                            ins = nc.vector.tensor_scalar(r.bitcast(I32), nw_x[:, :].bitcast(I32), -0.5, 1597463007.0, ALU.mult, ALU.add)
                        elif k == 2:
                            ins = nc.vector.tensor_scalar(nw_h[:, :], nw_x[:, :], -0.5, None, ALU.mult)
                        elif k % 3 == 0:
                            ins = nc.vector.tensor_tensor(nw_a[:, :], r, r, ALU.mult)
                        elif k % 3 == 1:
                            ins = nc.vector.tensor_tensor(nw_a[:, :], nw_a[:, :], nw_h[:, :], ALU.mult)
                        else:
                            ins = nc.vector.scalar_tensor_tensor(r, nw_a[:, :], 1.5, r, ALU.add, ALU.mult)
                    ins.then_inc(S["chain"], 1)

                def rotate(T, par, s):
                    d, u = take_up[s]
                    if not live(T + d):
                        return
                    dve.wait_ge(S["val_done"], nth(T + d, u))
                    if u == 0:
                        dve.wait_ge(S["rot_done"], nth(T + d, 0, 1))
                        wait(dve, S["chain"], (T + d - 1) * CHAIN + 1)
                    wait(dve, S["added"], nth(T + d, u - 2))
                    qkp = R4(ps_q[u % 2][:, 0:256])
                    cs = rot[:, (par + d) % 2, :, :].rearrange("p (a c) (o t x) -> p a c o t x", a=2, c=2, o=1, t=2)
                    nc.vector.tensor_tensor(R4(cos_part[:, u % 2, :]), qkp, cs[:, :, 0, :, :, :].to_broadcast([128, 2, 2, 2, 32]), ALU.mult)
                    nc.vector.tensor_tensor(R4(sin_part[:, u % 2, :]), qkp[:, :, :, ::-1, :], cs[:, :, 1, :, :, :].to_broadcast([128, 2, 2, 2, 32]), ALU.mult).then_inc(S["rotated"], 1)
                    nc.vector.tensor_reduce(sumsq[:, 4 * u:4 * u + 4], squares[:, u % 2, :].rearrange("p (g d) -> p g d", g=4), AX.X, ALU.add).then_inc(S["ss_done"], 1)

                def emit(T, slot):
                    par = slot % 2
                    for s in range(U):
                        def newton(spot):
                            if live(T + 1):
                                for k in links_at(s, spot):
                                    newton_link(T, (par + 1) % 2, k)
                        t, d, u = unit(T, s, AT_NORM)
                        if live(t):
                            dve.wait_ge(S["exp_done"], nth(t, u))
                            wait(dve, S["probs_done"], nth(t, u - 1))
                            nc.vector.reciprocal(p_rec[:, :], p_sum[:, u % 4, :]).then_inc(S["rec_done"], 1)
                            newton(0)
                            dve.wait_ge(S["rec_done"], nth(t, u))
                            pr = probs[:, u % 4, :, :]
                            nc.vector.tensor_tensor(pr, pr, p_rec[:, :].rearrange("p (h o) -> p h o", o=1).to_broadcast([128, 2, KW]), ALU.mult).then_inc(S["probs_done"], 1)
                        else:
                            newton(0)
                        if live(T):
                            newton(1)
                            dve.wait_ge(S["qkT_done"], nth(T, s))
                            wait(dve, S["score_ps"], nth(T - 1, s))
                            nc.vector.tensor_scalar(k_prev[:, par, s, :], qkT[:, s % 2, 256 - W:256], frame[:, 0:1], None, ALU.mult).then_inc(S["kprev_done"], 1)
                            newton(2)
                            dve.wait_ge(S["val_done"], nth(T, s))
                            wait(dve, S["pv_ps"], nth(T - R + 1, s))
                            nc.vector.tensor_copy(v_prev[128 - W:128, slot, s, :], val[128 - W:128, slot, s, :]).then_inc(S["vprev_done"], 1)
                        else:
                            newton(1)
                            newton(2)
                        t, d, u = unit(T, s, AT_MAX)
                        if live(t):
                            dve.wait_ge(S["score_ps"], nth(t, u))
                            wait(dve, S["exp_done"], nth(t, u - 4))
                            sc = ps_s[u % 2][:, 0:2 * KW].rearrange("p (h k) -> p h k", h=2)
                            nc.vector.tensor_reduce(neg_max[:, u % 4, :], sc, AX.X, ALU.max, negate=True).then_inc(S["max_done"], 1)
                        newton(3)
                        t, d, u = unit(T, s, AT_OUT)
                        if live(t) and u == U - 1:
                            dve.wait_ge(S["wo_used"], nth(t, u))
                            x_t = x[:, ds(t, 1), :].rearrange("p o d -> p (o d)")
                            nc.vector.tensor_tensor(x_t, ps_y[:, 0:128], x_t, ALU.add).then_inc(S["mid_done"], 1)
                        rotate(T, par, s)
                        newton(4)

                bodies(dve, emit)
                dve.wait_ge(S["mid_stored"], 16 * NT)
                step = Steps(dve, S["ln_steps"])
                PER = 7 + 2 + 3 * NEWTONS

                def normalise_group(g, par):
                    step.turn(0, g, PER)
                    dve.wait_ge(fin_in[par], (g // 2) * 32 + 32)
                    for j in range(4):
                        last = nc.vector.bn_stats(stats[:, j, :], f_in[:, par, j, :])
                    step(last)
                    step(nc.vector.memset(f_var[:, :], LN_EPS), settle=False)
                    for j in range(4):
                        step(nc.vector.bn_aggr(mean_var[:, j, :], stats[:, j, :]), settle=(j == 3))
                    step(nc.vector.tensor_tensor(f_var[:, :], f_var[:, :], mean_var[:, :, 1], ALU.add))
                    inverse_root(step, nc, f_rstd[:, :], f_var[:, :], f_half[:, :], f_tmp[:, :], NEWTONS)
                    wait(dve, S["fT_ps"], g)
                    for j in range(4):
                        last = nc.vector.tensor_scalar(f_norm[:, j, :], f_in[:, par, j, :], mean_var[:, j, 0:1], f_rstd[:, j:j + 1], ALU.subtract, ALU.mult)
                    last.then_inc(S["fnorm_done"], 1)

                def add_group(g):
                    dve.wait_ge(S["down_ps"], g + 1)
                    x_g = x[:, ds(g * 4, 4), :].rearrange("p t d -> p (t d)")
                    nc.vector.tensor_tensor(x_g, ps_y[:, :], x_g, ALU.add).then_inc(S["new_done"], 1)

                def emit_group(g, par):
                    if exists(g + 1):
                        normalise_group(g + 1, 1 - par)
                    wait(dve, S["down_ps"], g - 1 if exists(g - 2) else 0)
                    for c, (c0, cn) in enumerate(CH):
                        dve.wait_ge(S["up_ps"], g * 3 + (c + 1))
                        dve.wait_ge(S["gelu_done"], g * 3 + (c + 1))
                        nc.vector.scalar_tensor_tensor(hidden[0:cn, par, c, :], ps_fact[c][0:cn, :], b_up[0:cn, 0, c:c + 1],
                                                       gate[0:cn, c, :], ALU.add, ALU.mult).then_inc(S["hidden_done"], 1)
                    if exists(g - 1):
                        add_group(g - 1)

                normalise_group(0, 0)
                groups(dve, emit_group)
                add_group(NG - 1)

            @block.gpsimd
            def _(pool):
                def to_unit_length(T, par, s):
                    for d, u in normalise[s]:
                        if live(T + d):
                            pool.wait_ge(S["chain"], (T + d + 1) * CHAIN)
                            pool.wait_ge(S["added"], nth(T + d, u))
                            v = qk[:, (par + d) % 2, u, :].rearrange("p (g d) -> p g d", g=4)
                            rr = rnorm[:, (par + d) % 2, 4 * u:4 * u + 4].rearrange("p (g o) -> p g o", o=1).to_broadcast([128, 4, 64])
                            nc.gpsimd.tensor_tensor(v, v, rr, ALU.mult).then_inc(S["normed"], 1)

                def emit(T, slot):
                    par = slot % 2
                    for s in range(U):
                        to_unit_length(T, par, s)
                        d, u = take_up[s]
                        if live(T + d):
                            pool.wait_ge(S["rotated"], nth(T + d, u))
                            wait(pool, S["qkT_ps"], nth(T + d - 2, u))
                            nc.gpsimd.tensor_tensor(qk[:, (par + d) % 2, u, :], cos_part[:, u % 2, :], sin_part[:, u % 2, :], ALU.add).then_inc(S["added"], 1)
                        t = T + AHEAD
                        if s == ROT_STEP and live(t):
                            pool.wait_ge(S["rep_in"], 16 * 6)
                            wait(pool, S["rotated"], nth(t - 2, U - 1))
                            nc.gpsimd.tensor_tensor(rot[:, (par + AHEAD) % 2, :, :].rearrange("p a d -> p (a d)"), rot_base[:, ds(t % TPB, 1), :].rearrange("p o d -> p (o d)"),
                                                    qk_scales[:, :, :].rearrange("p a d -> p (a d)"), ALU.mult).then_inc(S["rot_done"], 1)

                bodies(pool, emit)

        for s in taken:
            nc.gpsimd.sem_clear(s)
        nc.all_engine_barrier()
        loop.close()


def two_layer_kernel(nc, t, out):
    dram = lambda n, shape: nc.dram_tensor(n, shape, F32, kind="Internal").ap()
    qkv = [dram(f"l0_{n}", [4096, 128]) for n in "qkv"]
    x_rows, mid_rows = dram("x_rows", [ROWS, 128]), dram("mid_rows", [ROWS, 128])
    with ExitStack() as ctx:
        mods = ctx.enter_context(nc.sbuf_tensor("mods", [128, 4, 6, 128], F32))
        xr = ctx.enter_context(nc.sbuf_tensor("xr", [128, TILES, 128], F32))
        z = ctx.enter_context(nc.sbuf_tensor("z", [128, TILES, 128], F32))
        zero_rows(nc, (x_rows, mid_rows), t["zeros"])
        modulation_stage(nc, mods, [t["L0_c"], t["L1_c"]], [t["L0_wmod"], t["L1_wmod"]])
        delta_attention_stage(nc, t["L0_attn_x"], xr, mods, [t["L0_attn_WqT"], t["L0_attn_WkT"], t["L0_attn_WvT"]], t["L0_attn_WoT"],
                              t["L0_attn_alpha_raw"], t["L0_attn_beta_raw"], t, qkv)
        feed_stage(nc, "feed0", xr, mods, 0, z, x_rows)
        names = dict(qkv="Wqkv", out="Wo", w1="W1", w2="W2", b1="b1", b2="b2", ln_g="ln_g", ln_b="ln_b", q_scale="q_scale", k_scale="k_scale")
        local_block_stage(nc, "L0", 6, 16, 32, z, x_rows, mid_rows, {k: t["L0_ffn_" + v] for k, v in names.items()}, t)
        residual_stage(nc, "res0", xr, mods, 0, z)
        linear_attention_stage(nc, xr, mods, {k[8:]: v for k, v in t.items() if k.startswith("L1_attn_")}, t)
        feed_stage(nc, "feed1", xr, mods, 1, z, x_rows)
        local_block_stage(nc, "L1", 2, 8, 64, z, x_rows, mid_rows, {k: t["L1_ffn_" + v.lower()] for k, v in names.items()}, t)
        residual_stage(nc, "res1", xr, mods, 2, z, out)


def zero_rows(nc, arrays, zeros):
    with stage_semaphores(nc, "zr") as sem, nc.Block() as block:
        stored = sem("stored")

        @block.sync
        def _(sp):
            total = 0
            for a in arrays:
                n = a.shape[0] // 2049
                sp.dma_start(a.rearrange("(n r) d -> n r d", r=2049)[:, 0, :], zeros[0:n, :]).then_inc(stored, 16)
                total += 16
            sp.wait_ge(stored, total)


def rotary_table(window, n=2048, dim=64):
    half = np.arange(0, dim, 2, dtype=np.float32)
    inv = (np.float32(1.0) / np.float32(10000.0) ** (half / np.float32(dim))).astype(np.float32)
    angle = (np.arange(n, dtype=np.float32)[:, None] * inv[None, :]).astype(np.float32).astype(np.float64)
    base = (half.astype(np.float64) + 0.4 * dim) / (1.4 * dim)
    scale = base[None, :] ** ((np.arange(n) % 128 - 64) / (window // 2))[:, None]
    out = np.zeros((n, 2, 2, dim))
    for a, f in ((0, 8.0 * scale), (1, 1.0 / scale)):
        out[:, a, 0, :] = np.tile(np.cos(angle) * f, 2)
        out[:, a, 1, :] = np.concatenate([-np.sin(angle) * f, np.sin(angle) * f], 1)
    frame = np.tile(base, 4) ** (128 / (window // 2))
    return out.reshape(n, 256).astype(np.float32), frame.reshape(128, 1).astype(np.float32)


def window_masks(window, tiles):
    q, k = np.arange(128)[:, None], np.arange(128)[None, :]
    own = (k <= q) & (q <= k + window) & (q // window - k // window <= 1)
    before = (q <= np.arange(window)[None, :]) & (q < window)
    m = np.zeros((tiles, 128, 128 + window), np.float32)
    for t in range(tiles):
        m[t, :, :128] = np.where(own, 0, -1e30)
        m[t, :, 128:] = np.where(before & (t > 0), 0, -1e30)
    return m.astype(mybir.dt.np(BF16))


def shape_constants():
    p = np.arange(128)
    c = {"ident": np.eye(128, dtype=np.float32), "ident_bf": np.eye(128, dtype=np.float32).astype(mybir.dt.np(BF16)),
         "zeros": np.zeros((16, 128), np.float32), "block01": (p[:, None] // 8 == np.arange(16)[None, :]).astype(np.float32),
         "causal64": np.where(p[:, None] % 64 >= np.arange(64)[None, :], 0, -1e30).astype(mybir.dt.np(BF16)),
         "keep": (p[:, None] <= p[None, :]).astype(np.float32)}
    for w in (32, 64):
        c[f"rot{w}"], c[f"frame{w}"] = rotary_table(w)
        c[f"masks{w}"] = window_masks(w, 16)
    return c


def kernel(**inputs):
    import concourse.bacc as bacc
    from concourse.bass_utils import run_bass_kernel_spmd

    nc = bacc.Bacc("TRN2", target_bir_lowering=False, num_devices=1)
    transposed = {"L0_attn_Wq", "L0_attn_Wk", "L0_attn_Wv", "L0_attn_Wo", "L1_attn_q_w", "L1_attn_k_w", "L1_attn_v_w", "L1_attn_o_w", "L1_attn_f1_w", "L1_attn_f2_w"}
    arrays = {}
    for name, a in inputs.items():
        a = np.asarray(a)
        if name in transposed:
            name, a = name + "T", a.T
        arrays[name] = np.ascontiguousarray(a)
    arrays.update(shape_constants())
    t = {n: nc.dram_tensor("in_" + n, a.shape, mybir.dt.from_np(a.dtype), kind="ExternalInput").ap() for n, a in arrays.items()}
    out = nc.dram_tensor("out_x", (2, 2048, 128), F32, kind="ExternalOutput").ap()
    two_layer_kernel(nc, t, out)
    r = run_bass_kernel_spmd(nc, [{"in_" + n: a for n, a in arrays.items()}], core_ids=[0])
    return r.results[0]["out_x"]
```
